# Optimizing a Trainium2 kernel written in Bass

```python
import numpy as np
import jax
import jax.numpy as jnp

def _softmax(x, axis=-1):
    return jax.nn.softmax(x, axis=axis)

def _gelu(x):
    return jax.nn.gelu(x, approximate=True)

def _silu(x):
    return jax.nn.silu(x)

def _sigmoid(x):
    return jax.nn.sigmoid(x)

def _layernorm(x, axis=-1, eps=1e-05):
    m = jnp.mean(x, axis=axis, keepdims=True)
    v = jnp.var(x, axis=axis, keepdims=True)
    return (x - m) / jnp.sqrt(v + eps)

def _scatter_add(tgt, idx, src, axis=0):
    return tgt.at[idx].add(src)

def _segment_sum(src, seg, n):
    return jax.ops.segment_sum(src, seg, n)
kernel_name = 'mk_decoder_preln_d1_seqx_r8_6795c0'

def setup_inputs(seed: int=0):
    np.random.seed(seed)
    _w = jnp.asarray

    def _rec_inputs():
        import jax
        import jax.numpy as jnp
        _rk = jax.random.key(seed)
        x = 7.22e-05 + 1 * jax.random.normal(jax.random.fold_in(_rk, 1), (128, 64, 128), jnp.float32)
        _lenS = 64 - jax.random.randint(jax.random.fold_in(_rk, 7), (128,), 0, max(1, 64 // 4) + 1, jnp.int32)
        _lenS2 = 64 - jax.random.randint(jax.random.fold_in(_rk, 8), (128,), 0, max(1, 64 // 4) + 1, jnp.int32)
        _ctx_1024P = jax.random.normal(jax.random.fold_in(_rk, 11), (128, 16, 128), jnp.float32)
        _ctx_1024c = jax.random.dirichlet(jax.random.fold_in(_rk, 511), 0.3 * jnp.ones((16,), jnp.float32), (128, 64))
        _ctx_1024t = jnp.einsum('bsk,bkd->bsd', _ctx_1024c, _ctx_1024P)
        _ctx_1024t = _ctx_1024t * jax.lax.rsqrt(jnp.mean(jnp.square(_ctx_1024t)) + 1e-12) * 0.953939
        ctx_1024 = 4.13588e-05 + 0.999923 * (_ctx_1024t + 0.3 * jax.random.normal(jax.random.fold_in(_rk, 611), (128, 64, 128), jnp.float32))
        _validS = jnp.arange(64)[None, :] < _lenS[:, None]
        _validS2 = jnp.arange(64)[None, :] < _lenS2[:, None]
        _causal = jnp.tril(jnp.ones((64, 64), dtype=bool))
        mask_BxS2_if1 = jnp.where(jnp.ones((128, 64), dtype=bool), 1, 0).astype(jnp.int32)
        return (x, ctx_1024, mask_BxS2_if1)
    x, ctx_1024, mask_BxS2_if1 = _rec_inputs()

    def _L0_attn_setup():
        import jax, jax.numpy as jnp
        import numpy as np
        D_MODEL = 128
        N_HEADS = 16
        DH = D_MODEL // N_HEADS
        B, T = (4, 256)
        ROPE_BASE = 10000.0
        EPS = 1e-06

        def _rope(q, k, base=ROPE_BASE):
            half = q.shape[-1] // 2
            freqs = jnp.arange(half, dtype=q.dtype)
            inv_freq = base ** (-freqs / half)
            pos = jnp.arange(q.shape[2], dtype=q.dtype)
            ang = pos[:, None] * inv_freq[None, :]
            c = jnp.cos(ang)[None, None]
            s = jnp.sin(ang)[None, None]

            def rot(x):
                x1 = x[..., :half]
                x2 = x[..., half:2 * half]
                return jnp.concatenate([x1 * c - x2 * s, x1 * s + x2 * c], axis=-1)
            return (rot(q), rot(k))

        def _phi(x):
            return jax.nn.elu(x) + 1.0

        def _forward(x, Wq, Wk, Wv, Wo):
            Bx, Tx, D = x.shape
            H, dh = (N_HEADS, D // N_HEADS)
            q = (x @ Wq.T).reshape(Bx, Tx, H, dh).transpose(0, 2, 1, 3)
            k = (x @ Wk.T).reshape(Bx, Tx, H, dh).transpose(0, 2, 1, 3)
            v = (x @ Wv.T).reshape(Bx, Tx, H, dh).transpose(0, 2, 1, 3)
            q, k = _rope(q, k)
            q = _phi(q)
            k = _phi(k)
            qT = q.transpose(2, 0, 1, 3)
            kT = k.transpose(2, 0, 1, 3)
            vT = v.transpose(2, 0, 1, 3)

            def step(carry, qkv):
                K_sum, KV = carry
                q_t, k_t, v_t = qkv
                K_sum = K_sum + k_t
                KV = KV + k_t[..., :, None] * v_t[..., None, :]
                num = jnp.einsum('bhd,bhde->bhe', q_t, KV)
                den = jnp.maximum(jnp.einsum('bhd,bhd->bh', q_t, K_sum), EPS)
                return ((K_sum, KV), num / den[..., None])
            init = (jnp.zeros((Bx, H, dh), x.dtype), jnp.zeros((Bx, H, dh, dh), x.dtype))
            _, Y = jax.lax.scan(step, init, (qT, kT, vT))
            Y = Y.transpose(1, 0, 2, 3).reshape(Bx, Tx, D)
            return Y @ Wo.T
        key = jax.random.key(seed)
        kx, kq, kk, kv, ko = jax.random.split(key, 5)
        scale = 0.02
        return {'x': jax.random.normal(kx, (B, T, D_MODEL), jnp.float32), 'Wq': jax.random.normal(kq, (D_MODEL, D_MODEL), jnp.float32) * scale, 'Wk': jax.random.normal(kk, (D_MODEL, D_MODEL), jnp.float32) * scale, 'Wv': jax.random.normal(kv, (D_MODEL, D_MODEL), jnp.float32) * scale, 'Wo': jax.random.normal(ko, (D_MODEL, D_MODEL), jnp.float32) * scale}
    _L0_attn_all = _L0_attn_setup()
    _L0_attn_in = {k: v for k, v in _L0_attn_all.items() if k in ('Wq', 'Wk', 'Wv', 'Wo')}
    del _L0_attn_all

    def _L0_xattn_setup():
        import jax, jax.numpy as jnp
        import numpy as np
        import math
        EMBED_DIM = 128
        NUM_HEADS = 16
        D_K = EMBED_DIM // NUM_HEADS

        def _separate_heads(x):
            B, S, _ = x.shape
            return x.reshape(B, S, NUM_HEADS, D_K).transpose(0, 2, 1, 3)
        key = jax.random.key(seed)
        kq, kk, kv = jax.random.split(key, 3)
        B, S, E = (4, 256, EMBED_DIM)
        q = jax.random.normal(kq, (B, S, E), dtype=jnp.float32)
        k = jax.random.normal(kk, (B, S, E), dtype=jnp.float32)
        v = jax.random.normal(kv, (B, S, E), dtype=jnp.float32)
        mask = jnp.ones((B, S), dtype=jnp.int32)
        return {'q': q, 'k': k, 'v': v, 'mask': mask}
    _L0_xattn_all = _L0_xattn_setup()
    _L0_xattn_in = {k: v for k, v in _L0_xattn_all.items() if k in ()}
    del _L0_xattn_all

    def _L0_ffn_setup():
        import jax, jax.numpy as jnp
        import numpy as np
        EPS = 1e-05
        LN_EPS = 1e-05
        NUM_EXPERTS = 8
        TOP_K = 2
        HIDDEN = 128
        INTER = 256

        def _swiglu(x, wg, wu, wd):
            return jax.nn.silu(x @ wg) * (x @ wu) @ wd
        key = jax.random.key(seed)
        ks = jax.random.split(key, 10)
        B, S, H, I, E = (8, 512, HIDDEN, INTER, NUM_EXPERTS)
        std_h = 1.0 / np.sqrt(H)
        std_i = 1.0 / np.sqrt(I)
        return {'x': jax.random.normal(ks[0], (B, S, H), dtype=jnp.float32), 'ln_scale': jnp.ones((H,), dtype=jnp.float32), 'ln_bias': jnp.zeros((H,), dtype=jnp.float32), 'gate_w': jax.random.normal(ks[1], (E, H), dtype=jnp.float32) * 0.01, 'Wg': jax.random.normal(ks[2], (E, H, I), dtype=jnp.float32) * std_h, 'Wu': jax.random.normal(ks[3], (E, H, I), dtype=jnp.float32) * std_h, 'Wd': jax.random.normal(ks[4], (E, I, H), dtype=jnp.float32) * std_i, 'sWg': jax.random.normal(ks[5], (H, I), dtype=jnp.float32) * std_h, 'sWu': jax.random.normal(ks[6], (H, I), dtype=jnp.float32) * std_h, 'sWd': jax.random.normal(ks[7], (I, H), dtype=jnp.float32) * std_i}
    _L0_ffn_all = _L0_ffn_setup()
    _L0_ffn_in = {k: v for k, v in _L0_ffn_all.items() if k in ('ln_scale', 'ln_bias', 'gate_w', 'Wg', 'Wu', 'Wd', 'sWg', 'sWu', 'sWd')}
    del _L0_ffn_all
    return {'x': x, 'ctx_1024': ctx_1024, 'mask_BxS2_if1': mask_BxS2_if1, 'L0_attn_Wq': _L0_attn_in['Wq'], 'L0_attn_Wk': _L0_attn_in['Wk'], 'L0_attn_Wv': _L0_attn_in['Wv'], 'L0_attn_Wo': _L0_attn_in['Wo'], 'L0_ffn_ln_scale': _L0_ffn_in['ln_scale'], 'L0_ffn_ln_bias': _L0_ffn_in['ln_bias'], 'L0_ffn_gate_w': _L0_ffn_in['gate_w'], 'L0_ffn_Wg': _L0_ffn_in['Wg'], 'L0_ffn_Wu': _L0_ffn_in['Wu'], 'L0_ffn_Wd': _L0_ffn_in['Wd'], 'L0_ffn_sWg': _L0_ffn_in['sWg'], 'L0_ffn_sWu': _L0_ffn_in['sWu'], 'L0_ffn_sWd': _L0_ffn_in['sWd']}

def reference(x, ctx_1024, mask_BxS2_if1, L0_attn_Wq, L0_attn_Wk, L0_attn_Wv, L0_attn_Wo, L0_ffn_ln_scale, L0_ffn_ln_bias, L0_ffn_gate_w, L0_ffn_Wg, L0_ffn_Wu, L0_ffn_Wd, L0_ffn_sWg, L0_ffn_sWu, L0_ffn_sWd):
    import jax
    import jax.numpy as jnp

    def _L0_attn_ref(x, Wq, Wk, Wv, Wo):
        import jax, jax.numpy as jnp
        import numpy as np
        D_MODEL = 128
        N_HEADS = 16
        DH = D_MODEL // N_HEADS
        B, T = (4, 256)
        ROPE_BASE = 10000.0
        EPS = 1e-06

        def _rope(q, k, base=ROPE_BASE):
            half = q.shape[-1] // 2
            freqs = jnp.arange(half, dtype=q.dtype)
            inv_freq = base ** (-freqs / half)
            pos = jnp.arange(q.shape[2], dtype=q.dtype)
            ang = pos[:, None] * inv_freq[None, :]
            c = jnp.cos(ang)[None, None]
            s = jnp.sin(ang)[None, None]

            def rot(x):
                x1 = x[..., :half]
                x2 = x[..., half:2 * half]
                return jnp.concatenate([x1 * c - x2 * s, x1 * s + x2 * c], axis=-1)
            return (rot(q), rot(k))

        def _phi(x):
            return jax.nn.elu(x) + 1.0

        def _forward(x, Wq, Wk, Wv, Wo):
            Bx, Tx, D = x.shape
            H, dh = (N_HEADS, D // N_HEADS)
            q = (x @ Wq.T).reshape(Bx, Tx, H, dh).transpose(0, 2, 1, 3)
            k = (x @ Wk.T).reshape(Bx, Tx, H, dh).transpose(0, 2, 1, 3)
            v = (x @ Wv.T).reshape(Bx, Tx, H, dh).transpose(0, 2, 1, 3)
            q, k = _rope(q, k)
            q = _phi(q)
            k = _phi(k)
            qT = q.transpose(2, 0, 1, 3)
            kT = k.transpose(2, 0, 1, 3)
            vT = v.transpose(2, 0, 1, 3)

            def step(carry, qkv):
                K_sum, KV = carry
                q_t, k_t, v_t = qkv
                K_sum = K_sum + k_t
                KV = KV + k_t[..., :, None] * v_t[..., None, :]
                num = jnp.einsum('bhd,bhde->bhe', q_t, KV)
                den = jnp.maximum(jnp.einsum('bhd,bhd->bh', q_t, K_sum), EPS)
                return ((K_sum, KV), num / den[..., None])
            init = (jnp.zeros((Bx, H, dh), x.dtype), jnp.zeros((Bx, H, dh, dh), x.dtype))
            _, Y = jax.lax.scan(step, init, (qT, kT, vT))
            Y = Y.transpose(1, 0, 2, 3).reshape(Bx, Tx, D)
            return Y @ Wo.T
        return _forward(x, Wq, Wk, Wv, Wo)

    def _L0_xattn_ref(q, k, v, mask):
        import jax, jax.numpy as jnp
        import numpy as np
        import math
        EMBED_DIM = 128
        NUM_HEADS = 16
        D_K = EMBED_DIM // NUM_HEADS

        def _separate_heads(x):
            B, S, _ = x.shape
            return x.reshape(B, S, NUM_HEADS, D_K).transpose(0, 2, 1, 3)
        B, S, E = q.shape
        Q = _separate_heads(q)
        K = _separate_heads(k)
        V = _separate_heads(v)
        scale = 1.0 / math.sqrt(D_K)
        scores = jnp.einsum('bhqd,bhkd->bhqk', Q, K) * scale
        scores = jnp.where(mask[:, None, None, :] == 0, jnp.float32(-1000000000.0), scores)
        attn = jax.nn.softmax(scores, axis=-1)
        context = jnp.einsum('bhqk,bhkd->bhqd', attn, V)
        context = context.transpose(0, 2, 1, 3).reshape(B, S, E)
        return context

    def _L0_ffn_ref(x, ln_scale, ln_bias, gate_w, Wg, Wu, Wd, sWg, sWu, sWd):
        import jax, jax.numpy as jnp
        import numpy as np
        EPS = 1e-05
        LN_EPS = 1e-05
        NUM_EXPERTS = 8
        TOP_K = 2
        HIDDEN = 128
        INTER = 256

        def _swiglu(x, wg, wu, wd):
            return jax.nn.silu(x @ wg) * (x @ wu) @ wd
        B, S, H = x.shape
        xf = x.reshape(-1, H)
        mu = jnp.mean(xf, axis=-1, keepdims=True)
        var = jnp.var(xf, axis=-1, keepdims=True)
        xn = (xf - mu) * jax.lax.rsqrt(var + LN_EPS) * ln_scale + ln_bias
        logits = xn @ gate_w.T
        probs = jax.nn.softmax(logits, axis=-1)
        tk_probs, tk_idx = jax.lax.top_k(probs, TOP_K)
        tk_probs = tk_probs / (jnp.sum(tk_probs, axis=-1, keepdims=True) + EPS)
        onehot = tk_idx[..., None] == jnp.arange(NUM_EXPERTS)[None, None, :]
        w = jnp.sum(tk_probs[..., None] * onehot.astype(tk_probs.dtype), axis=1)
        out = _swiglu(xf, sWg, sWu, sWd)
        for e in range(NUM_EXPERTS):
            out = out + w[:, e:e + 1] * _swiglu(xf, Wg[e], Wu[e], Wd[e])
        return out.reshape(B, S, H)
    x = x + _L0_attn_ref(_layernorm(x, axis=-1), L0_attn_Wq, L0_attn_Wk, L0_attn_Wv, L0_attn_Wo)
    x = x + _L0_xattn_ref(_layernorm(x, axis=-1), ctx_1024, ctx_1024, mask_BxS2_if1)
    x = x + _L0_ffn_ref(_layernorm(x, axis=-1), L0_ffn_ln_scale, L0_ffn_ln_bias, L0_ffn_gate_w, L0_ffn_Wg, L0_ffn_Wu, L0_ffn_Wd, L0_ffn_sWg, L0_ffn_sWu, L0_ffn_sWd)
    return x

_drawn_inputs = setup_inputs


def setup_inputs(seed=0):
    import zlib

    import numpy as np

    out = dict(_drawn_inputs(seed))
    spreads = {'L0_ffn_ln_scale': (1.0, 0.2), 'L0_ffn_ln_bias': (0.0, 0.1)}
    factors = {'L0_attn_Wq': 32.277, 'L0_attn_Wk': 27.642}
    for name, (base, spread) in spreads.items():
        noise = np.random.default_rng([zlib.crc32(name.encode()), seed]).standard_normal(out[name].shape)
        drawn = base * np.exp(spread * noise) if base else spread * noise
        out[name] = jnp.asarray(drawn.astype(out[name].dtype))
    for name, factor in factors.items():
        out[name] = (out[name] * factor).astype(out[name].dtype)
    return out
```

```python
import numpy as np
import concourse.bass as bass
from concourse import mybir
from contextlib import ExitStack

F32 = mybir.dt.float32
BF16 = mybir.dt.bfloat16
I32 = mybir.dt.int32
ALU = mybir.AluOpType
ACT = mybir.ActivationFunctionType
AX = mybir.AxisListType.X

P = 128
SEQS, T, D = 128, 64, 128
H, DH = 16, 8
HALF = DH // 2
TILES = SEQS * T // P
GT = 4
GROUPS = TILES // GT
GS = GT * P // T
GN = GT * P
R, C = 8, 2
E9 = DH + 1
E, INTER = 8, 256
CH = INTER // P
LN_EPS, DEN_EPS, TOP_EPS = 1e-5, 1e-6, 1e-5
SCALE = DH ** -0.5
MASKED = -1e9 / SCALE

CONST = {"ident": P, "causal": T, "cos": HALF, "sin": HALF, "row": R, "half": C, "ind": R * T, "lower": E}
CONST_AT = dict(zip(CONST, np.cumsum([0, *CONST.values()])[:-1].tolist()))
CONST_N = sum(CONST.values())


def shape_constants():
    c = np.zeros((P, CONST_N), np.float32)

    def part(name):
        return c[:, CONST_AT[name]:CONST_AT[name] + CONST[name]]

    p = np.arange(P)
    part("ident")[:] = np.eye(P)
    part("causal")[:] = (p % T)[:, None] <= np.arange(T)[None, :]
    inv = np.float32(10000.0) ** (-np.arange(HALF, dtype=np.float32) / np.float32(HALF))
    ang = (p % T).astype(np.float32)[:, None] * inv[None, :].astype(np.float32)
    part("cos")[:] = np.cos(ang)
    part("sin")[:] = np.sin(ang)
    part("row")[:] = (p // DH % R)[:, None] == np.arange(R)[None, :]
    part("half")[:] = (p // T)[:, None] == np.arange(C)[None, :]
    part("ind")[:2 * R] = np.kron(np.tile(np.eye(R), (2, 1)), np.ones((1, T)))
    part("lower")[:] = np.arange(E, 0, -1)[None, :]
    return c


def decoder_block(nc, x, ctx, mask, wq, wk, wv, wo, ln_scale, ln_bias, gate_w, wg, wu, wd, swg, swu, swd,
                  consts, out):
    with ExitStack() as stack:
        def sb(name, shape, dt=F32):
            return stack.enter_context(nc.sbuf_tensor(name, shape, dt))

        def sem(name):
            return stack.enter_context(nc.semaphore(name))

        banks = [stack.enter_context(nc.psum_tensor(f"bank{n}", [P, 512], F32)) for n in range(8)]

        X = sb("X", [P, TILES, D])
        xfT = sb("xfT", [P, TILES * P])
        con = sb("con", [P, CONST_N])
        wraw = sb("wraw", [P, 4, D])
        wqkvT = sb("wqkvT", [P, 3 * D])
        woT = sb("woT", [P, D])
        gate_raw = sb("gate_raw", [E, D])
        gateT = sb("gateT", [P, E])
        lnp = sb("lnp", [P, 2])
        wup = sb("wup", [P, E + 1, 2, INTER])
        wdn = sb("wdn", [P, E + 1, CH, D])
        ind = sb("ind", [2 * R, R * T], BF16)
        ones_row = sb("ones_row", [1, P], BF16)

        def const(name):
            return con[:, CONST_AT[name]:CONST_AT[name] + CONST[name]]

        ident, causal, cos, sin, row, halves = (const(n) for n in ("ident", "causal", "cos", "sin", "row", "half"))

        minus_half = sb("minus_half", [P, GT])

        a_stat = sb("a_stat", [P, GT, 6])
        a_mv = sb("a_mv", [P, GT, 2])
        a_rs = sb("a_rs", [P, GT])
        a_xn = sb("a_xn", [P, GT, D])
        a_xnT = sb("a_xnT", [P, GN])
        qk = sb("qk", [P, GT * 2 * D])
        rot = sb("rot", [P, GT * 2 * D])
        rot2 = sb("rot2", [P, GT * 2 * D])
        phi = sb("phi", [P, GT, 2, D])
        qT = sb("qT", [P, GN])
        Kc = sb("Kc", [P, GS, C, T])
        Qblk = sb("Qblk", [P, GS, R, T])
        Vblk = sb("Vblk", [P, GS, R, C, E9])
        Am = sb("Am", [P, 2, R * T])
        a_den = sb("a_den", [P, 2, R * C])
        a_rec = sb("a_rec", [P, 2, R * C])
        a_y = sb("a_y", [P, GT, D])
        a_yT = sb("a_yT", [P, GN])
        b_stat = sb("b_stat", [P, GT, 6])
        b_mv = sb("b_mv", [P, GT, 2])
        b_rs = sb("b_rs", [P, GT])
        b_xn = sb("b_xn", [P, GT, D])
        Qc = sb("Qc", [P, GS, C, T])
        ctxD = sb("ctxD", [P, GS, D])
        maskB = sb("maskB", [P, GN], I32)
        ctxT = sb("ctxT", [P, GN])
        bias_row = sb("bias_row", [1, GN], BF16)
        Kblk = sb("Kblk", [P, GS, R, T])
        Cblk = sb("Cblk", [P, GS, R // 2, C, 2, E9])
        mx = sb("mx", [P, GS, R])
        mhl = sb("mhl", [P, GS, 2, R], BF16)
        identb = sb("identb", [P, P], BF16)
        mT = sb("mT", [2 * R, 2, P], BF16)
        Ex = sb("Ex", [P, 2, R * T])
        ExT = sb("ExT", [P, 2, R // 2, C, T])
        b_rec = sb("b_rec", [P, 2, R * C])
        b_y = sb("b_y", [P, 2, D])
        r_lg = sb("r_lg", [P, TILES, E])
        r_w = sb("r_w", [P, TILES, E])
        r_m = sb("r_m", [P, TILES])
        room = Kblk[:, :, :, :].rearrange("p b r n -> p (b r n)")
        r_p, r_t, r_k = (room[:, n * TILES * E:(n + 1) * TILES * E].rearrange("p (t e) -> p t e", e=E)
                         for n in range(3))
        room = Qblk[:, :, :, :].rearrange("p b r n -> p (b r n)")
        f_h = room[:, 0:2 * CH * GN].rearrange("p (m c n) -> p m c n", m=2, c=CH)
        f_sg = room[:, 2 * CH * GN:3 * CH * GN].rearrange("p (c n) -> p c n", c=CH)
        f_acc = sb("f_acc", [P, GT, D])

        names = """w_in x_in0 x_in1 con_in ffw_in set_z set_ps set_cp
            a_st a_ag a_ve a_rsd a_xnd a_xnT_ps a_xnTd a_qk_ps a_qkd a_v_ps a_vd a_r2 a_r1 a_rt a_mn a_ex a_ph
            a_qT_ps a_qTd a_kT_ps a_kcd a_qb a_s a_am a_av a_dn a_rc a_yd a_yT_ps a_yTd a_o a_x1
            b_st b_ag b_ve b_rsd b_xnd b_qT_ps b_qcd b_in b_cT_ps b_cTd b_bi b_kb b_cb b_s b_mx b_mh b_ml b_mT_ps
            b_mTd b_sh b_e b_eT_ps b_eTd b_av b_rc b_yd b_x2
            r_st r_ag r_ve r_rsd r_xf r_xfT_ps r_xfTd r_st2 r_ag2 r_ve2 r_rsd2 r_xn r_xnT_ps r_xnTd r_lg_ps r_lgd r_ch r_ex
            f_up f_si f_hd f_dn f_ac f_o""".split()
        S = {n: sem(n) for n in names}
        block = stack.enter_context(nc.Block())

        tok = x.rearrange("(t s) k d -> (s k) t d", s=2)
        tok_out = out.rearrange("(t s) k d -> (s k) t d", s=2)
        ctx_v = ctx.rearrange("b k d -> k b d")

        def group(i):
            return bass.ds(i * GT, GT)

        @block.sync
        def _(sp):
            sp.dma_start(con[:, :], consts).then_inc(S["con_in"], 16)
            for n, w in enumerate((wq, wk, wv, wo)):
                sp.dma_start(wraw[:, n, :], w).then_inc(S["w_in"], 16)
            sp.dma_start(X[:, 0:GT, :], tok[:, 0:GT, :]).then_inc(S["x_in0"], 16)
            sp.dma_start(gate_raw[:, :], gate_w).then_inc(S["w_in"], 16)
            sp.dma_start(lnp[:, 0:1], ln_scale.rearrange("(d a) -> d a", a=1)).then_inc(S["w_in"], 16)
            sp.dma_start(lnp[:, 1:2], ln_bias.rearrange("(d a) -> d a", a=1)).then_inc(S["w_in"], 16)
            sp.dma_start(X[:, GT:TILES, :], tok[:, GT:TILES, :]).then_inc(S["x_in1"], 16)

            def load_ctx(j):
                for half in range(2):
                    sp.dma_start(ctxD[half * T:(half + 1) * T, :, :],
                                 ctx_v[:, bass.ds(j * GS, GS), :]).then_inc(S["b_in"], 16)
                sp.dma_start(maskB[:, :], mask[bass.ds(j * GS, GS), :].rearrange("b k -> (b k)")
                             .rearrange("(o n) -> o n", o=1).to_broadcast([P, GN])).then_inc(S["b_in"], 16)

            load_ctx(0)
            for n, w in enumerate((wg, wu)):
                sp.dma_start(wup[:, 0:E, n, :], w.rearrange("e d i -> d e i")).then_inc(S["ffw_in"], 16)
            for n, w in enumerate((swg, swu)):
                sp.dma_start(wup[:, E, n, :], w).then_inc(S["ffw_in"], 16)
            for c in range(CH):
                sp.dma_start(wdn[:, 0:E, c, :],
                             wd[:, c * P:(c + 1) * P, :].rearrange("e i d -> i e d")).then_inc(S["ffw_in"], 16)
                sp.dma_start(wdn[:, E, c, :], swd[c * P:(c + 1) * P, :]).then_inc(S["ffw_in"], 16)
            with sp.Fori(1, GROUPS) as j:
                sp.wait_ge(S["con_in"], 16)
                sp.wait_ge(S["b_cT_ps"], j)
                sp.wait_ge(S["b_cb"], 4 * j)
                sp.wait_ge(S["b_bi"], j)
                sp.wait_ge(S["b_cTd"], j)
                load_ctx(j)
            with sp.Fori(0, GROUPS) as i:
                sp.wait_ge(S["f_ac"], (E + 1) * i + E + 1)
                sp.dma_start(tok_out[:, group(i), :], f_acc[:, :, :]).then_inc(S["f_o"], 16)
            sp.wait_ge(S["f_o"], 16 * GROUPS)

        @block.tensor
        def _(pe):
            pe.wait_ge(S["con_in"], 16)
            pe.wait_ge(S["w_in"], 7 * 16)
            for n in range(4):
                pe.transpose(banks[0][:, n * D:(n + 1) * D], wraw[:, n, :], ident)
            pe.transpose(banks[1][:, 0:E], gate_raw[:, :], ident[0:E, 0:E]).then_inc(S["set_ps"], 1)
            pe.wait_ge(S["set_cp"], 6)
            pe.wait_ge(S["set_z"], 7)

            def a_norm_T(i):
                pe.wait_ge(S["a_xnd"], GT * i + GT)
                for t in range(GT):
                    ins = pe.transpose(banks[0][:, t * P:(t + 1) * P], a_xn[:, t, :], ident)
                ins.then_inc(S["a_xnT_ps"], 1)

            def a_project(i):
                pe.wait_ge(S["a_xnTd"], i + 1)
                for h in range(2):
                    for t in range(2):
                        n = 2 * h + t
                        ins = pe.matmul(banks[1 + h][:, t * 2 * D:(t + 1) * 2 * D], a_xnT[:, n * P:(n + 1) * P],
                                        wqkvT[:, 0:2 * D], start=True, stop=True)
                    ins.then_inc(S["a_qk_ps"], 1)
                for b in range(GS):
                    for c in range(C):
                        ins = pe.matmul(banks[0][c * T:(c + 1) * T, b * T:(b + 1) * T], a_xnT[:, b * T:(b + 1) * T],
                                        wqkvT[:, 2 * D + c * T:2 * D + (c + 1) * T], start=True, stop=True)
                ins.then_inc(S["a_v_ps"], 1)

            def a_qk_T(i):
                pe.wait_ge(S["a_ph"], i + 1)
                pe.wait_ge(S["a_qkd"], 2 * i + 2)
                for t in range(GT):
                    ins = pe.transpose(banks[2][:, t * P:(t + 1) * P], phi[:, t, 0, :], ident)
                ins.then_inc(S["a_qT_ps"], 1)
                pe.wait_ge(S["a_vd"], C * i + C)
                for t in range(GT):
                    ins = pe.transpose(banks[0][:, t * P:(t + 1) * P], phi[:, t, 1, :], ident)
                ins.then_inc(S["a_kT_ps"], 1)

            def a_scores(i, b):
                if b == 0:
                    pe.wait_ge(S["a_qb"], R * i + R)
                    pe.wait_ge(S["a_kcd"], C * i + C)
                if b >= 2:
                    pe.wait_ge(S["a_am"], GS * i + b - 1)
                pe.matmul(banks[b % 2][:, :], Kc[:, b, :, :].rearrange("p c n -> p (c n)"),
                          Qblk[:, b, :, :], start=True, stop=True).then_inc(S["a_s"], 1)

            def a_values(i, b):
                pe.wait_ge(S["a_am"], GS * i + b + 1)
                if b == GS // 2:
                    pe.wait_ge(S["a_yd"], GT * i + 2)
                t, s = b // 2, b % 2
                for r in range(R):
                    at = t % 2 * H * E9 + r * C * E9
                    ins = pe.matmul(banks[2][s * T:(s + 1) * T, at:at + C * E9], Am[:, b % 2, r * T:(r + 1) * T],
                                    Vblk[:, b, r, :, :].rearrange("p c e -> p (c e)"), start=True, stop=True)
                ins.then_inc(S["a_av"], 1)

            def a_out(i):
                pe.wait_ge(S["a_yd"], GT * i + GT)
                for t in range(GT):
                    ins = pe.transpose(banks[0][:, t * P:(t + 1) * P], a_y[:, t, :], ident)
                ins.then_inc(S["a_yT_ps"], 1)
                pe.wait_ge(S["a_yTd"], i + 1)
                for t in range(GT):
                    ins = pe.matmul(banks[1][:, t * D:(t + 1) * D], a_yT[:, t * P:(t + 1) * P], woT[:, :],
                                    start=True, stop=True)
                ins.then_inc(S["a_o"], 1)

            def b_ctx_T(j):
                for b in range(GS):
                    ins = pe.transpose(banks[3][:, b * T:(b + 1) * T], ctxD[0:T, b, :], ident[0:T, 0:T])
                ins.then_inc(S["b_cT_ps"], 1)

            def b_norm_T(j):
                pe.wait_ge(S["b_in"], 48 * j + 48)
                pe.wait_ge(S["b_xnd"], GT * j + GT)
                for t in range(GT):
                    ins = pe.transpose(banks[4][:, t * P:(t + 1) * P], b_xn[:, t, :], ident)
                ins.then_inc(S["b_qT_ps"], 1)

            def b_scores(j, b):
                if b == 0:
                    pe.wait_ge(S["b_qcd"], C * j + C)
                    pe.wait_ge(S["b_kb"], R * j + R)
                    pe.wait_ge(S["b_bi"], j + 1)
                    pe.wait_ge(S["b_cb"], 4 * j + 4)
                if b >= 2:
                    pe.wait_ge(S["b_e"], GS * j + b - 1)
                pe.matmul(banks[3 + b % 2][:, :], Qc[:, b, :, :].rearrange("p c n -> p (c n)"), Kblk[:, b, :, :],
                          start=True, stop=False)
                keys = bias_row[0:1, b * T:(b + 1) * T].rearrange("p (o n) -> p o n", o=1).to_broadcast([1, R, T])
                pe.matmul(banks[3 + b % 2][:, :], ones_row[0:1, :], keys, start=False, stop=True)\
                    .then_inc(S["b_s"], 1)

            def b_shift(j, b):
                pe.wait_ge(S["b_ml"], GS * j + b + 1)
                pe.transpose(banks[5][0:2 * R, 0:T].bitcast(BF16), mhl[:, b, :, :].rearrange("p a r -> p (a r)"),
                             identb[:, :]).then_inc(S["b_mT_ps"], 1)
                pe.wait_ge(S["b_mTd"], GS * j + b + 1)
                pe.matmul(banks[3 + b % 2][:, :], mT[:, b % 2, :], ind[:, :], start=False, stop=True,
                          skip_group_check=True).then_inc(S["b_sh"], 1)

            def b_probs_T(j, b):
                pe.wait_ge(S["b_e"], GS * j + b + 1)
                if b >= 1:
                    pe.wait_ge(S["b_eTd"], GS * j + b)
                for rp in range(R // 2):
                    ins = pe.transpose(banks[6][:, rp * P:(rp + 1) * P], Ex[:, b % 2, rp * P:(rp + 1) * P], ident)
                ins.then_inc(S["b_eT_ps"], 1)

            def b_values(j, b):
                pe.wait_ge(S["b_eTd"], GS * j + b + 1)
                if b == GS // 2:
                    pe.wait_ge(S["b_x2"], 2 * j + 1)
                t, s = b // 2, b % 2
                for rp in range(R // 2):
                    for c in range(C):
                        at = t % 2 * H * E9 + (rp * C + c) * 2 * E9
                        ins = pe.matmul(banks[7][s * T:(s + 1) * T, at:at + 2 * E9], ExT[:, b % 2, rp, c, :],
                                        Cblk[:, b, rp, c, :, :].rearrange("p q e -> p (q e)"),
                                        start=True, stop=True)
                ins.then_inc(S["b_av"], 1)

            def step(i, j):
                if i is not None:
                    a_norm_T(i)
                if j is not None:
                    b_norm_T(j)
                    b_ctx_T(j)
                if i is not None:
                    a_project(i)
                    a_qk_T(i)
                for k in range(GS + 3):
                    if i is not None and k < GS:
                        a_scores(i, k)
                    if j is not None and 2 <= k < GS + 2:
                        b_probs_T(j, k - 2)
                    if i is not None and 1 <= k <= GS:
                        a_values(i, k - 1)
                    if j is not None and 3 <= k:
                        b_values(j, k - 3)
                    if j is not None and k < GS:
                        b_scores(j, k)
                    if j is not None and 1 <= k <= GS:
                        b_shift(j, k - 1)
                if i is not None:
                    a_out(i)

            step(0, None)
            with pe.Fori(1, GROUPS) as i:
                step(i, i - 1)
            step(None, GROUPS - 1)

            with pe.Fori(0, GROUPS) as i:
                pe.wait_ge(S["r_xf"], GT * i + GT)
                for t in range(GT):
                    ins = pe.transpose(banks[0][:, t * P:(t + 1) * P], a_xn[:, t, :], ident)
                ins.then_inc(S["r_xfT_ps"], 1)
                pe.wait_ge(S["r_xn"], GT * i + GT)
                for t in range(GT):
                    ins = pe.transpose(banks[1][:, t * P:(t + 1) * P], b_xn[:, t, :], ident)
                ins.then_inc(S["r_xnT_ps"], 1)
                pe.wait_ge(S["r_xnTd"], i + 1)
                for t in range(GT):
                    ins = pe.matmul(banks[2][:, t * E:(t + 1) * E], a_xnT[:, t * P:(t + 1) * P], gateT[:, :],
                                    start=True, stop=True)
                ins.then_inc(S["r_lg_ps"], 1)
                pe.wait_ge(S["r_lgd"], i + 1)

            pe.wait_ge(S["ffw_in"], 8 * 16)

            def down(i, e):
                pe.wait_ge(S["f_hd"], ((E + 1) * i + e) * CH + CH)
                if e >= 2:
                    pe.wait_ge(S["f_ac"], (E + 1) * i + e - 1)
                for t in range(GT):
                    for c in range(CH):
                        ins = pe.matmul(banks[4 + e % 2][:, t * D:(t + 1) * D], f_h[:, e % 2, c, t * P:(t + 1) * P],
                                        wdn[:, (e + E) % (E + 1), c, :], start=(c == 0), stop=(c == CH - 1))
                ins.then_inc(S["f_dn"], 1)

            with pe.Fori(0, GROUPS) as i:
                for e in range(E + 2):
                    if e <= E:
                        for c in range(CH):
                            if e > 0:
                                pe.wait_ge(S["f_hd"], ((E + 1) * i + e - 1) * CH + c + 1)
                            for m in range(2):
                                ins = pe.matmul(banks[2 * c + m][:, :],
                                                wup[:, (e + E) % (E + 1), m, c * P:(c + 1) * P],
                                                xfT[:, bass.ds(i * GN, GN)], start=True, stop=True)
                            ins.then_inc(S["f_up"], 1)
                    if e >= 1:
                        down(i, e - 1)
                pe.wait_ge(S["f_ac"], (E + 1) * i + E + 1)

        @block.scalar
        def _(act):
            act.wait_ge(S["set_ps"], 1)
            act.wait_ge(S["set_z"], 7)
            act.copy(wqkvT[:, :], banks[0][:, 0:3 * D]).then_inc(S["set_cp"], 1)
            act.copy(woT[:, :], banks[0][:, 3 * D:4 * D]).then_inc(S["set_cp"], 1)
            act.copy(gateT[:, :], banks[1][:, 0:E]).then_inc(S["set_cp"], 1)

            def a_front(i):
                act.wait_ge(S["a_xnT_ps"], i + 1)
                act.copy(a_xnT[:, :], banks[0][:, :]).then_inc(S["a_xnTd"], 1)
                for h in range(2):
                    act.wait_ge(S["a_qk_ps"], 2 * i + h + 1)
                    act.copy(qk[:, h * GN:(h + 1) * GN], banks[1 + h][:, :]).then_inc(S["a_qkd"], 1)
                act.wait_ge(S["a_v_ps"], i + 1)
                for c in range(C):
                    rows = slice(c * T, (c + 1) * T)
                    src = banks[0][rows, :].rearrange("p (b r e) -> p b r e", r=R, e=DH)
                    act.copy(Vblk[rows, :, :, c, 0:DH], src).then_inc(S["a_vd"], 1)

            def a_middle(i):
                act.wait_ge(S["a_mn"], i + 1)
                act.activation(rot2[:, :], rot2[:, :], ACT.Exp).then_inc(S["a_ex"], 1)
                act.wait_ge(S["a_qT_ps"], i + 1)
                act.copy(qT[:, :], banks[2][:, :]).then_inc(S["a_qTd"], 1)
                act.wait_ge(S["a_kT_ps"], i + 1)
                for c in range(C):
                    rows = slice(c * T, (c + 1) * T)
                    act.copy(Kc[rows, :, c, :], banks[0][rows, :].rearrange("p (b n) -> p b n", n=T)).then_inc(S["a_kcd"], 1)

            def a_back(i):
                act.wait_ge(S["a_yT_ps"], i + 1)
                act.copy(a_yT[:, :], banks[0][:, :]).then_inc(S["a_yTd"], 1)

            def b_front(j):
                act.wait_ge(S["b_qT_ps"], j + 1)
                for c in range(C):
                    rows = slice(c * T, (c + 1) * T)
                    act.copy(Qc[rows, :, c, :], banks[4][rows, :].rearrange("p (b n) -> p b n", n=T)).then_inc(S["b_qcd"], 1)

            def b_exp(j, b):
                act.wait_ge(S["b_mT_ps"], GS * j + b + 1)
                act.copy(mT[:, b % 2, :], banks[5][0:2 * R, 0:T].bitcast(BF16)).then_inc(S["b_mTd"], 1)
                act.wait_ge(S["b_sh"], GS * j + b + 1)
                act.activation(Ex[:, b % 2, :], banks[3 + b % 2][:, :], ACT.Exp, scale=SCALE)\
                    .then_inc(S["b_e"], 1)

            def b_probs(j, b):
                act.wait_ge(S["b_eT_ps"], GS * j + b + 1)
                act.copy(ExT[:, b % 2].rearrange("p r c q -> p (r c q)"), banks[6][:, :]).then_inc(S["b_eTd"], 1)

            def step(i, j):
                if i is not None:
                    a_front(i)
                if j is not None:
                    b_front(j)
                if i is not None:
                    a_middle(i)
                if j is not None:
                    for k in range(GS + 2):
                        if 2 <= k:
                            b_probs(j, k - 2)
                        if 1 <= k <= GS:
                            b_exp(j, k - 1)
                if i is not None:
                    a_back(i)

            step(0, None)
            with act.Fori(1, GROUPS) as i:
                step(i, i - 1)
            step(None, GROUPS - 1)

            with act.Fori(0, GROUPS) as i:
                act.wait_ge(S["r_xfT_ps"], i + 1)
                act.copy(xfT[:, bass.ds(i * GN, GN)], banks[0][:, :]).then_inc(S["r_xfTd"], 1)
                act.wait_ge(S["r_xnT_ps"], i + 1)
                act.activation(a_xnT[:, :], banks[1][:, :], ACT.Identity, bias=lnp[:, 1:2], scale=lnp[:, 0:1])\
                    .then_inc(S["r_xnTd"], 1)
            act.wait_ge(S["r_ch"], 2)
            act.activation(r_p[:, :, :], r_p[:, :, :], ACT.Exp).then_inc(S["r_ex"], 1)
            with act.Fori(0, GROUPS) as i:
                for e in range(E + 1):
                    for c in range(CH):
                        act.wait_ge(S["f_up"], ((E + 1) * i + e) * CH + c + 1)
                        act.activation(f_sg[:, c, :], banks[2 * c][:, :], ACT.Silu).then_inc(S["f_si"], 1)

        @block.gpsimd
        def _(pool):
            pool.memset(Kc[:, :, :, :], 0.0).then_inc(S["set_z"], 1)
            pool.memset(Qc[:, :, :, :], 0.0).then_inc(S["set_z"], 1)
            pool.memset(ones_row[:, :], 1.0).then_inc(S["set_z"], 1)
            pool.memset(Vblk[:, :, :, :, :], 0.0).then_inc(S["set_z"], 1)
            pool.memset(Cblk[:, :, :, :, :, :], 0.0).then_inc(S["set_z"], 1)
            pool.memset(minus_half[:, :], -0.5).then_inc(S["set_z"], 1)
            pool.wait_ge(S["set_z"], 6)
            pool.wait_ge(S["con_in"], 16)
            for c in range(C):
                mark = halves[:, c:c + 1].rearrange("p (a o) -> p a o", o=1)
                pool.tensor_copy(Vblk[:, :, :, c, DH], mark.to_broadcast([P, GS, R]))
                for q in range(2):
                    mark = halves[:, q:q + 1].rearrange("p (a o) -> p a o", o=1)
                    ins = pool.tensor_copy(Cblk[:, :, :, c, q, DH], mark.to_broadcast([P, GS, R // 2]))
            ins.then_inc(S["set_z"], 1)

            def rsqrt(i, rs, s_ve, s_rs):
                pool.wait_ge(s_ve, i + 1)
                pool.tensor_tensor(rs[:, :], rs[:, :], minus_half[:, :], ALU.pow).then_inc(s_rs, 1)

            def a_rope(i):
                pool.wait_ge(S["a_qkd"], 2 * i + 2)
                src = qk[:, :].rearrange("p (n s f) -> p n s f", s=2, f=HALF)
                dst = rot2[:, :].rearrange("p (n s f) -> p n s f", s=2, f=HALF)
                for half in range(2):
                    pool.tensor_tensor(dst[:, :, half, :], src[:, :, 1 - half, :],
                                       sin.rearrange("p (o f) -> p o f", o=1).to_broadcast([P, GT * 2 * H, HALF]),
                                       ALU.mult).then_inc(S["a_r2"], 1)

            def a_blocks(i):
                pool.wait_ge(S["a_qTd"], i + 1)
                for r in range(5, R):
                    pool.tensor_tensor(Qblk[:, :, r, :], qT[:, :].rearrange("p (b n) -> p b n", n=T),
                                       row[:, r:r + 1].rearrange("p (a o) -> p a o", o=1).to_broadcast([P, GS, T]), ALU.mult).then_inc(S["a_qb"], 1)

            def b_context(j):
                src = ctxD[:, :, :].rearrange("p b (c r q e) -> p c q b r e", c=C, q=2, e=DH)
                for c in range(C):
                    for q in range(2):
                        mark = halves[:, q:q + 1].rearrange("p (a b o) -> p a b o", a=1, o=1)
                        pool.tensor_tensor(Cblk[:, :, :, c, q, 0:DH], src[:, c, q],
                                           mark.to_broadcast([P, GS, R // 2, DH]), ALU.mult).then_inc(S["b_cb"], 1)

            def b_blocks(j):
                pool.wait_ge(S["b_cTd"], j + 1)
                for r in range(5, R):
                    pool.tensor_tensor(Kblk[:, :, r, :], ctxT[:, :].rearrange("p (b n) -> p b n", n=T),
                                       row[:, r:r + 1].rearrange("p (a o) -> p a o", o=1).to_broadcast([P, GS, T]), ALU.mult).then_inc(S["b_kb"], 1)

            def step(i, j):
                if i is not None:
                    rsqrt(i, a_rs, S["a_ve"], S["a_rsd"])
                if j is not None:
                    pool.wait_ge(S["b_in"], 48 * j + 48)
                    rsqrt(j, b_rs, S["b_ve"], S["b_rsd"])
                    b_context(j)
                    b_blocks(j)
                if i is not None:
                    a_rope(i)
                    a_blocks(i)

            step(0, None)
            with pool.Fori(1, GROUPS) as i:
                step(i, i - 1)
            step(None, GROUPS - 1)
            with pool.Fori(0, GROUPS) as i:
                rsqrt(i, a_rs, S["r_ve"], S["r_rsd"])
                rsqrt(i, b_rs, S["r_ve2"], S["r_rsd2"])

        @block.vector
        def _(dve):
            dve.wait_ge(S["con_in"], 16)
            dve.wait_ge(S["set_z"], 7)
            dve.tensor_copy(ind[:, :], const("ind")[0:2 * R, :]).then_inc(S["set_cp"], 1)
            dve.tensor_copy(identb[:, :], ident).then_inc(S["set_cp"], 1)
            dve.memset(f_acc[:, :, :], 0.0).then_inc(S["set_cp"], 1)

            def norm(i, src, stat, mv, rs, dst, s_st, s_ag, s_ve, s_rs, s_xn):
                for t in range(GT):
                    dve.bn_stats(stat[:, t, :], src(t)).then_inc(s_st, 1)
                dve.wait_ge(s_st, GT * i + GT)
                dve.memset(rs[:, :], LN_EPS)
                for t in range(GT):
                    dve.bn_aggr(mv[:, t, :], stat[:, t, :]).then_inc(s_ag, 1)
                dve.wait_ge(s_ag, GT * i + GT)
                dve.tensor_tensor(rs[:, :], rs[:, :], mv[:, :, 1], ALU.add).then_inc(s_ve, 1)
                dve.wait_ge(s_rs, i + 1)
                for t in range(GT):
                    dve.tensor_scalar(dst[:, t, :], src(t), mv[:, t, 0:1], rs[:, t:t + 1], ALU.subtract, ALU.mult)\
                        .then_inc(s_xn, 1)

            def x_tile(i):
                return lambda t: X[:, bass.ds(i * GT + t, 1), :].rearrange("p o d -> p (o d)")

            def a_norm(i):
                if isinstance(i, int):
                    dve.wait_ge(S["x_in0"], 16)
                else:
                    dve.wait_ge(S["x_in1"], 16)
                norm(i, x_tile(i), a_stat, a_mv, a_rs, a_xn, S["a_st"], S["a_ag"], S["a_ve"], S["a_rsd"], S["a_xnd"])

            def b_norm(j):
                dve.wait_ge(S["a_x1"], j + 1)
                norm(j, x_tile(j), b_stat, b_mv, b_rs, b_xn, S["b_st"], S["b_ag"], S["b_ve"], S["b_rsd"], S["b_xnd"])

            def a_feature(i):
                dve.wait_ge(S["a_qkd"], 2 * i + 2)
                n = GT * 2 * H * 2
                dve.tensor_tensor(rot[:, :].rearrange("p (n f) -> p n f", f=HALF),
                                  qk[:, :].rearrange("p (n f) -> p n f", f=HALF),
                                  cos.rearrange("p (o f) -> p o f", o=1).to_broadcast([P, n, HALF]), ALU.mult)\
                    .then_inc(S["a_r1"], 1)
                dve.wait_ge(S["a_r1"], i + 1)
                dve.wait_ge(S["a_r2"], 2 * i + 2)
                for half, op in ((0, ALU.subtract), (1, ALU.add)):
                    v = rot[:, :].rearrange("p (n s f) -> p n s f", s=2, f=HALF)[:, :, half, :]
                    w = rot2[:, :].rearrange("p (n s f) -> p n s f", s=2, f=HALF)[:, :, half, :]
                    dve.tensor_tensor(v, v, w, op).then_inc(S["a_rt"], 1)
                dve.wait_ge(S["a_rt"], 2 * i + 2)
                dve.tensor_scalar(rot2[:, :], rot[:, :], 0.0, None, ALU.min).then_inc(S["a_mn"], 1)

            def a_feature2(i):
                dve.wait_ge(S["a_ex"], i + 1)
                dve.scalar_tensor_tensor(phi[:, :, :, :].rearrange("p t a d -> p (t a d)"), rot[:, :], 0.0, rot2[:, :],
                                         ALU.max, ALU.add).then_inc(S["a_ph"], 1)

            def a_blocks(i):
                dve.wait_ge(S["a_qTd"], i + 1)
                for r in range(5):
                    dve.tensor_scalar(Qblk[:, :, r, :], qT[:, :].rearrange("p (b n) -> p b n", n=T),
                                      row[:, r:r + 1], None, ALU.mult).then_inc(S["a_qb"], 1)

            def a_mask(i, b):
                dve.wait_ge(S["a_s"], GS * i + b + 1)
                if b >= 2:
                    dve.wait_ge(S["a_av"], GS * i + b - 1)
                dve.tensor_tensor(Am[:, b % 2, :].rearrange("p (r n) -> p r n", n=T),
                                  banks[b % 2][:, :].rearrange("p (r n) -> p r n", n=T),
                                  causal.rearrange("p (o n) -> p o n", o=1).to_broadcast([P, R, T]), ALU.mult)\
                    .then_inc(S["a_am"], 1)

            def a_divide(i, h):
                dve.wait_ge(S["a_av"], GS * i + (h + 1) * (GS // 2))
                num = banks[2][:, 0:2 * H * E9].rearrange("p (t n e) -> p t n e", t=2, e=E9)
                dve.tensor_scalar(a_den[:, :, :], num[:, :, :, DH], DEN_EPS, None, ALU.max).then_inc(S["a_dn"], 1)
                dve.wait_ge(S["a_dn"], 2 * i + h + 1)
                dve.reciprocal(a_rec[:, :, :], a_den[:, :, :]).then_inc(S["a_rc"], 1)
                dve.wait_ge(S["a_rc"], 2 * i + h + 1)
                for t in range(2):
                    dst = a_y[:, 2 * h + t, :].rearrange("p (c r e) -> p r c e", c=C, e=DH)
                    src = num[:, t, :, 0:DH].rearrange("p (r c) e -> p r c e", c=C)
                    rec = a_rec[:, t, :].rearrange("p (r c o) -> p r c o", c=C, o=1).to_broadcast([P, R, C, DH])
                    dve.tensor_tensor(dst, src, rec, ALU.mult).then_inc(S["a_yd"], 1)

            def a_residual(i):
                dve.wait_ge(S["a_o"], i + 1)
                xs = X[:, group(i), :]
                dve.tensor_tensor(xs, xs, banks[1][:, :].rearrange("p (t d) -> p t d", t=GT), ALU.add)\
                    .then_inc(S["a_x1"], 1)

            def b_context(j):
                dve.wait_ge(S["b_cT_ps"], j + 1)
                dve.scalar_tensor_tensor(ctxT[:, :], maskB[:, :], 0.0, banks[3][:, :], ALU.not_equal, ALU.mult)\
                    .then_inc(S["b_cTd"], 1)
                dve.tensor_scalar(bias_row[:, :], maskB[0:1, :], 0.0, MASKED, ALU.is_equal, ALU.mult)\
                    .then_inc(S["b_bi"], 1)
                dve.wait_ge(S["b_cTd"], j + 1)
                for r in range(5):
                    dve.tensor_scalar(Kblk[:, :, r, :], ctxT[:, :].rearrange("p (b n) -> p b n", n=T),
                                      row[:, r:r + 1], None, ALU.mult).then_inc(S["b_kb"], 1)

            def b_max(j, b):
                dve.wait_ge(S["b_s"], GS * j + b + 1)
                dve.tensor_reduce(mx[:, b, :], banks[3 + b % 2][:, :].rearrange("p (r n) -> p r n", n=T), AX, ALU.max)\
                    .then_inc(S["b_mx"], 1)
                dve.wait_ge(S["b_mx"], GS * j + b + 1)
                dve.tensor_scalar(mhl[:, b, 0, :], mx[:, b, :], -1.0, None, ALU.mult).then_inc(S["b_mh"], 1)
                dve.wait_ge(S["b_mh"], GS * j + b + 1)
                dve.scalar_tensor_tensor(mhl[:, b, 1, :], mx[:, b, :], -1.0, mhl[:, b, 0, :], ALU.mult, ALU.subtract)\
                    .then_inc(S["b_ml"], 1)

            def b_divide(j, h):
                dve.wait_ge(S["b_av"], GS * j + (h + 1) * (GS // 2))
                num = banks[7][:, 0:2 * H * E9].rearrange("p (t n e) -> p t n e", t=2, e=E9)
                dve.reciprocal(b_rec[:, :, :], num[:, :, :, DH]).then_inc(S["b_rc"], 1)
                dve.wait_ge(S["b_rc"], 2 * j + h + 1)
                for t in range(2):
                    for c in range(C):
                        dst = b_y[:, t, :].rearrange("p (c r q e) -> p c r q e", c=C, q=2, e=DH)[:, c]
                        src = num[:, t, :, 0:DH].rearrange("p (r c q) e -> p c r q e", c=C, q=2)[:, c]
                        rec = b_rec[:, t, :].rearrange("p (r c q o) -> p c r q o", c=C, q=2, o=1)[:, c]\
                            .to_broadcast([P, R // 2, 2, DH])
                        ins = dve.tensor_tensor(dst, src, rec, ALU.mult)
                        ins.then_inc(S["b_yd"], 1)
                dve.wait_ge(S["b_yd"], 8 * j + 4 * h + 4)
                xs = X[:, bass.ds(j * GT + 2 * h, 2), :]
                dve.tensor_tensor(xs, xs, b_y[:, :, :], ALU.add).then_inc(S["b_x2"], 1)

            def step(i, j):
                if i is not None:
                    a_norm(i)
                if j is not None:
                    b_norm(j)
                    b_context(j)
                if i is not None:
                    a_feature(i)
                    a_feature2(i)
                    a_blocks(i)
                for k in range(GS + 3):
                    if i is not None and k < GS:
                        a_mask(i, k)
                    if j is not None and k < GS:
                        b_max(j, k)
                    if i is not None and k in (4, 8):
                        a_divide(i, k // 4 - 1)
                    if j is not None and k in (6, 10):
                        b_divide(j, (k - 6) // 4)
                if i is not None:
                    a_residual(i)

            step(0, None)
            with dve.Fori(1, GROUPS) as i:
                step(i, i - 1)
            step(None, GROUPS - 1)

            dve.wait_ge(S["b_x2"], 2 * GROUPS)
            with dve.Fori(0, GROUPS) as i:
                norm(i, x_tile(i), a_stat, a_mv, a_rs, a_xn, S["r_st"], S["r_ag"], S["r_ve"], S["r_rsd"], S["r_xf"])
                dve.wait_ge(S["r_xf"], GT * i + GT)
                norm(i, lambda t: a_xn[:, t, :], b_stat, b_mv, b_rs, b_xn, S["r_st2"], S["r_ag2"], S["r_ve2"], S["r_rsd2"],
                     S["r_xn"])
                dve.wait_ge(S["r_lg_ps"], i + 1)
                dve.tensor_copy(r_lg[:, group(i), :], banks[2][:, 0:GT * E].rearrange("p (t e) -> p t e", e=E))\
                    .then_inc(S["r_lgd"], 1)

            done = [0]

            def chain(ins):
                done[0] += 1
                ins.then_inc(S["r_ch"], 1)
                dve.wait_ge(S["r_ch"], done[0])

            def per_token(v):
                return v[:, :].rearrange("p (t o) -> p t o", o=1).to_broadcast([P, TILES, E])

            order = const("lower").rearrange("p (o e) -> p o e", o=1).to_broadcast([P, TILES, E])
            dve.wait_ge(S["r_lgd"], GROUPS)
            chain(dve.tensor_reduce(r_m[:, :], r_lg[:, :, :], AX, ALU.max))
            chain(dve.tensor_tensor(r_p[:, :, :], r_lg[:, :, :], per_token(r_m), ALU.subtract))
            dve.wait_ge(S["r_ex"], 1)
            chain(dve.tensor_reduce(r_m[:, :], r_p[:, :, :], AX, ALU.add))
            chain(dve.reciprocal(r_m[:, :], r_m[:, :]))
            chain(dve.tensor_tensor(r_p[:, :, :], r_p[:, :, :], per_token(r_m), ALU.mult))
            chain(dve.tensor_copy(r_t[:, :, :], r_p[:, :, :]))
            for n in range(2):
                chain(dve.tensor_reduce(r_m[:, :], r_t[:, :, :], AX, ALU.max))
                chain(dve.tensor_tensor(r_k[:, :, :], r_t[:, :, :], per_token(r_m), ALU.is_equal))
                chain(dve.tensor_tensor(r_k[:, :, :], r_k[:, :, :], order, ALU.mult))
                chain(dve.tensor_reduce(r_m[:, :], r_k[:, :, :], AX, ALU.max))
                chain(dve.tensor_tensor(r_k[:, :, :], order, per_token(r_m), ALU.is_equal))
                if n == 0:
                    chain(dve.tensor_copy(r_w[:, :, :], r_k[:, :, :]))
                    chain(dve.scalar_tensor_tensor(r_t[:, :, :], r_k[:, :, :], -2.0, r_t[:, :, :], ALU.mult, ALU.add))
                else:
                    chain(dve.tensor_tensor(r_w[:, :, :], r_w[:, :, :], r_k[:, :, :], ALU.add))
            chain(dve.tensor_tensor(r_w[:, :, :], r_w[:, :, :], r_p[:, :, :], ALU.mult))
            chain(dve.tensor_reduce(r_m[:, :], r_w[:, :, :], AX, ALU.add))
            chain(dve.tensor_scalar(r_m[:, :], r_m[:, :], TOP_EPS, None, ALU.add))
            chain(dve.reciprocal(r_m[:, :], r_m[:, :]))
            chain(dve.tensor_tensor(r_w[:, :, :], r_w[:, :, :], per_token(r_m), ALU.mult))

            def add_expert(i, e):
                n = (E + 1) * i + e
                dve.wait_ge(S["f_dn"], n + 1)
                bank = banks[4 + e % 2][:, :].rearrange("p (t d) -> p t d", t=GT)
                if e == 0:
                    if not (isinstance(i, int) and i == 0):
                        dve.wait_ge(S["f_o"], 16 * i)
                    dve.tensor_tensor(f_acc[:, :, :], X[:, group(i), :], bank, ALU.add).then_inc(S["f_ac"], 1)
                    return
                dve.wait_ge(S["f_ac"], n)
                for t in range(GT):
                    w = r_w[:, bass.ds(i * GT + t, 1), e - 1:e].rearrange("p o e -> p (o e)")
                    ins = dve.scalar_tensor_tensor(f_acc[:, t, :], bank[:, t, :], w, f_acc[:, t, :], ALU.mult, ALU.add)
                ins.then_inc(S["f_ac"], 1)

            def experts(i):
                for e in range(E + 2):
                    if e <= E:
                        for c in range(CH):
                            n = ((E + 1) * i + e) * CH + c
                            dve.wait_ge(S["f_si"], n + 1)
                            dve.tensor_tensor(f_h[:, e % 2, c, :], f_sg[:, c, :], banks[2 * c + 1][:, :], ALU.mult)\
                                .then_inc(S["f_hd"], 1)
                    if e >= 1:
                        add_expert(i, e - 1)

            experts(0)
            with dve.Fori(1, GROUPS) as i:
                experts(i)


_INS = ["x", "ctx_1024", "mask_BxS2_if1", "L0_attn_Wq", "L0_attn_Wk", "L0_attn_Wv", "L0_attn_Wo", "L0_ffn_ln_scale",
        "L0_ffn_ln_bias", "L0_ffn_gate_w", "L0_ffn_Wg", "L0_ffn_Wu", "L0_ffn_Wd", "L0_ffn_sWg", "L0_ffn_sWu",
        "L0_ffn_sWd"]


def kernel(**inputs):
    import numpy as _np
    import concourse.bacc as _bacc
    from concourse import mybir as _mybir
    from concourse.bass_utils import run_bass_kernel_spmd as _run

    nc = _bacc.Bacc("TRN2", target_bir_lowering=False, num_devices=1)
    arrays, args = {}, []
    for name in _INS:
        a = _np.ascontiguousarray(inputs[name])
        arrays[f"in_{name}"] = a
        args.append(nc.dram_tensor(f"in_{name}", a.shape, _mybir.dt.from_np(a.dtype), kind="ExternalInput").ap())
    a = shape_constants()
    arrays["shape_constants"] = a
    args.append(nc.dram_tensor("shape_constants", a.shape, _mybir.dt.from_np(a.dtype), kind="ExternalInput").ap())
    args.append(nc.dram_tensor("block_out", (SEQS, T, D), _mybir.dt.float32, kind="ExternalOutput").ap())
    decoder_block(nc, *args)
    r = _run(nc, [arrays], core_ids=[0])
    return r.results[0]["block_out"]
```

```python
import numpy as np
import concourse.bass as bass
from concourse import mybir
from contextlib import ExitStack

F32 = mybir.dt.float32
BF16 = mybir.dt.bfloat16
I32 = mybir.dt.int32
ALU = mybir.AluOpType
ACT = mybir.ActivationFunctionType
AX = mybir.AxisListType.X

P = 128
SEQS, T, D = 128, 64, 128
TOKENS = SEQS * T
H, DH = 16, 8
HALF = DH // 2
TILES = TOKENS // P
GT = 4
GROUPS = TILES // GT
GS = GT * P // T
GN = GT * P
R, C = 8, 2
E9 = DH + 1
BEHIND = 4
RING = 4
E, INTER, TOP = 8, 256, 2
CH = INTER // P
LN_EPS, DEN_EPS, TOP_EPS = 1e-5, 1e-6, 1e-5
SCALE = DH ** -0.5
MASKED = -1e9 / SCALE
REGION = TOKENS + P
TILE_MAX = (TOP * TOKENS + E * (P - 1)) // P
SPARE = TILE_MAX - TOP * TOKENS // P
ROW = D + 2
NOWHERE = 1 << 20
UNROLL = 5
TURNS = TILE_MAX // UNROLL
THIRD = (0, 1, 2, 0, 1)
SCATTER_SLOTS = (2, 4, 6, 7)
TILE_BITS = 7
C_STEPS = 24
B_LOADS = 4
SET_ZERO, SET_DVE = 10, 8
Y_RING = 4

CONST = {"ident": P, "causal": T, "cos": HALF, "sin": HALF, "row": R, "half": C, "order": E, "before": P,
         "region": E, "place": GT * TOP, "upto": E * E, "tile": TILE_MAX}
CONST_AT = dict(zip(CONST, np.cumsum([0, *CONST.values()])[:-1].tolist()))
CONST_N = sum(CONST.values())


def shape_constants():
    c = np.zeros((P, CONST_N), np.float32)

    def part(name):
        return c[:, CONST_AT[name]:CONST_AT[name] + CONST[name]]

    p = np.arange(P)
    part("ident")[:] = np.eye(P)
    part("causal")[:] = (p % T)[:, None] <= np.arange(T)[None, :]
    inv = np.float32(10000.0) ** (-np.arange(HALF, dtype=np.float32) / np.float32(HALF))
    ang = (p % T).astype(np.float32)[:, None] * inv[None, :].astype(np.float32)
    part("cos")[:] = np.cos(ang)
    part("sin")[:] = np.sin(ang)
    part("row")[:] = (p // DH % R)[:, None] == np.arange(R)[None, :]
    part("half")[:] = (p // T)[:, None] == np.arange(C)[None, :]
    part("order")[:] = np.arange(E, 0, -1)[None, :]
    part("before")[:] = p[:, None] < p[None, :]
    part("region")[:] = np.arange(E)[None, :] * REGION
    n = np.arange(GT * TOP)
    part("place")[:] = p[:, None] + (n // TOP * P + n % TOP * TOKENS)[None, :]
    part("upto")[:] = np.tril(np.ones((E, E))).reshape(1, -1)
    part("tile")[:] = np.arange(TILE_MAX)[None, :]
    return c


def indicator():
    return np.kron(np.tile(np.eye(R), (2, 1)), np.ones((1, T))).astype(np.float32)


def on(g):
    return not isinstance(g, int) or 0 <= g < GROUPS


def since(g, first):
    return not isinstance(g, int) or g >= first


def decoder_block(nc, x, ctx, mask, wq, wk, wv, wo, ln_scale, ln_bias, gate_w, wg, wu, wd, swg, swu, swd,
                  consts, ind_in, out):
    routed = nc.dram_tensor("routed", [E * REGION + SPARE * P, ROW], F32, kind="Internal").ap()
    mixed = nc.dram_tensor("mixed", [TOP * TOKENS, D], F32, kind="Internal").ap()

    with ExitStack() as stack:
        def sb(name, shape, dt=F32):
            return stack.enter_context(nc.sbuf_tensor(name, shape, dt))

        banks = [stack.enter_context(nc.psum_tensor(f"bank{n}", [P, 512], F32)) for n in range(8)]
        A_S, A_O, FRONT0, B_S, B_T, B_O, FRONT1 = 0, 1, 2, (3, 4), 5, 6, 7
        F_UP, F_HT, F_X, F_O = (0, 1, 2), (3, 4, 5), 6, 7

        X = sb("X", [P, TILES, D])
        xfT = sb("xfT", [P, TOKENS])
        con = sb("con", [P, CONST_N])
        wqkvT = sb("wqkvT", [P, 3 * D])
        woT = sb("woT", [P, D])
        gateT = sb("gateT", [P, E])
        gate_sum = sb("gate_sum", [P, 2, E])
        lnp = sb("lnp", [P, 2])
        shared_up_w = sb("shared_up_w", [P, 2, INTER])
        shared_down_w = sb("shared_down_w", [P, CH, D])
        ind = sb("ind", [2 * R, R * T], BF16)
        ones_row = sb("ones_row", [1, P], BF16)
        identb = sb("identb", [P, P], BF16)
        before = sb("before", [P, P], BF16)
        ones = sb("ones", [P, P], BF16)
        minus_half = sb("minus_half", [P, GT])

        def const(name):
            return con[:, CONST_AT[name]:CONST_AT[name] + CONST[name]]

        ident, causal, cos, sin, row, halves, order = (
            const(n) for n in ("ident", "causal", "cos", "sin", "row", "half", "order"))

        a_stat = sb("a_stat", [P, GT, 6])
        a_mv = sb("a_mv", [P, GT, 2])
        a_rs = sb("a_rs", [P, GT])
        a_xn = sb("a_xn", [P, GT, D])
        a_xnT = sb("a_xnT", [P, GN])
        qk = sb("qk", [P, GT * 2 * D])
        rot = sb("rot", [P, GT * 2 * D])
        phi = sb("phi", [P, GT * 2 * D])
        qT = sb("qT", [P, 2, GN])
        KQ = sb("KQ", [P, 2, 2, GS, C, T])
        Kc, Qc = KQ[:, 0], KQ[:, 1]
        Vblk = sb("Vblk", [P, 2, GS, R, C, E9])
        Qblk = sb("Qblk", [P, RING, R, T])
        Am = sb("Am", [P, 2, R * T])
        a_den = sb("a_den", [P, 2, R * C])
        a_rec = sb("a_rec", [P, 2, R * C])
        a_y = sb("a_y", [P, GT, D])
        a_yT = sb("a_yT", [P, GN])
        b_stat = sb("b_stat", [P, GT, 6])
        b_mv = sb("b_mv", [P, GT, 2])
        b_rs = sb("b_rs", [P, GT])
        b_xn = sb("b_xn", [P, GT, D])
        ctxP = sb("ctxP", [P, GT, D])
        ctxD = sb("ctxD", [P, GS, D])
        maskB = sb("maskB", [P, GN], I32)
        ctxT = sb("ctxT", [P, 2, GN])
        bias_row = sb("bias_row", [1, 2, GN], BF16)
        Kblk = sb("Kblk", [P, RING, R, T])
        Cblk = sb("Cblk", [P, 2, GS, R // 2, C, 2, E9])
        mx = sb("mx", [P, GS, R])
        mhl = sb("mhl", [P, GS, 2, R], BF16)
        mT = sb("mT", [2 * R, 2, P], BF16)
        Ex = sb("Ex", [P, 2, R * T])
        ExT = sb("ExT", [P, 2, R // 2, C, T])
        b_rec = sb("b_rec", [P, 2, R * C])
        b_y = sb("b_y", [P, 2, D])
        c_stat = sb("c_stat", [P, GT, 6])
        c_mv = sb("c_mv", [P, GT, 2])
        c_rs = sb("c_rs", [P, GT])
        c_stat2 = sb("c_stat2", [P, GT, 6])
        c_mv2 = sb("c_mv2", [P, GT, 2])
        c_rs2 = sb("c_rs2", [P, GT])
        c_row = sb("c_row", [P, 2, GT, TOP, ROW])
        c_xfT = sb("c_xfT", [P, GN])
        c_p = sb("c_p", [P, GT, E])
        c_t = sb("c_t", [P, GT, E])
        c_pick = sb("c_pick", [P, TOP, GT, E])
        c_sel = sb("c_sel", [P, GT, E], BF16)
        c_m = sb("c_m", [P, GT])
        c_best = sb("c_best", [P, TOP, GT])
        c_pos = sb("c_pos", [P, GT, E])
        c_hit = sb("c_hit", [P, TOP, GT, E])
        c_at = sb("c_at", [P, GT, TOP])
        c_idx = sb("c_idx", [P, 2, GT, TOP], I32)
        c_place = sb("c_place", [P, GT, TOP])
        c_base = sb("c_base", [P, E])
        pad = sb("pad", [P, ROW])
        tick = sb("tick", [P, UNROLL + 1])
        t_cnt = sb("t_cnt", [1, E])
        t_int = sb("t_int", [1, E], I32)
        t_nt = sb("t_nt", [1, E])
        t_sq = sb("t_sq", [1, E, E])
        t_end = sb("t_end", [1, E])
        t_ge = Kblk[0:1, :, :, :].rearrange("p m r n -> p (m r n)")[:, 0:TILE_MAX * E].rearrange("p (n e) -> p n e", e=E)
        t_e = sb("t_e", [1, TILE_MAX])
        t_st = sb("t_st", [1, TILE_MAX])
        t_pad = sb("t_pad", [1, E], I32)
        t_expert = sb("t_expert", [1, TILE_MAX], I32)
        t_row = sb("t_row", [1, TILE_MAX], I32)
        wup = KQ[:, :, :, :, :, :].rearrange("p a m b c n -> p (a m b c n)").rearrange("p (e m i) -> p e m i", e=E, m=2)
        wdn = Qblk[:, :, :, :].rearrange("p m r n -> p (m r n)").rearrange("p (e c d) -> p e c d", e=E, c=CH)
        s_sg = phi[:, :].rearrange("p (c n) -> p c n", c=CH)
        s_h = Vblk[:, :, :, :, :, :].rearrange("p m b r c e -> p (m b r c e)")[:, 0:2 * CH * GN]\
            .rearrange("p (m c n) -> p m c n", m=2, c=CH)
        f_x = sb("f_x", [P, UNROLL, ROW])
        f_xT = sb("f_xT", [P, 3, P])
        f_sg, f_h, f_hT = (room[:, n * 3 * INTER:(n + 1) * 3 * INTER].rearrange("p (m i) -> p m i", i=INTER)
                           for room, n in ((qk[:, :], 0), (rot[:, :], 0), (Am[:, :, :].rearrange("p m n -> p (m n)"), 0)))
        f_y = sb("f_y", [P, UNROLL, D])
        y_in = Cblk[:, :, :, :, :, :, :].rearrange("p m b r c q e -> p (m b r c q e)")
        y_in2 = Kblk[:, :, :, :].rearrange("p m r n -> p (m r n)")

        names = """w_in x_in0 x_in1 con_in s_in ffw_in set_z set_ps set_cp set_ps2 set_d
            a_st a_ag a_ve a_rsd a_xnd a_xnT_ps a_xnTd a_qk_ps a_qkd a_v_ps a_vd a_r2 a_r1 a_rt a_mn a_ex a_ph
            a_qT_ps a_qTd a_kT_ps a_kcd a_qb a_s a_am a_av a_dn a_rc a_yd a_yT_ps a_yTd a_o a_x1
            b_st b_ag b_ve b_rsd b_xnd b_qT_ps b_qcd b_in b_cT_ps b_cTd b_bi b_kb b_cb b_s b_mx b_mh b_ml b_mT_ps
            b_mTd b_sh b_e b_eT_ps b_eTd b_av b_rc b_yd b_x2
            c_st c_ag c_ve c_rsd c_xf c_cp c_st2 c_ag2 c_ve2 c_rsd2 c_xfT_ps c_xfTd c_lg_ps c_ch c_lg c_ex c_seld
            c_ps c_posd c_hitd c_atd c_read c_idxd c_sc0 c_sc1
            t_ch t_done t_spare t_padded
            s_up s_si s_hd s_dn s_ac
            f_in0 f_in1 f_in2 f_in3 f_in4 f_xT_ps f_xTd f_up f_si f_hd f_hT_ps f_hTd f_dn f_yd f_tick f_out0 f_out1 f_out2 f_out3 f_out4
            y_ld0 y_ld1 y_ld2 y_ld3 y_ad y_sum y_st""".split()
        S = {n: stack.enter_context(nc.semaphore(n)) for n in names}
        c_sc = [S["c_sc0"], S["c_sc1"]]
        f_in = [S[f"f_in{u}"] for u in range(UNROLL)]
        f_out = [S[f"f_out{u}"] for u in range(UNROLL)]
        y_ld = [S[f"y_ld{u}"] for u in range(Y_RING)]
        block = stack.enter_context(nc.Block())

        tok = x.rearrange("(t s) k d -> (s k) t d", s=2)
        tok_out = out.rearrange("(t s) k d -> (s k) t d", s=2)
        ctx_v = ctx.rearrange("b k d -> k b d")
        ctx_p = ctx.rearrange("(t s) k d -> (s k) t d", s=2)
        mixed_v = mixed.rearrange("(o t p) d -> o p t d", o=TOP, p=P)

        def group(i):
            return bass.ds(i * GT, GT)

        def steps(eng, step):
            first, last = BEHIND + 2, GROUPS - 2
            for s in range(-1, first):
                step(s, s % 2)
            with eng.Fori(first, last, 2) as s:
                step(s, 0)
                step(s + 1, 1)
            for s in range(last, GROUPS + BEHIND):
                step(s, s % 2)

        def slot_of(g, k):
            return (g, k) if 0 <= k < GS else (g - 1, k + GS) if k < 0 else (g + 1, k - GS)

        def shared_slots(eng, up, down):
            up(0, 0)
            up(1, 1)
            down(0, 0)
            with eng.Fori(2, GROUPS - 1, 2) as i:
                up(i, 0)
                down(i - 1, 1)
                up(i + 1, 1)
                down(i, 0)
            down(GROUPS - 1, 1)

        def routed_slots(eng, slot):
            for u in range(UNROLL):
                slot(0, u)
            with eng.Fori(1, TURNS) as t:
                for u in range(UNROLL):
                    slot(t, u)
            slot(TURNS, 0)

        def is_tile(t):
            return not isinstance(t, int) or t < TURNS

        def is_first(t, u):
            return isinstance(t, int) and t == 0 and u == 0

        def before_tile(t, u):
            return (t, u - 1) if u else (t - 1, UNROLL - 1)

        @block.sync
        def _(sp):
            sp.dma_start(con[:, :], consts).then_inc(S["con_in"], 16)
            for n, w in enumerate((wq, wk, wv, wo)):
                sp.dma_start(a_xn[:, n, :], w).then_inc(S["w_in"], 16)
            sp.dma_start(X[:, 0:GT, :], tok[:, 0:GT, :]).then_inc(S["x_in0"], 16)
            sp.dma_start(b_xn[0:E, 0, :], gate_w).then_inc(S["w_in"], 16)
            sp.dma_start(lnp[:, 0:1], ln_scale.rearrange("(d a) -> d a", a=1)).then_inc(S["w_in"], 16)
            sp.dma_start(lnp[:, 1:2], ln_bias.rearrange("(d a) -> d a", a=1)).then_inc(S["w_in"], 16)
            sp.dma_start(qk[0:2 * R, 0:R * T], ind_in).then_inc(S["w_in"], 16)
            sp.dma_start(X[:, GT:TILES, :], tok[:, GT:TILES, :]).then_inc(S["x_in1"], 16)

            def load_ctx(j):
                sp.dma_start(ctxP[:, :, :], ctx_p[:, group(j), :]).then_inc(S["b_in"], 16)
                for half in range(2):
                    sp.dma_start(ctxD[half * T:(half + 1) * T, :, :],
                                 ctx_v[:, bass.ds(j * GS, GS), :]).then_inc(S["b_in"], 16)
                sp.dma_start(maskB[:, :], mask[bass.ds(j * GS, GS), :].rearrange("b k -> (b k)")
                             .rearrange("(o n) -> o n", o=1).to_broadcast([P, GN])).then_inc(S["b_in"], 16)

            load_ctx(0)
            for n, w in enumerate((swg, swu)):
                sp.dma_start(shared_up_w[:, n, :], w).then_inc(S["s_in"], 16)
            sp.dma_start(shared_down_w[:, :, :], swd.rearrange("(c i) d -> i c d", c=CH)).then_inc(S["s_in"], 16)
            sp.wait_ge(S["set_z"], 1)
            sp.wait_ge(S["set_d"], 1)
            sp.dma_start(routed[E * REGION:E * REGION + SPARE * P, :].rearrange("(n p) f -> p n f", p=P),
                         pad[:, :].rearrange("p (o f) -> p o f", o=1).to_broadcast([P, SPARE, ROW]))\
                .then_inc(S["t_spare"], 16)
            with sp.Fori(1, GROUPS) as j:
                sp.wait_ge(S["con_in"], 16)
                sp.wait_ge(S["b_cT_ps"], j)
                sp.wait_ge(S["b_cb"], 4 * j)
                sp.wait_ge(S["b_bi"], j)
                sp.wait_ge(S["b_cTd"], j)
                load_ctx(j)

            sp.wait_ge(S["a_s"], GS * GROUPS)
            sp.wait_ge(S["b_s"], GS * GROUPS)
            for n, w in enumerate((wg, wu)):
                sp.dma_start(wup[:, :, n, :], w.rearrange("e d i -> d e i")).then_inc(S["ffw_in"], 16)
            for c in range(CH):
                sp.dma_start(wdn[:, :, c, :],
                             wd[:, c * P:(c + 1) * P, :].rearrange("e i d -> i e d")).then_inc(S["ffw_in"], 16)

            sp.wait_ge(S["t_done"], 1)
            for e in range(E):
                at = sp.value_load(t_pad[0:1, e:e + 1], min_val=e * REGION, max_val=e * REGION + TOKENS)
                sp.dma_start(routed[bass.ds(at, P), :], pad[:, :]).then_inc(S["t_padded"], 16)
            sp.wait_ge(S["t_padded"], 16 * E)
            sp.wait_ge(S["t_spare"], 16)
            for m in range(2):
                sp.wait_ge(c_sc[m], 16 * GT * TOP * (GROUPS // 2))

            def load_tile(t, u):
                at = sp.value_load(t_row[0:1, bass.ds(t * UNROLL + u, 1)], min_val=0,
                                   max_val=E * REGION + (SPARE - 1) * P)
                if since(t, 1):
                    sp.wait_ge(f_out[u], 16 * t)
                sp.dma_start(f_x[:, u, :], routed[bass.ds(at, P), :]).then_inc(f_in[u], 16)

            for u in range(UNROLL):
                load_tile(0, u)
            with sp.Fori(1, TURNS) as t:
                for u in range(UNROLL):
                    load_tile(t, u)

            for u in range(UNROLL):
                sp.wait_ge(f_out[u], 16 * TURNS)

            def load_mixed(i, u):
                sp.dma_start(y_in[:, u * GN:(u + 1) * GN].rearrange("p (t d) -> p t d", t=GT),
                             mixed_v[0][:, group(i), :]).then_inc(y_ld[u], 16)
                sp.dma_start(y_in2[:, u * GN:(u + 1) * GN].rearrange("p (t d) -> p t d", t=GT),
                             mixed_v[1][:, group(i), :]).then_inc(y_ld[u], 16)

            for u in range(Y_RING):
                load_mixed(u, u)
            for i in range(Y_RING, GROUPS):
                sp.wait_ge(S["y_sum"], i - Y_RING + 1)
                load_mixed(i, i % Y_RING)
            sp.wait_ge(S["y_st"], 16 * GROUPS)

        @block.tensor
        def _(pe):
            pe.wait_ge(S["con_in"], 16)
            pe.wait_ge(S["w_in"], 8 * 16)
            for n in range(4):
                pe.transpose(banks[0][:, n * D:(n + 1) * D], a_xn[:, n, :], ident)
            pe.transpose(banks[1][:, 0:E], b_xn[0:E, 0, :], ident[0:E, 0:E]).then_inc(S["set_ps"], 1)
            pe.wait_ge(S["set_z"], SET_ZERO)
            pe.wait_ge(S["set_d"], SET_DVE)
            pe.matmul(banks[1][:, E:2 * E], rot[:, 0:P], gateT[:, :], start=True, stop=True)
            pe.matmul(banks[1][:, 2 * E:3 * E], rot[:, 0:P], rot[:, P:P + E], start=True, stop=True)\
                .then_inc(S["set_ps2"], 1)
            pe.wait_ge(S["set_cp"], 3)

            def a_norm_T(f, d):
                pe.wait_ge(S["a_xnd"], GT * f + GT)
                if on(d):
                    pe.wait_ge(S["c_read"], d + 1)
                elif not isinstance(f, int) or f >= 1:
                    pe.wait_ge(S["a_kcd"], C * f)
                for t in range(GT):
                    ins = pe.transpose(banks[FRONT0][:, t * P:(t + 1) * P], a_xn[:, t, :], ident)
                ins.then_inc(S["a_xnT_ps"], 1)

            def a_project(f, h):
                if on(h):
                    pe.wait_ge(S["b_cTd"], h + 1)
                elif f >= 1:
                    pe.wait_ge(S["a_qTd"], f)
                pe.wait_ge(S["a_xnTd"], f + 1)
                for m, bank in enumerate((FRONT1, FRONT0)):
                    for t in range(2):
                        n = 2 * m + t
                        ins = pe.matmul(banks[bank][:, t * 2 * D:(t + 1) * 2 * D], a_xnT[:, n * P:(n + 1) * P],
                                        wqkvT[:, 0:2 * D], start=True, stop=True)
                    ins.then_inc(S["a_qk_ps"], 1)

            def a_project_v(f):
                pe.wait_ge(S["a_qkd"], 2 * f + 1)
                for b in range(GS):
                    for c in range(C):
                        ins = pe.matmul(banks[FRONT1][c * T:(c + 1) * T, b * T:(b + 1) * T],
                                        a_xnT[:, b * T:(b + 1) * T],
                                        wqkvT[:, 2 * D + c * T:2 * D + (c + 1) * T], start=True, stop=True)
                ins.then_inc(S["a_v_ps"], 1)

            def a_qk_T(f, h, c):
                pe.wait_ge(S["a_ph"], f + 1)
                if on(h):
                    pe.wait_ge(S["a_x1"], h + 1)
                else:
                    pe.wait_ge(S["a_vd"], C * f + C)
                v = phi[:, :].rearrange("p (t a d) -> p t a d", t=GT, a=2)
                for t in range(GT):
                    ins = pe.transpose(banks[FRONT1][:, t * P:(t + 1) * P], v[:, t, 0, :], ident)
                ins.then_inc(S["a_qT_ps"], 1)
                if on(c):
                    pe.wait_ge(S["c_xfTd"], 2 * c + 2)
                elif on(h):
                    pe.wait_ge(S["a_yTd"], h + 1)
                for t in range(GT):
                    ins = pe.transpose(banks[FRONT0][:, t * P:(t + 1) * P], v[:, t, 1, :], ident)
                ins.then_inc(S["a_kT_ps"], 1)

            def a_scores(a, k, par):
                pe.wait_ge(S["a_qb"], GS * a + k + 1)
                if k == 0:
                    pe.wait_ge(S["a_kcd"], C * a + C)
                if not (isinstance(a, int) and a == 0 and k == 0):
                    pe.wait_ge(S["a_am"], GS * a + k)
                pe.matmul(banks[A_S][:, :], Kc[:, par, k, :, :].rearrange("p c n -> p (c n)"),
                          Qblk[:, k % RING, :, :], start=True, stop=True).then_inc(S["a_s"], 1)

            def a_values(a, k, par):
                pe.wait_ge(S["a_am"], GS * a + k + 1)
                if k == GS // 2:
                    pe.wait_ge(S["a_yd"], GT * a + 2)
                elif k == 0:
                    pe.wait_ge(S["a_vd"], C * a + C)
                    if not isinstance(a, int) or a >= 1:
                        pe.wait_ge(S["a_yd"], GT * a)
                t, s = k // 2, k % 2
                for r in range(R):
                    at = t % 2 * H * E9 + r * C * E9
                    ins = pe.matmul(banks[A_O][s * T:(s + 1) * T, at:at + C * E9], Am[:, k % 2, r * T:(r + 1) * T],
                                    Vblk[:, par, k, r, :, :].rearrange("p c e -> p (c e)"), start=True, stop=True)
                ins.then_inc(S["a_av"], 1)

            def a_out_T(h, f, d):
                pe.wait_ge(S["a_yd"], GT * h + GT)
                if on(f):
                    pe.wait_ge(S["a_qkd"], 2 * f + 2)
                elif on(d):
                    pe.wait_ge(S["c_read"], d + 1)
                for t in range(GT):
                    ins = pe.transpose(banks[FRONT0][:, t * P:(t + 1) * P], a_y[:, t, :], ident)
                ins.then_inc(S["a_yT_ps"], 1)

            def a_out(h, f):
                if on(f):
                    pe.wait_ge(S["a_vd"], C * f + C)
                else:
                    pe.wait_ge(S["b_cTd"], h + 1)
                pe.wait_ge(S["a_yTd"], h + 1)
                for t in range(GT):
                    ins = pe.matmul(banks[FRONT1][:, t * D:(t + 1) * D], a_yT[:, t * P:(t + 1) * P], woT[:, :],
                                    start=True, stop=True)
                ins.then_inc(S["a_o"], 1)

            def b_ctx_T(h, a):
                pe.wait_ge(S["b_in"], B_LOADS * 16 * (h + 1))
                if not isinstance(h, int) or h >= 1:
                    pe.wait_ge(S["b_qcd"], C * h)
                else:
                    pe.wait_ge(S["a_qTd"], a + 1)
                for b in range(GS // 2):
                    ins = pe.transpose(banks[FRONT1][:, b * P:(b + 1) * P], ctxP[:, b, :], ident)
                ins.then_inc(S["b_cT_ps"], 1)

            def b_norm_T(h, f):
                pe.wait_ge(S["b_xnd"], GT * h + GT)
                if on(f):
                    pe.wait_ge(S["a_qTd"], f + 1)
                for t in range(GT):
                    ins = pe.transpose(banks[FRONT1][:, t * P:(t + 1) * P], b_xn[:, t, :], ident)
                ins.then_inc(S["b_qT_ps"], 1)

            def b_scores(b, k, par):
                pe.wait_ge(S["b_kb"], GS * b + k + 1)
                if k == 0:
                    pe.wait_ge(S["b_qcd"], C * b + C)
                    pe.wait_ge(S["b_bi"], b + 1)
                if not (isinstance(b, int) and b == 0 and k < 2):
                    pe.wait_ge(S["b_e"], GS * b + k - 1)
                bank = banks[B_S[k % 2]]
                pe.matmul(bank[:, :], Qc[:, par, k, :, :].rearrange("p c n -> p (c n)"), Kblk[:, k % RING, :, :],
                          start=True, stop=False)
                keys = bias_row[0:1, par, k * T:(k + 1) * T].rearrange("p (o n) -> p o n", o=1)\
                    .to_broadcast([1, R, T])
                pe.matmul(bank[:, :], ones_row[0:1, :], keys, start=False, stop=True).then_inc(S["b_s"], 1)

            def b_max_T(b, k):
                pe.wait_ge(S["b_ml"], GS * b + k + 1)
                if not (isinstance(b, int) and b == 0 and k == 0):
                    pe.wait_ge(S["b_eTd"], GS * b + k)
                pe.transpose(banks[B_T][0:2 * R, 0:T].bitcast(BF16), mhl[:, k, :, :].rearrange("p a r -> p (a r)"),
                             identb[:, :]).then_inc(S["b_mT_ps"], 1)

            def b_shift(b, k):
                pe.wait_ge(S["b_mTd"], GS * b + k + 1)
                pe.matmul(banks[B_S[k % 2]][:, :], mT[:, k % 2, :], ind[:, :], start=False, stop=True,
                          skip_group_check=True).then_inc(S["b_sh"], 1)

            def b_probs_T(b, k):
                pe.wait_ge(S["b_e"], GS * b + k + 1)
                for rp in range(R // 2):
                    ins = pe.transpose(banks[B_T][:, rp * P:(rp + 1) * P], Ex[:, k % 2, rp * P:(rp + 1) * P], ident)
                ins.then_inc(S["b_eT_ps"], 1)

            def b_values(b, k, par):
                pe.wait_ge(S["b_eTd"], GS * b + k + 1)
                if k == GS // 2:
                    pe.wait_ge(S["b_x2"], 2 * b + 1)
                elif k == 0:
                    pe.wait_ge(S["b_cb"], 4 * b + 4)
                    if not isinstance(b, int) or b >= 1:
                        pe.wait_ge(S["b_x2"], 2 * b)
                t, s = k // 2, k % 2
                for rp in range(R // 2):
                    for c in range(C):
                        at = t % 2 * H * E9 + (rp * C + c) * 2 * E9
                        ins = pe.matmul(banks[B_O][s * T:(s + 1) * T, at:at + 2 * E9], ExT[:, k % 2, rp, c, :],
                                        Cblk[:, par, k, rp, c, :, :].rearrange("p q e -> p (q e)"),
                                        start=True, stop=True)
                ins.then_inc(S["b_av"], 1)

            def c_norm_T(c, h, d, par):
                pe.wait_ge(S["c_xf"], GT * c + GT)
                if on(h):
                    pe.wait_ge(S["a_yTd"], h + 1)
                elif on(d):
                    pe.wait_ge(S["c_read"], d + 1)
                for t in range(GT):
                    ins = pe.transpose(banks[FRONT0][:, t * P:(t + 1) * P], c_row[:, par, t, 0, 0:D], ident)
                ins.then_inc(S["c_xfT_ps"], 1)

            def c_logits(c, f):
                if on(f):
                    pe.wait_ge(S["a_kcd"], C * f + C)
                pe.wait_ge(S["c_xfTd"], 2 * c + 2)
                for t in range(GT):
                    ins = pe.matmul(banks[FRONT0][:, t * E:(t + 1) * E], c_xfT[:, t * P:(t + 1) * P], gateT[:, :],
                                    start=True, stop=True)
                ins.then_inc(S["c_lg_ps"], 1)

            def c_positions(d):
                pe.wait_ge(S["c_seld"], d + 1)
                bank = banks[FRONT0]
                pe.matmul(bank[:, 0:GT * E], before[:, :], c_sel[:, :, :].rearrange("p t e -> p (t e)"),
                          start=True, stop=False, skip_group_check=True)
                for t in range(GT - 1):
                    later = GT - 1 - t
                    pe.matmul(bank[:, (t + 1) * E:GT * E], ones[:, :],
                              c_sel[:, t:t + 1, :].to_broadcast([P, later, E]), start=False, stop=False,
                              skip_group_check=True)
                for t in range(GT):
                    ins = pe.matmul(bank[:, GT * E:(GT + 1) * E], ones[:, :], c_sel[:, t, :], start=False,
                                    stop=(t == GT - 1), skip_group_check=True)
                ins.then_inc(S["c_ps"], 1)

            def step(s, par):
                f, a, h, b, c, d = s + 1, s, s - 1, s - 2, s - 3, s - BEHIND
                odd = 1 - par
                for k in range(GS):
                    if on(a):
                        a_scores(a, k, par)
                    if on(b):
                        b_scores(b, k, par)
                    g, n = slot_of(b, k - 1)
                    if on(g):
                        b_probs_T(g, n)
                    g, n = slot_of(a, k - 1)
                    if on(g):
                        a_values(g, n, par if k else odd)
                    if on(b):
                        b_max_T(b, k)
                    if k == 0 and on(d):
                        c_positions(d)
                    if k == 0 and on(h):
                        b_ctx_T(h, a)
                    if k == 1 and on(f):
                        a_norm_T(f, d)
                    if k == 2 and on(f):
                        a_project(f, h)
                    if k == 3 and on(f):
                        a_project_v(f)
                    if k == 3 and on(h):
                        a_out_T(h, f, d)
                    if k == 4 and on(h):
                        a_out(h, f)
                    if k == 4 and on(c):
                        c_norm_T(c, h, d, odd)
                    if k == 5 and on(f):
                        a_qk_T(f, h, c)
                    if k == 6 and on(h):
                        b_norm_T(h, f)
                    if k == 6 and on(c):
                        c_logits(c, f)
                    g, n = slot_of(b, k - 1)
                    if on(g):
                        b_values(g, n, par if k else odd)
                    if on(b):
                        b_shift(b, k)

            steps(pe, step)

            pe.wait_ge(S["s_in"], 3 * 16)
            pe.wait_ge(S["c_xfTd"], 2 * GROUPS)
            pe.wait_ge(S["c_read"], GROUPS)

            def shared_up(i):
                for c in range(CH):
                    n = i * CH + c
                    if not (isinstance(i, int) and i == 0):
                        pe.wait_ge(S["s_hd"], n - CH + 1)
                    for m in range(2):
                        ins = pe.matmul(banks[2 * c + m][:, :], shared_up_w[:, m, c * P:(c + 1) * P],
                                        xfT[:, bass.ds(i * GN, GN)], start=True, stop=True)
                    ins.then_inc(S["s_up"], 1)

            def shared_down(i, par):
                pe.wait_ge(S["s_hd"], CH * i + CH)
                if not isinstance(i, int) or i >= 2:
                    pe.wait_ge(S["s_ac"], i - 1)
                for t in range(GT):
                    for c in range(CH):
                        ins = pe.matmul(banks[4 + par][:, t * D:(t + 1) * D], s_h[:, par, c, t * P:(t + 1) * P],
                                        shared_down_w[:, c, :], start=(c == 0), stop=(c == CH - 1))
                ins.then_inc(S["s_dn"], 1)

            shared_slots(pe, lambda i, par: shared_up(i), shared_down)

            pe.wait_ge(S["s_ac"], GROUPS)
            pe.wait_ge(S["ffw_in"], (2 + CH) * 16)
            pe.wait_ge(S["t_done"], 1)

            def tile_T(t, u):
                n = t * UNROLL + u
                pe.wait_ge(f_in[u], 16 * t + 16)
                if not is_first(t, u):
                    pe.wait_ge(S["f_xTd"], n)
                pe.transpose(banks[F_X][:, 0:P], f_x[:, u, 0:D], ident).then_inc(S["f_xT_ps"], 1)

            def tile_up(t, u):
                n = t * UNROLL + u
                e = pe.value_load(t_expert[0:1, bass.ds(n, 1)], min_val=0, max_val=E - 1)
                pe.wait_ge(S["f_xTd"], n + 1)
                pe.matmul(banks[F_UP[THIRD[u]]][:, :], f_xT[:, THIRD[u], :],
                          wup[:, bass.ds(e, 1), :, :].rearrange("p o m i -> p (o m i)"), start=True, stop=True)\
                    .then_inc(S["f_up"], 1)

            def hidden_T(t, u):
                pe.wait_ge(S["f_hd"], t * UNROLL + u + 1)
                for c in range(CH):
                    ins = pe.transpose(banks[F_HT[THIRD[u]]][:, c * P:(c + 1) * P],
                                       f_h[:, THIRD[u], c * P:(c + 1) * P], ident)
                ins.then_inc(S["f_hT_ps"], 1)

            def tile_down(t, u):
                n = t * UNROLL + u
                e = pe.value_load(t_expert[0:1, bass.ds(n, 1)], min_val=0, max_val=E - 1)
                pe.wait_ge(S["f_hTd"], n + 1)
                if not is_first(t, u):
                    pe.wait_ge(S["f_yd"], n)
                for c in range(CH):
                    ins = pe.matmul(banks[F_O][:, 0:D], f_hT[:, THIRD[u], c * P:(c + 1) * P],
                                    wdn[:, bass.ds(e, 1), c, :].rearrange("p o d -> p (o d)"),
                                    start=(c == 0), stop=(c == CH - 1))
                ins.then_inc(S["f_dn"], 1)

            def slot(t, u):
                if is_tile(t):
                    tile_T(t, u)
                if not is_first(t, u):
                    hidden_T(*before_tile(t, u))
                if is_tile(t):
                    tile_up(t, u)
                if not is_first(t, u):
                    tile_down(*before_tile(t, u))

            routed_slots(pe, slot)

        @block.scalar
        def _(act):
            act.wait_ge(S["set_ps"], 1)
            act.copy(wqkvT[:, :], banks[0][:, 0:3 * D]).then_inc(S["set_cp"], 1)
            act.copy(woT[:, :], banks[0][:, 3 * D:4 * D]).then_inc(S["set_cp"], 1)
            act.wait_ge(S["set_ps2"], 1)
            act.copy(gate_sum[:, :, :], banks[1][:, E:3 * E].rearrange("p (n e) -> p n e", e=E)).then_inc(S["set_cp"], 1)
            act.wait_ge(S["set_z"], SET_ZERO)

            def halves_of(bank, c):
                return banks[bank][c * T:(c + 1) * T, :].rearrange("p (b n) -> p b n", n=T)

            def a_norm_evac(f):
                act.wait_ge(S["a_xnT_ps"], f + 1)
                act.copy(a_xnT[:, :], banks[FRONT0][:, :]).then_inc(S["a_xnTd"], 1)

            def a_qk_evac(f):
                if since(f, 1):
                    act.wait_ge(S["a_ph"], f)
                for m, bank in enumerate((FRONT1, FRONT0)):
                    act.wait_ge(S["a_qk_ps"], 2 * f + m + 1)
                    act.copy(qk[:, m * GN:(m + 1) * GN], banks[bank][:, :]).then_inc(S["a_qkd"], 1)

            def a_v_evac(f, par):
                if since(f, 2):
                    act.wait_ge(S["a_av"], GS * (f - 1))
                act.wait_ge(S["a_v_ps"], f + 1)
                for c in range(C):
                    rows = slice(c * T, (c + 1) * T)
                    act.copy(Vblk[rows, par, :, :, c, 0:DH],
                             banks[FRONT1][rows, :].rearrange("p (b r e) -> p b r e", r=R, e=DH))\
                        .then_inc(S["a_vd"], 1)

            def a_exp(f):
                act.wait_ge(S["a_mn"], f + 1)
                act.activation(qk[:, :], qk[:, :], ACT.Exp).then_inc(S["a_ex"], 1)

            def a_qk_T_evac(f, par):
                act.wait_ge(S["a_qT_ps"], f + 1)
                if since(f, 2):
                    act.wait_ge(S["a_qb"], GS * (f - 1))
                    act.wait_ge(S["a_s"], GS * (f - 1))
                act.copy(qT[:, par, :], banks[FRONT1][:, :]).then_inc(S["a_qTd"], 1)
                act.wait_ge(S["a_kT_ps"], f + 1)
                for c in range(C):
                    act.copy(Kc[c * T:(c + 1) * T, par, :, c, :], halves_of(FRONT0, c)).then_inc(S["a_kcd"], 1)

            def a_out_evac(h):
                act.wait_ge(S["a_yT_ps"], h + 1)
                act.copy(a_yT[:, :], banks[FRONT0][:, :]).then_inc(S["a_yTd"], 1)

            def b_norm_evac(h, par):
                act.wait_ge(S["b_qT_ps"], h + 1)
                if since(h, 2):
                    act.wait_ge(S["b_s"], GS * (h - 1))
                for c in range(C):
                    act.copy(Qc[c * T:(c + 1) * T, par, :, c, :], halves_of(FRONT1, c)).then_inc(S["b_qcd"], 1)

            def b_exp(b, k):
                act.wait_ge(S["b_sh"], GS * b + k + 1)
                act.activation(Ex[:, k % 2, :], banks[B_S[k % 2]][:, :], ACT.Exp, scale=SCALE).then_inc(S["b_e"], 1)

            def b_probs_evac(b, k):
                act.wait_ge(S["b_eT_ps"], GS * b + k + 1)
                act.copy(ExT[:, k % 2].rearrange("p r c q -> p (r c q)"), banks[B_T][:, :]).then_inc(S["b_eTd"], 1)

            def b_max_evac(b, k):
                act.wait_ge(S["b_mT_ps"], GS * b + k + 1)
                act.copy(mT[:, k % 2, :], banks[B_T][0:2 * R, 0:T].bitcast(BF16)).then_inc(S["b_mTd"], 1)

            def c_norm_evac(c, par):
                act.wait_ge(S["c_xfT_ps"], c + 1)
                if since(c, 1):
                    act.wait_ge(S["c_lg_ps"], c)
                act.copy(c_xfT[:, :], banks[FRONT0][:, :]).then_inc(S["c_xfTd"], 1)
                act.copy(xfT[:, bass.ds(c * GN, GN)], banks[FRONT0][:, :]).then_inc(S["c_xfTd"], 1)
                act.copy(c_row[:, par, :, 1, 0:D], c_row[:, par, :, 0, 0:D]).then_inc(S["c_cp"], 1)

            def c_exp(c):
                act.wait_ge(S["c_lg"], c + 1)
                act.activation(c_p[:, :, :], c_p[:, :, :], ACT.Exp).then_inc(S["c_ex"], 1)

            def step(s, par):
                f, a, h, b, c, d = s + 1, s, s - 1, s - 2, s - 3, s - BEHIND
                odd = 1 - par
                for k in range(GS):
                    g, n = slot_of(b, k - 1)
                    if on(g):
                        b_exp(g, n)
                        b_probs_evac(g, n)
                    if on(b):
                        b_max_evac(b, k)
                    if k == 1 and on(f):
                        a_norm_evac(f)
                    if k == 2 and on(f):
                        a_qk_evac(f)
                    if k == 3 and on(f):
                        a_v_evac(f, odd)
                    if k == 3 and on(h):
                        a_out_evac(h)
                    if k == 4 and on(f):
                        a_exp(f)
                    if k == 4 and on(c):
                        c_norm_evac(c, odd)
                    if k == 5 and on(f):
                        a_qk_T_evac(f, odd)
                    if k == 6 and on(h):
                        b_norm_evac(h, odd)
                    if k == 7 and on(c):
                        c_exp(c)

            steps(act, step)

            def shared(i):
                for c in range(CH):
                    act.wait_ge(S["s_up"], i * CH + c + 1)
                    if since(i, 1):
                        act.wait_ge(S["s_hd"], (i - 1) * CH + c + 1)
                    act.activation(s_sg[:, c, :], banks[2 * c][:, :], ACT.Silu).then_inc(S["s_si"], 1)

            shared(0)
            with act.Fori(1, GROUPS) as i:
                shared(i)

            act.wait_ge(S["s_ac"], GROUPS)

            def tile_start(t, u):
                n = t * UNROLL + u
                act.wait_ge(S["f_xT_ps"], n + 1)
                act.copy(f_xT[:, THIRD[u], :], banks[F_X][:, 0:P]).then_inc(S["f_xTd"], 1)
                act.wait_ge(S["f_up"], n + 1)
                act.activation(f_sg[:, THIRD[u], :], banks[F_UP[THIRD[u]]][:, 0:INTER], ACT.Silu).then_inc(S["f_si"], 1)

            def tile_end(t, u):
                act.wait_ge(S["f_dn"], t * UNROLL + u + 1)
                act.activation(f_y[:, u, :], banks[F_O][:, 0:D], ACT.Copy, scale=f_x[:, u, D:D + 1]).then_inc(S["f_yd"], 1)

            def slot(t, u):
                if is_tile(t):
                    tile_start(t, u)
                if not is_first(t, u):
                    tile_end(*before_tile(t, u))

            routed_slots(act, slot)

            for i in range(GROUPS):
                act.wait_ge(S["y_sum"], i + 1)
                act.dma_start(tok_out[:, group(i), :], X[:, group(i), :]).then_inc(S["y_st"], 16)

        @block.gpsimd
        def _(pool):
            pool.memset(pad[:, :], 0.0).then_inc(S["set_z"], 1)
            pool.memset(rot[:, 0:P], 1.0).then_inc(S["set_z"], 1)
            pool.memset(Kc[:, :, :, :, :], 0.0).then_inc(S["set_z"], 1)
            pool.memset(Qc[:, :, :, :, :], 0.0).then_inc(S["set_z"], 1)
            pool.memset(ones_row[:, :], 1.0).then_inc(S["set_z"], 1)
            pool.memset(ones[:, :], 1.0).then_inc(S["set_z"], 1)
            pool.memset(minus_half[:, :], -0.5).then_inc(S["set_z"], 1)
            pool.memset(Vblk[:, :, :, :, :, :], 0.0).then_inc(S["set_z"], 1)
            pool.memset(Cblk[:, :, :, :, :, :, :], 0.0).then_inc(S["set_z"], 1)
            pool.wait_ge(S["set_z"], SET_ZERO - 1)
            pool.wait_ge(S["con_in"], 16)
            for m in range(2):
                for c in range(C):
                    mark = halves[:, c:c + 1].rearrange("p (a o) -> p a o", o=1)
                    pool.tensor_copy(Vblk[:, m, :, :, c, DH], mark.to_broadcast([P, GS, R]))
                    for q in range(2):
                        mark = halves[:, q:q + 1].rearrange("p (a o) -> p a o", o=1)
                        ins = pool.tensor_copy(Cblk[:, m, :, :, c, q, DH], mark.to_broadcast([P, GS, R // 2]))
            ins.then_inc(S["set_z"], 1)

            def carry_wait(u):
                return pool.tensor_tensor(tick[:, u:u + 1], minus_half[:, 0:1], minus_half[:, 0:1], ALU.add)

            rows = row.rearrange("p (r o) -> p r o", o=1).to_broadcast([P, R, T])

            def rsqrt(i, rs, s_ve, s_rs):
                pool.wait_ge(s_ve, i + 1)
                pool.tensor_tensor(rs[:, :], rs[:, :], minus_half[:, :], ALU.pow).then_inc(s_rs, 1)

            def build(dst, src, k):
                return pool.tensor_tensor(dst[:, k % RING, :, :], src[:, k * T:(k + 1) * T].rearrange("p (o n) -> p o n", o=1)
                                          .to_broadcast([P, R, T]), rows, ALU.mult)

            def a_block(g, k, par):
                if k == 0:
                    pool.wait_ge(S["a_qTd"], g + 1)
                if since(g, 1) or k >= RING:
                    pool.wait_ge(S["a_s"], GS * g + k - RING + 1)
                build(Qblk, qT[:, par, :], k).then_inc(S["a_qb"], 1)

            def b_block(g, k, par):
                if k == 0:
                    pool.wait_ge(S["b_cTd"], g + 1)
                if since(g, 1) or k >= RING:
                    pool.wait_ge(S["b_s"], GS * g + k - RING + 1)
                build(Kblk, ctxT[:, par, :], k).then_inc(S["b_kb"], 1)

            def a_rope(f):
                pool.wait_ge(S["a_qkd"], 2 * f + 2)
                if since(f, 1):
                    pool.wait_ge(S["a_kT_ps"], f)
                src = qk[:, :].rearrange("p (n s f) -> p n s f", s=2, f=HALF)
                dst = phi[:, :].rearrange("p (n s f) -> p n s f", s=2, f=HALF)
                for half in range(2):
                    pool.tensor_tensor(dst[:, :, half, :], src[:, :, 1 - half, :],
                                       sin.rearrange("p (o f) -> p o f", o=1).to_broadcast([P, GT * 2 * H, HALF]),
                                       ALU.mult).then_inc(S["a_r2"], 1)

            def b_context(h, par):
                pool.wait_ge(S["b_in"], B_LOADS * 16 * (h + 1))
                if since(h, 2):
                    pool.wait_ge(S["b_av"], GS * (h - 1))
                src = ctxD[:, :, :].rearrange("p b (c r q e) -> p c q b r e", c=C, q=2, e=DH)
                for c in range(C):
                    for q in range(2):
                        mark = halves[:, q:q + 1].rearrange("p (a b o) -> p a b o", a=1, o=1)
                        pool.tensor_tensor(Cblk[:, par, :, :, c, q, 0:DH], src[:, c, q],
                                           mark.to_broadcast([P, GS, R // 2, DH]), ALU.mult).then_inc(S["b_cb"], 1)

            def c_scatter(d, par, t):
                if t == 0:
                    pool.wait_ge(S["c_idxd"], d + 1)
                    pool.wait_ge(S["c_cp"], d + 1)
                    carry_wait(UNROLL)
                for n in range(TOP):
                    pool.indirect_dma_start(routed[:, :], bass.IndirectOffsetOnAxis(ap=c_idx[:, par, t, n:n + 1], axis=0),
                                            c_row[:, par, t, n, :], None, bounds_check=E * REGION - 1, oob_is_err=False)\
                        .then_inc(c_sc[par], 16)

            def step(s, par):
                f, a, h, b, c, d = s + 1, s, s - 1, s - 2, s - 3, s - BEHIND
                odd = 1 - par
                for k in range(GS):
                    g, n = slot_of(a, k + 2)
                    if on(g):
                        a_block(g, n, odd if n < 2 else par)
                    g, n = slot_of(b, k + 2)
                    if on(g):
                        b_block(g, n, odd if n < 2 else par)
                    if k == 0 and on(f):
                        rsqrt(f, a_rs, S["a_ve"], S["a_rsd"])
                    if k == 1 and on(h):
                        b_context(h, odd)
                    if k == 2 and on(c):
                        rsqrt(c, c_rs, S["c_ve"], S["c_rsd"])
                    if k == 3 and on(f):
                        a_rope(f)
                    if k == 3 and on(c):
                        rsqrt(c, c_rs2, S["c_ve2"], S["c_rsd2"])
                    if k == 5 and on(h):
                        rsqrt(h, b_rs, S["b_ve"], S["b_rsd"])
                    if k in SCATTER_SLOTS and on(d):
                        c_scatter(d, par, SCATTER_SLOTS.index(k))

            steps(pool, step)



            def slot(t, u):
                if is_first(t, u):
                    return
                t, u = before_tile(t, u)
                pool.wait_ge(S["f_yd"], t * UNROLL + u + 1)
                if since(t, 1):
                    pool.wait_ge(S["f_tick"], t * UNROLL + u + 1 - UNROLL)
                carry_wait(u).then_inc(S["f_tick"], 1)
                pool.indirect_dma_start(mixed[:, :],
                                        bass.IndirectOffsetOnAxis(ap=f_x[:, u, D + 1:D + 2].bitcast(I32), axis=0),
                                        f_y[:, u, :], None, bounds_check=TOP * TOKENS - 1, oob_is_err=False)\
                    .then_inc(f_out[u], 16)

            routed_slots(pool, slot)

        @block.vector
        def _(dve):
            dve.wait_ge(S["set_z"], 1)
            dve.memset(pad[:, D + 1:D + 2].bitcast(I32), NOWHERE).then_inc(S["set_d"], 1)
            dve.wait_ge(S["con_in"], 16)
            dve.tensor_copy(identb[:, :], ident).then_inc(S["set_d"], 1)
            dve.tensor_copy(before[:, :], const("before")).then_inc(S["set_d"], 1)
            dve.tensor_copy(c_base[:, :], const("region")).then_inc(S["set_d"], 1)
            dve.tensor_copy(c_place[:, :, :].rearrange("p t n -> p (t n)"), const("place")).then_inc(S["set_d"], 1)
            dve.wait_ge(S["w_in"], 8 * 16)
            dve.tensor_copy(ind[:, :], qk[0:2 * R, 0:R * T]).then_inc(S["set_d"], 1)
            dve.wait_ge(S["set_ps"], 1)
            dve.tensor_scalar(gateT[:, :], banks[1][:, 0:E], lnp[:, 0:1], None, ALU.mult).then_inc(S["set_d"], 1)
            dve.tensor_scalar(rot[:, P:P + E], banks[1][:, 0:E], lnp[:, 1:2], None, ALU.mult).then_inc(S["set_d"], 1)
            dve.wait_ge(S["set_cp"], 3)

            def statistics(i, src, stat, mv, rs, s_st, s_ag, s_ve):
                for t in range(GT):
                    dve.bn_stats(stat[:, t, :], src(t)).then_inc(s_st, 1)
                dve.wait_ge(s_st, GT * i + GT)
                dve.memset(rs[:, :], LN_EPS)
                for t in range(GT):
                    dve.bn_aggr(mv[:, t, :], stat[:, t, :]).then_inc(s_ag, 1)
                dve.wait_ge(s_ag, GT * i + GT)
                dve.tensor_tensor(rs[:, :], rs[:, :], mv[:, :, 1], ALU.add).then_inc(s_ve, 1)

            def normalise(i, src, mv, rs, dst, s_rs, s_xn):
                dve.wait_ge(s_rs, i + 1)
                for t in range(GT):
                    dve.tensor_scalar(dst(t), src(t), mv[:, t, 0:1], rs[:, t:t + 1], ALU.subtract, ALU.mult)\
                        .then_inc(s_xn, 1)

            def x_tile(i):
                return lambda t: X[:, bass.ds(i * GT + t, 1), :].rearrange("p o d -> p (o d)")

            def a_norm(f):
                dve.wait_ge(S["x_in0" if isinstance(f, int) and f == 0 else "x_in1"], 16)
                statistics(f, x_tile(f), a_stat, a_mv, a_rs, S["a_st"], S["a_ag"], S["a_ve"])
                if since(f, 1):
                    dve.wait_ge(S["a_xnT_ps"], f)
                normalise(f, x_tile(f), a_mv, a_rs, lambda t: a_xn[:, t, :], S["a_rsd"], S["a_xnd"])

            def a_feature(f):
                dve.wait_ge(S["a_qkd"], 2 * f + 2)
                n = GT * 2 * H * 2
                dve.tensor_tensor(rot[:, :].rearrange("p (n f) -> p n f", f=HALF),
                                  qk[:, :].rearrange("p (n f) -> p n f", f=HALF),
                                  cos.rearrange("p (o f) -> p o f", o=1).to_broadcast([P, n, HALF]), ALU.mult)\
                    .then_inc(S["a_r1"], 1)
                dve.wait_ge(S["a_r1"], f + 1)
                dve.wait_ge(S["a_r2"], 2 * f + 2)
                for half, op in ((0, ALU.subtract), (1, ALU.add)):
                    v = rot[:, :].rearrange("p (n s f) -> p n s f", s=2, f=HALF)[:, :, half, :]
                    w = phi[:, :].rearrange("p (n s f) -> p n s f", s=2, f=HALF)[:, :, half, :]
                    dve.tensor_tensor(v, v, w, op).then_inc(S["a_rt"], 1)
                dve.wait_ge(S["a_rt"], 2 * f + 2)
                dve.tensor_scalar(qk[:, :], rot[:, :], 0.0, None, ALU.min).then_inc(S["a_mn"], 1)

            def a_feature2(f):
                dve.wait_ge(S["a_ex"], f + 1)
                dve.scalar_tensor_tensor(phi[:, :], rot[:, :], 0.0, qk[:, :], ALU.max, ALU.add).then_inc(S["a_ph"], 1)

            def a_mask(a, k):
                dve.wait_ge(S["a_s"], GS * a + k + 1)
                dve.tensor_tensor(Am[:, k % 2, :].rearrange("p (r n) -> p r n", n=T),
                                  banks[A_S][:, :].rearrange("p (r n) -> p r n", n=T),
                                  causal.rearrange("p (o n) -> p o n", o=1).to_broadcast([P, R, T]), ALU.mult)\
                    .then_inc(S["a_am"], 1)

            def a_divide(g, m):
                dve.wait_ge(S["a_av"], GS * g + (m + 1) * (GS // 2))
                num = banks[A_O][:, 0:2 * H * E9].rearrange("p (t n e) -> p t n e", t=2, e=E9)
                dve.tensor_scalar(a_den[:, :, :], num[:, :, :, DH], DEN_EPS, None, ALU.max).then_inc(S["a_dn"], 1)
                dve.wait_ge(S["a_dn"], 2 * g + m + 1)
                dve.reciprocal(a_rec[:, :, :], a_den[:, :, :]).then_inc(S["a_rc"], 1)
                dve.wait_ge(S["a_rc"], 2 * g + m + 1)
                if m == 0 and since(g, 1):
                    dve.wait_ge(S["a_yT_ps"], g)
                for t in range(2):
                    dst = a_y[:, 2 * m + t, :].rearrange("p (c r e) -> p r c e", c=C, e=DH)
                    src = num[:, t, :, 0:DH].rearrange("p (r c) e -> p r c e", c=C)
                    rec = a_rec[:, t, :].rearrange("p (r c o) -> p r c o", c=C, o=1).to_broadcast([P, R, C, DH])
                    dve.tensor_tensor(dst, src, rec, ALU.mult).then_inc(S["a_yd"], 1)

            def a_residual(h):
                dve.wait_ge(S["a_o"], h + 1)
                xs = X[:, group(h), :]
                dve.tensor_tensor(xs, xs, banks[FRONT1][:, :].rearrange("p (t d) -> p t d", t=GT), ALU.add)\
                    .then_inc(S["a_x1"], 1)
                dve.wait_ge(S["a_x1"], h + 1)

            def b_norm(h):
                statistics(h, x_tile(h), b_stat, b_mv, b_rs, S["b_st"], S["b_ag"], S["b_ve"])
                if since(h, 1):
                    dve.wait_ge(S["b_qT_ps"], h)
                normalise(h, x_tile(h), b_mv, b_rs, lambda t: b_xn[:, t, :], S["b_rsd"], S["b_xnd"])

            def b_context(h, par):
                dve.wait_ge(S["b_cT_ps"], h + 1)
                if since(h, 2):
                    dve.wait_ge(S["b_s"], GS * (h - 1))
                dve.scalar_tensor_tensor(ctxT[:, par, :], maskB[:, :], 0.0, banks[FRONT1][:, :], ALU.not_equal, ALU.mult)\
                    .then_inc(S["b_cTd"], 1)
                dve.tensor_scalar(bias_row[:, par, :], maskB[0:1, :], 0.0, MASKED, ALU.is_equal, ALU.mult)\
                    .then_inc(S["b_bi"], 1)

            def b_max(b, k):
                dve.wait_ge(S["b_s"], GS * b + k + 1)
                dve.tensor_reduce(mx[:, k, :], banks[B_S[k % 2]][:, :].rearrange("p (r n) -> p r n", n=T), AX, ALU.max)\
                    .then_inc(S["b_mx"], 1)
                dve.wait_ge(S["b_mx"], GS * b + k + 1)
                dve.tensor_scalar(mhl[:, k, 0, :], mx[:, k, :], -1.0, None, ALU.mult).then_inc(S["b_mh"], 1)
                dve.wait_ge(S["b_mh"], GS * b + k + 1)
                dve.scalar_tensor_tensor(mhl[:, k, 1, :], mx[:, k, :], -1.0, mhl[:, k, 0, :], ALU.mult, ALU.subtract)\
                    .then_inc(S["b_ml"], 1)

            def b_divide(g, m):
                dve.wait_ge(S["b_av"], GS * g + (m + 1) * (GS // 2))
                num = banks[B_O][:, 0:2 * H * E9].rearrange("p (t n e) -> p t n e", t=2, e=E9)
                dve.reciprocal(b_rec[:, :, :], num[:, :, :, DH]).then_inc(S["b_rc"], 1)
                dve.wait_ge(S["b_rc"], 2 * g + m + 1)
                for t in range(2):
                    for c in range(C):
                        dst = b_y[:, t, :].rearrange("p (c r q e) -> p c r q e", c=C, q=2, e=DH)[:, c]
                        src = num[:, t, :, 0:DH].rearrange("p (r c q) e -> p c r q e", c=C, q=2)[:, c]
                        rec = b_rec[:, t, :].rearrange("p (r c q o) -> p c r q o", c=C, q=2, o=1)[:, c]\
                            .to_broadcast([P, R // 2, 2, DH])
                        ins = dve.tensor_tensor(dst, src, rec, ALU.mult)
                        ins.then_inc(S["b_yd"], 1)
                dve.wait_ge(S["b_yd"], 8 * g + 4 * m + 4)
                xs = X[:, bass.ds(g * GT + 2 * m, 2), :]
                dve.tensor_tensor(xs, xs, b_y[:, :, :], ALU.add).then_inc(S["b_x2"], 1)
                if m == 1:
                    dve.wait_ge(S["b_x2"], 2 * g + 2)

            def c_norm(c, par):
                statistics(c, x_tile(c), c_stat, c_mv, c_rs, S["c_st"], S["c_ag"], S["c_ve"])
                if since(c, 2):
                    dve.wait_ge(c_sc[par], 16 * TOP * GT // 2 * (c - par))

                def xf(t):
                    return c_row[:, par, t, 0, 0:D]

                normalise(c, x_tile(c), c_mv, c_rs, xf, S["c_rsd"], S["c_xf"])
                dve.wait_ge(S["c_xf"], GT * c + GT)
                statistics(c, xf, c_stat2, c_mv2, c_rs2, S["c_st2"], S["c_ag2"], S["c_ve2"])

            def per_token(v):
                return v.rearrange("p (t o) -> p t o", o=1).to_broadcast([P, GT, E])

            def per_expert(v):
                return v.rearrange("p (o e) -> p o e", o=1).to_broadcast([P, GT, E])

            def c_route(c, par):
                done = [0]

                def chain(ins):
                    done[0] += 1
                    ins.then_inc(S["c_ch"], 1)
                    dve.wait_ge(S["c_ch"], C_STEPS * c + done[0])

                dve.wait_ge(S["c_rsd2"], c + 1)
                chain(dve.scalar_tensor_tensor(c_m[:, :], c_mv2[:, :, 0], -1.0, c_rs2[:, :], ALU.mult, ALU.mult))
                chain(dve.tensor_tensor(c_t[:, :, :], per_expert(gate_sum[:, 0, :]), per_token(c_m[:, :]), ALU.mult))
                chain(dve.tensor_tensor(c_t[:, :, :], c_t[:, :, :], per_expert(gate_sum[:, 1, :]), ALU.add))
                dve.wait_ge(S["c_lg_ps"], c + 1)
                logits = banks[FRONT0][:, 0:GT * E].rearrange("p (t e) -> p t e", e=E)
                chain(dve.tensor_tensor(c_p[:, :, :], logits, per_token(c_rs2[:, :]), ALU.mult))
                chain(dve.tensor_tensor(c_p[:, :, :], c_p[:, :, :], c_t[:, :, :], ALU.add))
                chain(dve.tensor_reduce(c_m[:, :], c_p[:, :, :], AX, ALU.max))
                dve.tensor_tensor(c_p[:, :, :], c_p[:, :, :], per_token(c_m[:, :]), ALU.subtract).then_inc(S["c_lg"], 1)
                dve.wait_ge(S["c_ex"], c + 1)
                chain(dve.tensor_reduce(c_m[:, :], c_p[:, :, :], AX, ALU.add))
                chain(dve.reciprocal(c_m[:, :], c_m[:, :]))
                chain(dve.tensor_tensor(c_t[:, :, :], c_p[:, :, :], per_token(c_m[:, :]), ALU.mult))
                hit = c_hit[:, 0, :, :]
                for n in range(TOP):
                    chain(dve.tensor_reduce(c_best[:, n, :], c_t[:, :, :], AX, ALU.max))
                    chain(dve.tensor_tensor(hit, c_t[:, :, :], per_token(c_best[:, n, :]), ALU.is_equal))
                    chain(dve.tensor_tensor(hit, hit, per_expert(order), ALU.mult))
                    chain(dve.tensor_reduce(c_m[:, :], hit, AX, ALU.max))
                    chain(dve.tensor_tensor(c_pick[:, n, :, :], per_expert(order), per_token(c_m[:, :]), ALU.is_equal))
                    if n == 0:
                        chain(dve.scalar_tensor_tensor(c_t[:, :, :], c_pick[:, 0, :, :], -2.0, c_t[:, :, :],
                                                       ALU.mult, ALU.add))
                dve.tensor_tensor(c_sel[:, :, :], c_pick[:, 0, :, :], c_pick[:, 1, :, :], ALU.add).then_inc(S["c_seld"], 1)
                chain(dve.scalar_tensor_tensor(c_m[:, :], c_best[:, 0, :], TOP_EPS, c_best[:, 1, :], ALU.add, ALU.add))
                chain(dve.reciprocal(c_m[:, :], c_m[:, :]))
                dve.tensor_tensor(c_row[:, par, :, :, D].rearrange("p t n -> p n t"), c_best[:, :, :],
                                  c_m[:, :].rearrange("p (o t) -> p o t", o=1).to_broadcast([P, TOP, GT]), ALU.mult)
                chain(dve.tensor_copy(c_row[:, par, :, :, D + 1:ROW].bitcast(I32).rearrange("p t n o -> p t (n o)"),
                                      c_place[:, :, :]))
                chain(dve.tensor_scalar(c_place[:, :, :], c_place[:, :, :], float(GN), None, ALU.add))
                assert done[0] == C_STEPS

            def c_index(d, par):
                dve.wait_ge(S["c_ps"], d + 1)
                bank = banks[FRONT0]
                dve.tensor_tensor(c_pos[:, :, :], bank[:, 0:GT * E].rearrange("p (t e) -> p t e", e=E),
                                  per_expert(c_base[:, :]), ALU.add).then_inc(S["c_posd"], 1)
                dve.wait_ge(S["c_posd"], d + 1)
                dve.tensor_tensor(c_base[:, :], c_base[:, :], bank[:, GT * E:(GT + 1) * E], ALU.add).then_inc(S["c_read"], 1)
                dve.tensor_tensor(c_hit[:, :, :, :], c_pick[:, :, :, :],
                                  c_pos[:, :, :].rearrange("p (o t) e -> p o t e", o=1).to_broadcast([P, TOP, GT, E]),
                                  ALU.mult).then_inc(S["c_hitd"], 1)
                dve.wait_ge(S["c_hitd"], d + 1)
                dve.tensor_reduce(c_at[:, :, :].rearrange("p t n -> p n t"), c_hit[:, :, :, :], AX, ALU.add)\
                    .then_inc(S["c_atd"], 1)
                dve.wait_ge(S["c_atd"], d + 1)
                dve.tensor_copy(c_idx[:, par, :, :], c_at[:, :, :]).then_inc(S["c_idxd"], 1)

            def step(s, par):
                f, a, h, b, c, d = s + 1, s, s - 1, s - 2, s - 3, s - BEHIND
                odd = 1 - par
                for k in range(GS):
                    if k % 4 == 1:
                        g, m = (a, 0) if k == 5 else (a - 1, 1)
                        if on(g):
                            a_divide(g, m)
                    if on(a):
                        a_mask(a, k)
                    if on(b):
                        b_max(b, k)
                    if k % 4 == 1:
                        g, m = (b, 0) if k == 5 else (b - 1, 1)
                        if on(g):
                            b_divide(g, m)
                    if k == 0 and on(h):
                        b_context(h, odd)
                    if k == 0 and on(f):
                        a_norm(f)
                    if k == 1 and on(d):
                        c_index(d, par)
                    if k == 2 and on(c):
                        c_norm(c, odd)
                    if k == 3 and on(f):
                        a_feature(f)
                    if k == 4 and on(f):
                        a_feature2(f)
                    if k == 4 and on(h):
                        a_residual(h)
                    if k == 5 and on(h):
                        b_norm(h)
                    if k == 7 and on(c):
                        c_route(c, odd)

            steps(dve, step)

            links = [0]

            def link(ins):
                links[0] += 1
                ins.then_inc(S["t_ch"], 1)
                dve.wait_ge(S["t_ch"], links[0])

            dve.wait_ge(S["c_read"], GROUPS)
            tile_n = const("tile")[0:1, :]
            by_tile = [1, TILE_MAX, E]
            dve.tensor_copy(t_pad[:, :], c_base[0:1, :])
            link(dve.tensor_tensor(t_cnt[:, :], c_base[0:1, :], const("region")[0:1, :], ALU.subtract))
            link(dve.tensor_scalar(t_int[:, :], t_cnt[:, :], float(P - 1), None, ALU.add))
            link(dve.tensor_scalar(t_int[:, :], t_int[:, :], TILE_BITS, None, ALU.arith_shift_right))
            link(dve.tensor_copy(t_nt[:, :], t_int[:, :]))
            nt = t_nt[:, :].rearrange("p (o e) -> p o e", o=1)
            link(dve.tensor_tensor(t_sq[:, :, :], const("upto")[0:1, :].rearrange("p (a b) -> p a b", b=E),
                                   nt.to_broadcast([1, E, E]), ALU.mult))
            link(dve.tensor_reduce(t_end[:, :], t_sq[:, :, :], AX, ALU.add))
            link(dve.tensor_tensor(t_ge[:, :, :], tile_n.rearrange("p (n o) -> p n o", o=1).to_broadcast(by_tile),
                                   t_end[:, :].rearrange("p (o e) -> p o e", o=1).to_broadcast(by_tile), ALU.is_ge))
            link(dve.tensor_reduce(t_e[:, :], t_ge[:, :, :], AX, ALU.add))
            link(dve.tensor_tensor(t_ge[:, :, :], t_ge[:, :, :], nt.to_broadcast(by_tile), ALU.mult))
            link(dve.tensor_reduce(t_st[:, :], t_ge[:, :, :], AX, ALU.add))
            link(dve.tensor_tensor(t_st[:, :], tile_n, t_st[:, :], ALU.subtract))
            link(dve.tensor_scalar(t_st[:, :], t_st[:, :], float(P), None, ALU.mult))
            link(dve.scalar_tensor_tensor(t_row[:, :], t_e[:, :], float(REGION), t_st[:, :], ALU.mult, ALU.add))
            dve.tensor_scalar(t_expert[:, :], t_e[:, :], float(E - 1), None, ALU.min).then_inc(S["t_done"], 1)

            def shared_up(i, par):
                for c in range(CH):
                    dve.wait_ge(S["s_si"], i * CH + c + 1)
                    dve.tensor_tensor(s_h[:, par, c, :], s_sg[:, c, :], banks[2 * c + 1][:, :], ALU.mult)\
                        .then_inc(S["s_hd"], 1)

            def shared_add(i, par):
                dve.wait_ge(S["s_dn"], i + 1)
                xs = X[:, group(i), :]
                dve.tensor_tensor(xs, xs, banks[4 + par][:, :].rearrange("p (t d) -> p t d", t=GT), ALU.add)\
                    .then_inc(S["s_ac"], 1)

            shared_slots(dve, shared_up, shared_add)

            def hidden(t, u):
                dve.wait_ge(S["f_si"], t * UNROLL + u + 1)
                dve.tensor_tensor(f_h[:, THIRD[u], :], f_sg[:, THIRD[u], :], banks[F_UP[THIRD[u]]][:, INTER:2 * INTER],
                                  ALU.mult).then_inc(S["f_hd"], 1)

            def hidden_evac(t, u):
                dve.wait_ge(S["f_hT_ps"], t * UNROLL + u + 1)
                dve.tensor_copy(f_hT[:, THIRD[u], :], banks[F_HT[THIRD[u]]][:, 0:INTER]).then_inc(S["f_hTd"], 1)

            def slot(t, u):
                if not is_first(t, u):
                    hidden_evac(*before_tile(t, u))
                if is_tile(t):
                    hidden(t, u)

            routed_slots(dve, slot)

            for i in range(GROUPS):
                u = i % Y_RING
                dve.wait_ge(y_ld[u], 32 * (i // Y_RING + 1))
                xs = X[:, group(i), :].rearrange("p t d -> p (t d)")
                dve.tensor_tensor(xs, xs, y_in[:, u * GN:(u + 1) * GN], ALU.add).then_inc(S["y_ad"], 1)
                dve.wait_ge(S["y_ad"], i + 1)
                dve.tensor_tensor(xs, xs, y_in2[:, u * GN:(u + 1) * GN], ALU.add).then_inc(S["y_sum"], 1)


_INS = ["x", "ctx_1024", "mask_BxS2_if1", "L0_attn_Wq", "L0_attn_Wk", "L0_attn_Wv", "L0_attn_Wo", "L0_ffn_ln_scale",
        "L0_ffn_ln_bias", "L0_ffn_gate_w", "L0_ffn_Wg", "L0_ffn_Wu", "L0_ffn_Wd", "L0_ffn_sWg", "L0_ffn_sWu",
        "L0_ffn_sWd"]


def kernel(**inputs):
    import numpy as _np
    import concourse.bacc as _bacc
    from concourse import mybir as _mybir
    from concourse.bass_utils import run_bass_kernel_spmd as _run

    nc = _bacc.Bacc("TRN2", target_bir_lowering=False, num_devices=1)
    arrays, args = {}, []
    for name in _INS:
        a = _np.ascontiguousarray(inputs[name])
        arrays[f"in_{name}"] = a
        args.append(nc.dram_tensor(f"in_{name}", a.shape, _mybir.dt.from_np(a.dtype), kind="ExternalInput").ap())
    for name, a in (("shape_constants", shape_constants()), ("indicator", indicator())):
        arrays[name] = a
        args.append(nc.dram_tensor(name, a.shape, _mybir.dt.from_np(a.dtype), kind="ExternalInput").ap())
    args.append(nc.dram_tensor("block_out", (SEQS, T, D), _mybir.dt.float32, kind="ExternalOutput").ap())
    decoder_block(nc, *args)
    r = _run(nc, [arrays], core_ids=[0])
    return r.results[0]["block_out"]
```

```python
import numpy as np
import concourse.bass as bass
from concourse import mybir
from contextlib import ExitStack

F32 = mybir.dt.float32
BF16 = mybir.dt.bfloat16
F32R = mybir.dt.float32r
I32 = mybir.dt.int32
ALU = mybir.AluOpType
ACT = mybir.ActivationFunctionType
AX = mybir.AxisListType.X

P = 128
SEQS, T, D = 128, 64, 128
TOKENS = SEQS * T
H, DH = 16, 8
HALF = DH // 2
TILES = TOKENS // P
GT = 4
GROUPS = TILES // GT
GS = GT * P // T
GN = GT * P
R, C = 8, 2
E9 = DH + 1
SHARED_FROM = GROUPS + 2
BEHIND = 4
RING = 4
E, INTER, TOP = 8, 256, 2
CH = INTER // P
LN_EPS, DEN_EPS, TOP_EPS = 1e-5, 1e-6, 1e-5
SCALE = DH ** -0.5
MASKED = -1e9 / SCALE
REGION = TOKENS + P
TILE_MAX = (TOP * TOKENS + E * (P - 1)) // P
SPARE = TILE_MAX - TOP * TOKENS // P
ROW = D + 2
NOWHERE = 1 << 20
UNROLL = 15
TURNS = TILE_MAX // UNROLL
LAG = 3
E_RING = 5
TILE_BITS = 7
C_STEPS = 21
X_FIRST = 4 * GT
B_LOADS = 4
SET_ZERO, SET_DVE = 9, 6
Y_RING = 4
SB_ALIGN = 32

CONST = {"ident": P, "causal": T, "cos": HALF, "sin": HALF, "row": R, "half": C, "order": E, "before": P,
         "region": E, "place": GT * TOP, "upto": E * E, "tile": TILE_MAX}
CONST_AT = dict(zip(CONST, np.cumsum([0, *CONST.values()])[:-1].tolist()))
CONST_N = sum(CONST.values())


def shape_constants():
    c = np.zeros((P, CONST_N), np.float32)

    def part(name):
        return c[:, CONST_AT[name]:CONST_AT[name] + CONST[name]]

    p = np.arange(P)
    part("ident")[:] = np.eye(P)
    part("causal")[:] = (p % T)[:, None] <= np.arange(T)[None, :]
    inv = np.float32(10000.0) ** (-np.arange(HALF, dtype=np.float32) / np.float32(HALF))
    ang = (p % T).astype(np.float32)[:, None] * inv[None, :].astype(np.float32)
    part("cos")[:] = np.cos(ang)
    part("sin")[:] = np.sin(ang)
    part("row")[:] = (p // DH % R)[:, None] == np.arange(R)[None, :]
    part("half")[:] = (p // T)[:, None] == np.arange(C)[None, :]
    part("order")[:] = np.arange(E, 0, -1)[None, :]
    part("before")[:] = p[:, None] < p[None, :]
    part("region")[:] = np.arange(E)[None, :] * REGION
    n = np.arange(GT * TOP)
    part("place")[:] = p[:, None] + (n // TOP * P + n % TOP * TOKENS)[None, :]
    part("upto")[:] = np.tril(np.ones((E, E))).reshape(1, -1)
    part("tile")[:] = np.arange(TILE_MAX)[None, :]
    return c


def on(g):
    return not isinstance(g, int) or 0 <= g < GROUPS


def since(g, first):
    return not isinstance(g, int) or g >= first


def decoder_block(nc, x, ctx, mask, wq, wk, wv, wo, ln_scale, ln_bias, gate_w, wg, wu, wd, swg, swu, swd,
                  consts, out):
    routed = nc.dram_tensor("routed", [E * REGION + SPARE * P, ROW], F32, kind="Internal").ap()
    mixed = nc.dram_tensor("mixed", [TOP * TOKENS, D], F32, kind="Internal").ap()

    with ExitStack() as stack:
        def sb(name, shape, dt=F32):
            room_of[name] = -(-nc.sbuf_base // SB_ALIGN) * SB_ALIGN
            return stack.enter_context(nc.sbuf_tensor(name, shape, dt))

        def in_room_of(other, name, shape, dt):
            return nc.alloc_sbuf_tensor_at(name, shape, dt, offset=room_of[other])

        room_of = {}

        banks = [stack.enter_context(nc.psum_tensor(f"bank{n}", [P, 512], F32)) for n in range(8)]
        A_S, A_O, FRONT0, B_S, B_T, B_O, FRONT1 = 0, 1, 2, (3, 4), 5, 6, 7
        S_UP, S_O = ((0, 1), (3, 4)), (5, 6)
        F_UP, F_HT, F_X, F_O = (0, 1, 2), (3, 4, 5), 6, 7

        X = sb("X", [P, TILES, D])
        xfT = sb("xfT", [P, TOKENS])
        con = sb("con", [P, CONST_N])
        wqkvT = sb("wqkvT", [P, 3 * D])
        woT = sb("woT", [P, D])
        gateT = sb("gateT", [P, E])
        gate_sum = sb("gate_sum", [P, E])
        lnp = sb("lnp", [P, 2])
        shared_up_w = sb("shared_up_w", [P, 2, INTER])
        shared_down_w = sb("shared_down_w", [P, CH, D])
        ones_row = sb("ones_row", [1, P], BF16)
        before = sb("before", [P, P], BF16)
        ones = sb("ones", [P, P], BF16)
        minus_half = sb("minus_half", [P, GT])
        epsilon = sb("epsilon", [P, GT])

        def const(name):
            return con[:, CONST_AT[name]:CONST_AT[name] + CONST[name]]

        ident, causal, cos, sin, row, halves, order = (
            const(n) for n in ("ident", "causal", "cos", "sin", "row", "half", "order"))

        a_stat = sb("a_stat", [P, GT, 6])
        a_mv = sb("a_mv", [P, GT, 2])
        a_rs = sb("a_rs", [P, GT])
        a_nm = sb("a_nm", [P, GT])
        a_xn = sb("a_xn", [P, GT, D])
        a_xnT = sb("a_xnT", [P, GN])
        qk = sb("qk", [P, GT * 2 * D])
        rot = sb("rot", [P, GT * 2 * D])
        phi = sb("phi", [P, GT * 2 * D])
        qT = sb("qT", [P, 2, GN])
        KQ = sb("KQ", [P, 2, 2, GS, C, T])
        Kc, Qc = KQ[:, 0], KQ[:, 1]
        Vblk = sb("Vblk", [P, 2, GS, R, C, E9])
        Qblk = sb("Qblk", [P, RING, R, T])
        Am = sb("Am", [P, 2, R * T])
        a_den = sb("a_den", [P, 2, R * C])
        a_rec = sb("a_rec", [P, 2, R * C])
        a_y = sb("a_y", [P, GT, D])
        a_yT = sb("a_yT", [P, GN])
        b_stat = sb("b_stat", [P, GT, 6])
        b_mv = sb("b_mv", [P, GT, 2])
        b_rs = sb("b_rs", [P, GT])
        b_nm = sb("b_nm", [P, GT])
        b_xn = sb("b_xn", [P, GT, D])
        ctxP = sb("ctxP", [P, GT, D])
        ctxD = sb("ctxD", [P, GS, D])
        maskB = sb("maskB", [P, GN], I32)
        ctxT = sb("ctxT", [P, 2, GN])
        bias_row = sb("bias_row", [1, 2, GN], BF16)
        Kblk = sb("Kblk", [P, RING, R, T])
        Cblk = sb("Cblk", [P, 2, GS, R // 2, C, 2, E9])
        mx = sb("mx", [P, GS, R])
        shift = sb("shift", [P, GS, R])
        Ex = sb("Ex", [P, 2, R * T])
        ExT = sb("ExT", [P, 2, R // 2, C, T])
        b_rec = sb("b_rec", [P, 2, R * C])
        b_y = sb("b_y", [P, 2, D])
        c_stat = sb("c_stat", [P, GT, 6])
        c_mv = sb("c_mv", [P, GT, 2])
        c_rs = sb("c_rs", [P, GT])
        c_nm = sb("c_nm", [P, GT])
        c_rs2 = sb("c_rs2", [P, GT])
        c_row = sb("c_row", [P, 2, GT, TOP, ROW])
        c_xfT = sb("c_xfT", [P, GN])
        c_p = sb("c_p", [P, GT, E])
        c_t = sb("c_t", [P, GT, E])
        c_pick = sb("c_pick", [P, TOP, GT, E])
        c_sel = sb("c_sel", [P, GT, E], BF16)
        c_m = sb("c_m", [P, GT])
        c_best = sb("c_best", [P, TOP, GT])
        c_pos = sb("c_pos", [P, GT, E])
        c_hit = sb("c_hit", [P, TOP, GT, E])
        c_at = sb("c_at", [P, GT, TOP])
        c_idx = sb("c_idx", [P, 2, GT, TOP], I32)
        c_place = sb("c_place", [P, GT, TOP])
        c_base = sb("c_base", [P, E])
        pad = sb("pad", [P, ROW])
        tick = sb("tick", [P, 2])
        t_cnt = sb("t_cnt", [1, E])
        t_int = sb("t_int", [1, E], I32)
        t_nt = sb("t_nt", [1, E])
        t_sq = sb("t_sq", [1, E, E])
        t_end = sb("t_end", [1, E])
        t_ge = Kblk[0:1, :, :, :].rearrange("p m r n -> p (m r n)")[:, 0:TILE_MAX * E].rearrange("p (n e) -> p n e", e=E)
        t_e = sb("t_e", [1, TILE_MAX])
        t_st = sb("t_st", [1, TILE_MAX])
        t_pad = sb("t_pad", [1, E], I32)
        t_expert = sb("t_expert", [1, TILE_MAX], I32)
        t_row = sb("t_row", [1, TILE_MAX], I32)
        wup = KQ[:, :, :, :, :, :].rearrange("p a m b c n -> p (a m b c n)").rearrange("p (e m i) -> p e m i", e=E, m=2)
        wdn = Qblk[:, :, :, :].rearrange("p m r n -> p (m r n)").rearrange("p (e c d) -> p e c d", e=E, c=CH)
        s_sg = phi[:, :].rearrange("p (c n) -> p c n", c=CH)
        s_h = Vblk[:, :, :, :, :, :].rearrange("p m b r c e -> p (m b r c e)")[:, 0:2 * CH * GN]\
            .rearrange("p (m c n) -> p m c n", m=2, c=CH)
        WUP_N = E * 2 * INTER
        wup_hi = in_room_of("xfT", "wup_hi", [P, E, 2, INTER], F32R)
        wup_lo = in_room_of("KQ", "wup_lo", [P, E, 2, INTER], F32R)
        f_x = sb("f_x", [P, UNROLL, ROW])
        f_xT_hi = in_room_of("phi", "f_xT_hi", [P, 3, P], F32R)
        f_xT_lo = in_room_of("qT", "f_xT_lo", [P, 3, P], F32R)
        s_x_hi = in_room_of("qk", "s_x_hi", [P, 2, GN], F32R)
        s_x_lo = in_room_of("rot", "s_x_lo", [P, 2, GN], F32R)
        shared_up_hi = in_room_of("a_xn", "shared_up_hi", [P, 2, INTER], F32R)
        shared_up_lo = in_room_of("a_xnT", "shared_up_lo", [P, 2, INTER], F32R)
        f_sg, f_h, f_hT = (room[:, n * 3 * INTER:(n + 1) * 3 * INTER].rearrange("p (m i) -> p m i", i=INTER)
                           for room, n in ((qk[:, :], 0), (rot[:, :], 0), (Am[:, :, :].rearrange("p m n -> p (m n)"), 0)))
        f_y = sb("f_y", [P, UNROLL, D])
        y_in = Cblk[:, :, :, :, :, :, :].rearrange("p m b r c q e -> p (m b r c q e)")
        y_in2 = Kblk[:, :, :, :].rearrange("p m r n -> p (m r n)")

        names = """w_in x_in0 x_in1 x_in2 con_in s_in ffw_in set_z set_ps set_cp set_ps2 set_d
            a_st a_ag a_ve a_pw a_rsd a_xnd a_xnT_ps a_xnTd a_qk_ps a_qkd a_v_ps a_vd a_r2 a_r1 a_rt a_mn a_ex a_ph
            a_qT_ps a_qTd a_kT_ps a_kcd a_qb a_s a_am a_av a_dn a_rc a_yd a_yT_ps a_yTd a_o a_x1
            b_st b_ag b_ve b_pw b_rsd b_xnd b_qT_ps b_qcd b_in b_cT_ps b_cTd b_bi b_kb b_cb b_s b_mx b_mh
            b_e b_eT_ps b_eTd b_av b_rc b_yd b_x2
            c_st c_ag c_ve c_pw c_rsd c_xf c_cp c_v1 c_v2 c_ve2 c_rsd2 c_xfT_ps c_xfTd c_lg_ps c_ch c_lg c_ex c_seld
            c_ps c_posd c_hitd c_atd c_read c_idxd c_tick c_sc0 c_sc1
            t_ch t_done t_spare t_padded
            s_xh s_xl s_up s_si s_hd s_dn s_ac
            f_xT_ps f_xTd f_xTl w_hi w_lo f_up f_si f_hd f_hT_ps f_hTd f_dn f_yd f_tick
            y_ad y_sum y_st""".split()
        S = {n: stack.enter_context(nc.semaphore(n)) for n in names}
        c_sc = [S["c_sc0"], S["c_sc1"]]
        f_in = [stack.enter_context(nc.semaphore(f"f_in{u}")) for u in range(UNROLL)]
        f_out = [stack.enter_context(nc.semaphore(f"f_out{u}")) for u in range(UNROLL)]
        y_ld = [stack.enter_context(nc.semaphore(f"y_ld{u}")) for u in range(Y_RING)]
        block = stack.enter_context(nc.Block())

        tok = x.rearrange("(t s) k d -> (s k) t d", s=2)
        tok_out = out.rearrange("(t s) k d -> (s k) t d", s=2)
        ctx_v = ctx.rearrange("b k d -> k b d")
        ctx_p = ctx.rearrange("(t s) k d -> (s k) t d", s=2)
        mixed_v = mixed.rearrange("(o t p) d -> o p t d", o=TOP, p=P)

        def group(i):
            return bass.ds(i * GT, GT)

        def steps(eng, step):
            first, last = BEHIND + 2, GROUPS - BEHIND
            for s in range(-3, first):
                step(s, s % 2)
            with eng.Fori(first, last - 1, 2) as s:
                step(s, 0)
                step(s + 1, 1)
            for s in range(last, GROUPS + BEHIND + 1):
                step(s, s % 2)

        def slot_of(g, k):
            return (g, k) if 0 <= k < GS else (g - 1, k + GS) if k < 0 else (g + 1, k - GS)

        def b_alone(s):
            return isinstance(s, int) and s in (GROUPS, GROUPS + 1)

        def b_starts_of(s, k):
            if not b_alone(s):
                return [k]
            return [0, 1] if k == 0 else [k + 1] if k + 1 < GS else []

        def b_bank(alone, k):
            return banks[(*B_S, A_S, A_O)[k % 4] if alone else B_S[k % 2]]

        def b_ends_of(s, k):
            def before(n):
                return (-2, k - n, True) if k >= n else (-3, k - n + GS, False)

            if not isinstance(s, int) or s < GROUPS or s == GROUPS and k == 0:
                return [before(1)]
            if b_alone(s):
                return [before(2)] if s > GROUPS or k > 1 else []
            return [before(2), before(1)] if s == GROUPS + 2 and k == 0 else []

        def b_last_half(s):
            return {GROUPS + 1: 2, GROUPS + 2: 0}.get(s, 1) if isinstance(s, int) else 1

        def b_half(s, k):
            if k == 5 + b_alone(s):
                return -2, 0
            return (-3, 1) if k == b_last_half(s) else None

        def s_before(s, n):
            return isinstance(s, int) and s < n

        def s_is_last(s):
            return isinstance(s, int) and s == GROUPS + BEHIND - 1

        def routing(s):
            return (0, 1, 2, 1, 2) if s_is_last(s) else (2, 3, 4, 6, 5)

        def shared_of(s, k):
            return (s - SHARED_FROM) * GS + k if isinstance(s, int) else -GS

        def routed_slots(eng, slot):
            for u in range(UNROLL):
                slot(0, u)
            with eng.Fori(1, TURNS) as t:
                for u in range(UNROLL):
                    slot(t, u)
            for u in range(LAG):
                slot(TURNS, u)

        def tile_of(t, u, back):
            t, u = (t, u - back) if u >= back else (t - 1, u - back + UNROLL)
            return None if isinstance(t, int) and not 0 <= t < TURNS else (t, u)

        def is_first(t, u):
            return isinstance(t, int) and t == 0 and u == 0

        @block.sync
        def _(sp):
            sp.dma_start(X[:, 0:GT, :], tok[:, 0:GT, :]).then_inc(S["x_in0"], 16)
            sp.dma_start(con[:, :], consts).then_inc(S["con_in"], 16)
            for n, w in enumerate((wq, wk, wv, wo)):
                sp.dma_start(a_xn[:, n, :], w).then_inc(S["w_in"], 16)
            sp.dma_start(b_xn[0:E, 0, :], gate_w).then_inc(S["w_in"], 16)
            sp.dma_start(lnp[:, 0:1], ln_scale.rearrange("(d a) -> d a", a=1)).then_inc(S["w_in"], 16)
            sp.dma_start(lnp[:, 1:2], ln_bias.rearrange("(d a) -> d a", a=1)).then_inc(S["w_in"], 16)
            sp.dma_start(X[:, GT:X_FIRST, :], tok[:, GT:X_FIRST, :]).then_inc(S["x_in1"], 16)

            def load_ctx(j):
                sp.dma_start(ctxP[:, :, :], ctx_p[:, group(j), :]).then_inc(S["b_in"], 16)
                for half in range(2):
                    sp.dma_start(ctxD[half * T:(half + 1) * T, :, :],
                                 ctx_v[:, bass.ds(j * GS, GS), :]).then_inc(S["b_in"], 16)
                sp.dma_start(maskB[:, :], mask[bass.ds(j * GS, GS), :].rearrange("b k -> (b k)")
                             .rearrange("(o n) -> o n", o=1).to_broadcast([P, GN])).then_inc(S["b_in"], 16)

            load_ctx(0)
            sp.dma_start(X[:, X_FIRST:TILES, :], tok[:, X_FIRST:TILES, :]).then_inc(S["x_in2"], 16)
            for n, w in enumerate((swg, swu)):
                sp.dma_start(shared_up_w[:, n, :], w).then_inc(S["s_in"], 16)
            sp.dma_start(shared_down_w[:, :, :], swd.rearrange("(c i) d -> i c d", c=CH)).then_inc(S["s_in"], 16)
            sp.wait_ge(S["set_z"], 2)
            sp.wait_ge(S["set_d"], SET_DVE)
            sp.dma_start(routed[E * REGION:E * REGION + SPARE * P, :].rearrange("(n p) f -> p n f", p=P),
                         pad[:, :].rearrange("p (o f) -> p o f", o=1).to_broadcast([P, SPARE, ROW]))\
                .then_inc(S["t_spare"], 16)
            with sp.Fori(1, GROUPS) as j:
                sp.wait_ge(S["con_in"], 16)
                sp.wait_ge(S["b_cT_ps"], j)
                sp.wait_ge(S["b_cb"], 4 * j)
                sp.wait_ge(S["b_bi"], j)
                sp.wait_ge(S["b_cTd"], j)
                load_ctx(j)

            sp.wait_ge(S["a_s"], GS * GROUPS)
            sp.wait_ge(S["b_s"], GS * GROUPS)
            for n, w in enumerate((wg, wu)):
                sp.dma_start(wup[:, :, n, :], w.rearrange("e d i -> d e i")).then_inc(S["ffw_in"], 16)
            for c in range(CH):
                sp.dma_start(wdn[:, :, c, :],
                             wd[:, c * P:(c + 1) * P, :].rearrange("e i d -> i e d")).then_inc(S["ffw_in"], 16)

            sp.wait_ge(S["t_ch"], 1)
            for e in range(E):
                at = sp.value_load(t_pad[0:1, e:e + 1], min_val=e * REGION, max_val=e * REGION + TOKENS)
                sp.dma_start(routed[bass.ds(at, P), :], pad[:, :]).then_inc(S["t_padded"], 16)
            sp.wait_ge(S["t_done"], 1)
            sp.wait_ge(S["t_padded"], 16 * E)
            sp.wait_ge(S["t_spare"], 16)
            for m in range(2):
                sp.wait_ge(c_sc[m], 16 * GT * TOP * (GROUPS // 2))

            def load_tile(t, u):
                at = sp.value_load(t_row[0:1, bass.ds(t * UNROLL + u, 1)], min_val=0,
                                   max_val=E * REGION + (SPARE - 1) * P)
                if since(t, 1):
                    sp.wait_ge(f_out[u], 16 * t)
                sp.dma_start(f_x[:, u, :], routed[bass.ds(at, P), :]).then_inc(f_in[u], 16)

            for u in range(UNROLL):
                load_tile(0, u)
            with sp.Fori(1, TURNS) as t:
                for u in range(UNROLL):
                    load_tile(t, u)

            for u in range(UNROLL):
                sp.wait_ge(f_out[u], 16 * TURNS)

            def load_mixed(i, u):
                sp.dma_start(y_in[:, u * GN:(u + 1) * GN].rearrange("p (t d) -> p t d", t=GT),
                             mixed_v[0][:, group(i), :]).then_inc(y_ld[u], 16)
                sp.dma_start(y_in2[:, u * GN:(u + 1) * GN].rearrange("p (t d) -> p t d", t=GT),
                             mixed_v[1][:, group(i), :]).then_inc(y_ld[u], 16)

            for u in range(Y_RING):
                load_mixed(u, u)
            for i in range(Y_RING, GROUPS):
                sp.wait_ge(S["y_sum"], i - Y_RING + 1)
                load_mixed(i, i % Y_RING)
            sp.wait_ge(S["y_st"], 16 * GROUPS)

        @block.tensor
        def _(pe):
            pe.wait_ge(S["con_in"], 16)
            pe.wait_ge(S["w_in"], 7 * 16)
            for n in range(4):
                pe.transpose(banks[0][:, n * D:(n + 1) * D], a_xn[:, n, :], ident)
            pe.transpose(banks[1][:, 0:E], b_xn[0:E, 0, :], ident[0:E, 0:E]).then_inc(S["set_ps"], 1)
            pe.wait_ge(S["set_z"], 1)
            pe.wait_ge(S["set_d"], SET_DVE)
            pe.matmul(banks[1][:, E:2 * E], rot[:, 0:P], rot[:, P:P + E], start=True, stop=True).then_inc(S["set_ps2"], 1)
            pe.wait_ge(S["set_cp"], 2)

            def a_norm_T(f, d):
                pe.wait_ge(S["a_xnd"], GT * f + GT)
                if on(d):
                    pe.wait_ge(S["c_lg"], d + 1)
                elif since(f, 1):
                    pe.wait_ge(S["a_kcd"], C * f)
                for t in range(GT):
                    ins = pe.transpose(banks[FRONT0][:, t * P:(t + 1) * P], a_xn[:, t, :], ident)
                ins.then_inc(S["a_xnT_ps"], 1)

            def a_project(f, h):
                if on(h):
                    pe.wait_ge(S["b_cTd"], h + 1)
                elif f >= 1:
                    pe.wait_ge(S["a_qTd"], f)
                pe.wait_ge(S["a_xnTd"], f + 1)
                for m, bank in enumerate((FRONT1, FRONT0)):
                    for t in range(2):
                        n = 2 * m + t
                        ins = pe.matmul(banks[bank][:, t * 2 * D:(t + 1) * 2 * D], a_xnT[:, n * P:(n + 1) * P],
                                        wqkvT[:, 0:2 * D], start=True, stop=True)
                    ins.then_inc(S["a_qk_ps"], 1)

            def a_project_v(f):
                pe.wait_ge(S["a_qkd"], 2 * f + 1)
                for b in range(GS):
                    for c in range(C):
                        ins = pe.matmul(banks[FRONT1][c * T:(c + 1) * T, b * T:(b + 1) * T],
                                        a_xnT[:, b * T:(b + 1) * T],
                                        wqkvT[:, 2 * D + c * T:2 * D + (c + 1) * T], start=True, stop=True)
                ins.then_inc(S["a_v_ps"], 1)

            def a_q_T(f, h, c):
                pe.wait_ge(S["a_ph"], f + 1)
                if on(c):
                    pe.wait_ge(S["c_xfTd"], 2 * c + 2)
                elif on(h):
                    pe.wait_ge(S["a_x1"], h + 1)
                else:
                    pe.wait_ge(S["a_vd"], C * f + C)
                v = phi[:, :].rearrange("p (t a d) -> p t a d", t=GT, a=2)
                for t in range(GT):
                    ins = pe.transpose(banks[FRONT1][:, t * P:(t + 1) * P], v[:, t, 0, :], ident)
                ins.then_inc(S["a_qT_ps"], 1)

            def a_k_T(f, h, d):
                if on(d):
                    pe.wait_ge(S["c_read"], d + 1)
                elif on(h):
                    pe.wait_ge(S["a_yTd"], h + 1)
                v = phi[:, :].rearrange("p (t a d) -> p t a d", t=GT, a=2)
                for t in range(GT):
                    ins = pe.transpose(banks[FRONT0][:, t * P:(t + 1) * P], v[:, t, 1, :], ident)
                ins.then_inc(S["a_kT_ps"], 1)

            def a_scores(a, k, par):
                pe.wait_ge(S["a_qb"], GS * a + k + 1)
                if k == 0:
                    pe.wait_ge(S["a_kcd"], C * a + C)
                if not (isinstance(a, int) and a == 0 and k == 0):
                    pe.wait_ge(S["a_am"], GS * a + k)
                pe.matmul(banks[A_S][:, :], Kc[:, par, k, :, :].rearrange("p c n -> p (c n)"),
                          Qblk[:, k % RING, :, :], start=True, stop=True).then_inc(S["a_s"], 1)

            def a_values_wait(a, k):
                pe.wait_ge(S["a_am"], GS * a + k + 1)
                if k == GS // 2:
                    pe.wait_ge(S["a_yd"], GT * a + 2)
                elif k == 0:
                    if not since(a, 1):
                        pe.wait_ge(S["set_cp"], 3)
                    pe.wait_ge(S["a_vd"], C * a + C)
                    if since(a, 1):
                        pe.wait_ge(S["a_yd"], GT * a)

            def a_values(k, par, r):
                at = k // 2 % 2 * H * E9 + r * C * E9
                return pe.matmul(banks[A_O][k % 2 * T:(k % 2 + 1) * T, at:at + C * E9], Am[:, k % 2, r * T:(r + 1) * T],
                                 Vblk[:, par, k, r, :, :].rearrange("p c e -> p (c e)"), start=True, stop=True)

            def a_out_T(h, f, d):
                pe.wait_ge(S["a_yd"], GT * h + GT)
                if on(f):
                    pe.wait_ge(S["a_qkd"], 2 * f + 2)
                elif on(d):
                    pe.wait_ge(S["c_lg"], d + 1)
                for t in range(GT):
                    ins = pe.transpose(banks[FRONT0][:, t * P:(t + 1) * P], a_y[:, t, :], ident)
                ins.then_inc(S["a_yT_ps"], 1)

            def a_out(h, f):
                if on(f):
                    pe.wait_ge(S["a_vd"], C * f + C)
                else:
                    pe.wait_ge(S["b_cTd"], h + 1)
                pe.wait_ge(S["a_yTd"], h + 1)
                for t in range(GT):
                    ins = pe.matmul(banks[FRONT1][:, t * D:(t + 1) * D], a_yT[:, t * P:(t + 1) * P], woT[:, :],
                                    start=True, stop=True)
                ins.then_inc(S["a_o"], 1)

            def b_ctx_T(h, a):
                pe.wait_ge(S["b_in"], B_LOADS * 16 * (h + 1))
                if not isinstance(h, int) or h >= 1:
                    pe.wait_ge(S["b_qcd"], C * h)
                else:
                    pe.wait_ge(S["a_qTd"], a + 1)
                for b in range(GS // 2):
                    ins = pe.transpose(banks[FRONT1][:, b * P:(b + 1) * P], ctxP[:, b, :], ident)
                ins.then_inc(S["b_cT_ps"], 1)

            def b_norm_T(h, f):
                pe.wait_ge(S["b_xnd"], GT * h + GT)
                if on(f):
                    pe.wait_ge(S["a_qTd"], f + 1)
                for t in range(GT):
                    ins = pe.transpose(banks[FRONT1][:, t * P:(t + 1) * P], b_xn[:, t, :], ident)
                ins.then_inc(S["b_qT_ps"], 1)

            def b_scores(b, k, par, alone):
                pe.wait_ge(S["b_kb"], GS * b + k + 1)
                if k == 0:
                    pe.wait_ge(S["b_qcd"], C * b + C)
                    pe.wait_ge(S["b_bi"], b + 1)
                first = alone and b == GROUPS - 2
                if first and k in (2, 3):
                    pe.wait_ge(S["a_yd"], GT * GROUPS)
                elif not (isinstance(b, int) and b == 0 and k < 2):
                    pe.wait_ge(S["b_e"], GS * b + k - (3 if alone and not (first and k < 2) else 1))
                bank = b_bank(alone, k)
                pe.matmul(bank[:, :], Qc[:, par, k, :, :].rearrange("p c n -> p (c n)"), Kblk[:, k % RING, :, :],
                          start=True, stop=False)
                keys = bias_row[0:1, par, k * T:(k + 1) * T].rearrange("p (o n) -> p o n", o=1)\
                    .to_broadcast([1, R, T])
                pe.matmul(bank[:, :], ones_row[0:1, :], keys, start=False, stop=True).then_inc(S["b_s"], 1)

            def b_probs_T(b, k):
                pe.wait_ge(S["b_e"], GS * b + k + 1)
                if since(b, 1) or k >= 1:
                    pe.wait_ge(S["b_eTd"], GS * b + k)
                for rp in range(R // 2):
                    ins = pe.transpose(banks[B_T][:, rp * P:(rp + 1) * P], Ex[:, k % 2, rp * P:(rp + 1) * P], ident)
                ins.then_inc(S["b_eT_ps"], 1)

            def b_values_wait(b, k):
                pe.wait_ge(S["b_eTd"], GS * b + k + 1)
                if k == GS // 2:
                    pe.wait_ge(S["b_yd"], 8 * b + 4)
                elif k == 0:
                    pe.wait_ge(S["b_cb"], 4 * b + 4)
                    if since(b, 1):
                        pe.wait_ge(S["b_yd"], 8 * b)

            def b_values(k, par, r):
                rp, c = r // C, r % C
                at = k // 2 % 2 * H * E9 + r * 2 * E9
                return pe.matmul(banks[B_O][k % 2 * T:(k % 2 + 1) * T, at:at + 2 * E9], ExT[:, k % 2, rp, c, :],
                                 Cblk[:, par, k, rp, c, :, :].rearrange("p q e -> p (q e)"), start=True, stop=True)

            def c_norm_T(c, h, par):
                pe.wait_ge(S["c_xf"], GT * c + GT)
                if on(h):
                    pe.wait_ge(S["a_x1"], h + 1)
                for t in range(GT):
                    ins = pe.transpose(banks[FRONT1][:, t * P:(t + 1) * P], c_row[:, par, t, 0, 0:D], ident)
                ins.then_inc(S["c_xfT_ps"], 1)

            def c_logits(c, f, d):
                if on(f):
                    pe.wait_ge(S["a_kcd"], C * f + C)
                elif on(d):
                    pe.wait_ge(S["c_read"], d + 1)
                pe.wait_ge(S["c_xfTd"], 2 * c + 2)
                for t in range(GT):
                    ins = pe.matmul(banks[FRONT0][:, t * E:(t + 1) * E], c_xfT[:, t * P:(t + 1) * P], gateT[:, :],
                                    start=True, stop=True)
                ins.then_inc(S["c_lg_ps"], 1)

            def c_positions(d, h):
                pe.wait_ge(S["c_seld"], d + 1)
                if on(h):
                    pe.wait_ge(S["a_yTd"], h + 1)
                bank = banks[FRONT0]
                pe.matmul(bank[:, 0:GT * E], before[:, :], c_sel[:, :, :].rearrange("p t e -> p (t e)"),
                          start=True, stop=False, skip_group_check=True)
                for t in range(GT - 1):
                    later = GT - 1 - t
                    pe.matmul(bank[:, (t + 1) * E:GT * E], ones[:, :],
                              c_sel[:, t:t + 1, :].to_broadcast([P, later, E]), start=False, stop=False,
                              skip_group_check=True)
                for t in range(GT):
                    ins = pe.matmul(bank[:, GT * E:(GT + 1) * E], ones[:, :], c_sel[:, t, :], start=False,
                                    stop=(t == GT - 1), skip_group_check=True)
                ins.then_inc(S["c_ps"], 1)

            def s_up(i):
                if i == 0:
                    pe.wait_ge(S["s_in"], 3 * 16)
                    pe.wait_ge(S["w_lo"], 1)
                    pe.wait_ge(S["a_yd"], GT * GROUPS)
                    pe.wait_ge(S["b_eTd"], GS * GROUPS)
                pe.wait_ge(S["s_xl"], i + 1)
                for c in range(CH):
                    if i:
                        pe.wait_ge(S["s_hd"], CH * i + c - 1)
                    for m in range(2):
                        for n, (w_part, x_part) in enumerate(((shared_up_hi, s_x_hi), (shared_up_hi, s_x_lo),
                                                              (shared_up_lo, s_x_hi))):
                            ins = pe.matmul(banks[S_UP[c][m]][:, :], w_part[:, m, c * P:(c + 1) * P],
                                            x_part[:, i % 2, :], start=(n == 0), stop=(n == 2))
                    ins.then_inc(S["s_up"], 1)

            def s_down(i):
                pe.wait_ge(S["s_hd"], CH * i + CH)
                if i >= 2:
                    pe.wait_ge(S["s_ac"], i - 1)
                else:
                    pe.wait_ge(S["b_yd"], 8 * GROUPS)
                for t in range(GT):
                    for c in range(CH):
                        ins = pe.matmul(banks[S_O[i % 2]][:, t * D:(t + 1) * D], s_h[:, i % 2, c, t * P:(t + 1) * P],
                                        shared_down_w[:, c, :], start=(c == 0), stop=(c == CH - 1))
                ins.then_inc(S["s_dn"], 1)

            def step(s, par):
                f, a, h, b, c, d = s + 1, s, s - 1, s - 2, s - 3, s - BEHIND
                odd = 1 - par
                for k in range(GS):
                    if k == 0 and on(h):
                        b_ctx_T(h, a)
                    if k == 0 and on(f):
                        a_norm_T(f, d)
                    if k == 1 and on(f):
                        a_project(f, h)
                    if k == 2 and on(f):
                        a_project_v(f)
                    if k == 2 and on(h):
                        a_out_T(h, f, d)
                    if k == 3 and on(h):
                        a_out(h, f)
                    if k == 4 and on(c):
                        c_norm_T(c, h, odd)
                    if k == 5 and on(f):
                        a_q_T(f, h, c)
                    if k == 7 and on(h) and not b_alone(s):
                        b_norm_T(h, f)
                    for n in b_starts_of(s, k) if on(b) else ():
                        b_scores(b, n, par, b_alone(s))
                    last_b, n = slot_of(b, k - 1)
                    if on(last_b):
                        b_probs_T(last_b, n)
                    next_a, m = slot_of(a, k + 1)
                    if on(next_a):
                        a_scores(next_a, m, odd if m == 0 else par)
                    if on(a):
                        a_values_wait(a, k)
                    ends = [(s + back, n, par if own else odd) for back, n, own in b_ends_of(s, k) if on(s + back)]
                    for g, n, g_par in ends[:1]:
                        b_values_wait(g, n)
                    for r in range(R):
                        if on(a):
                            ins_a = a_values(k, par, r)
                        for g, n, g_par in ends[:1]:
                            ins_b = b_values(n, g_par, r)
                    if on(a):
                        ins_a.then_inc(S["a_av"], 1)
                    if ends:
                        ins_b.then_inc(S["b_av"], 1)
                    for g, n, g_par in ends[1:]:
                        b_values_wait(g, n)
                        for r in range(R):
                            ins_b = b_values(n, g_par, r)
                        ins_b.then_inc(S["b_av"], 1)
                    if k == routing(s)[2] and on(d):
                        c_positions(d, h)
                    if k == 5 and on(f):
                        a_k_T(f, h, d)
                    if k == 6 and on(c):
                        c_logits(c, f, d)
                    if k == 6 and on(h) and b_alone(s):
                        b_norm_T(h, f)
                    i = shared_of(s, k)
                    if i in range(GROUPS):
                        s_up(i)
                    if i in range(1, GROUPS + 1):
                        s_down(i - 1)

            steps(pe, step)

            pe.wait_ge(S["s_ac"], GROUPS)
            pe.wait_ge(S["ffw_in"], (2 + CH) * 16)
            pe.wait_ge(S["w_lo"], 1 + E)
            pe.wait_ge(S["t_done"], 1)

            def tile_T(t, u):
                n = t * UNROLL + u
                pe.wait_ge(f_in[u], 16 * t + 16)
                if not is_first(t, u):
                    pe.wait_ge(S["f_xTl"], n)
                pe.transpose(banks[F_X][:, 0:P], f_x[:, u, 0:D], ident).then_inc(S["f_xT_ps"], 1)

            def load_expert(t, u):
                at = t_expert[0:1, bass.ds(t * UNROLL + u, 1)]
                pe.reg_load(experts[u % E_RING], at)

            def expert_of(tile):
                return pe.snap(experts[tile[1] % E_RING], min_val=0, max_val=E - 1)

            def tile_up(t, u, e):
                pe.wait_ge(S["f_xTl"], t * UNROLL + u + 1)
                for n, (x_part, w_part) in enumerate(((f_xT_hi, wup_hi), (f_xT_lo, wup_hi), (f_xT_hi, wup_lo))):
                    ins = pe.matmul(banks[F_UP[u % 3]][:, :], x_part[:, u % 3, :],
                                    w_part[:, bass.ds(e, 1), :, :].rearrange("p o m i -> p (o m i)"),
                                    start=(n == 0), stop=(n == 2))
                ins.then_inc(S["f_up"], 1)

            def hidden_T(t, u):
                pe.wait_ge(S["f_hd"], t * UNROLL + u + 1)
                for c in range(CH):
                    ins = pe.transpose(banks[F_HT[u % 3]][:, c * P:(c + 1) * P],
                                       f_h[:, u % 3, c * P:(c + 1) * P], ident)
                ins.then_inc(S["f_hT_ps"], 1)

            def tile_down(t, u, e):
                n = t * UNROLL + u
                pe.wait_ge(S["f_hTd"], n + 1)
                if not is_first(t, u):
                    pe.wait_ge(S["f_yd"], n)
                for c in range(CH):
                    ins = pe.matmul(banks[F_O][:, 0:D], f_hT[:, u % 3, c * P:(c + 1) * P],
                                    wdn[:, bass.ds(e, 1), c, :].rearrange("p o d -> p (o d)"),
                                    start=(c == 0), stop=(c == CH - 1))
                ins.then_inc(S["f_dn"], 1)

            def slot(t, u):
                last, third = tile_of(t, u, 1), tile_of(t, u, LAG)
                if tile_of(t, u, 0):
                    tile_T(t, u)
                if last:
                    tile_up(*last, expert_of(last))
                if tile_of(t, u, 0):
                    load_expert(t, u)
                if third:
                    tile_down(*third, expert_of(third))
                if tile_of(t, u, 2):
                    hidden_T(*tile_of(t, u, 2))

            experts = [pe.alloc_register(f"expert{n}") for n in range(E_RING)]
            routed_slots(pe, slot)

        @block.scalar
        def _(act):
            act.wait_ge(S["set_ps"], 1)
            act.copy(wqkvT[:, :], banks[0][:, 0:3 * D]).then_inc(S["set_cp"], 1)
            act.copy(woT[:, :], banks[0][:, 3 * D:4 * D]).then_inc(S["set_cp"], 1)
            act.wait_ge(S["set_ps2"], 1)
            act.copy(gate_sum[:, :], banks[1][:, E:2 * E]).then_inc(S["set_cp"], 1)
            def halves_of(bank, c):
                return banks[bank][c * T:(c + 1) * T, :].rearrange("p (b n) -> p b n", n=T)

            def normalise(i, src, rs, nm, dst, s_rs, s_xn):
                act.wait_ge(s_rs, i + 1)
                for t in range(GT):
                    act.activation(dst(t), src(t), ACT.Identity, bias=nm[:, t:t + 1], scale=rs[:, t:t + 1]).then_inc(s_xn, 1)

            def x_tile(i):
                return lambda t: X[:, bass.ds(i * GT + t, 1), :].rearrange("p o d -> p (o d)")

            def a_norm(f):
                if since(f, 1):
                    act.wait_ge(S["a_xnT_ps"], f)
                normalise(f, x_tile(f), a_rs, a_nm, lambda t: a_xn[:, t, :], S["a_rsd"], S["a_xnd"])

            def a_norm_evac(f):
                act.wait_ge(S["a_xnT_ps"], f + 1)
                act.copy(a_xnT[:, :], banks[FRONT0][:, :]).then_inc(S["a_xnTd"], 1)

            def a_qk_evac(f):
                if since(f, 1):
                    act.wait_ge(S["a_ph"], f)
                for m, bank in enumerate((FRONT1, FRONT0)):
                    act.wait_ge(S["a_qk_ps"], 2 * f + m + 1)
                    act.copy(qk[:, m * GN:(m + 1) * GN], banks[bank][:, :]).then_inc(S["a_qkd"], 1)

            def a_v_evac(f, par):
                if since(f, 2):
                    act.wait_ge(S["a_av"], GS * (f - 1))
                else:
                    act.wait_ge(S["set_z"], SET_ZERO)
                act.wait_ge(S["a_v_ps"], f + 1)
                for c in range(C):
                    rows = slice(c * T, (c + 1) * T)
                    act.copy(Vblk[rows, par, :, :, c, 0:DH],
                             banks[FRONT1][rows, :].rearrange("p (b r e) -> p b r e", r=R, e=DH))\
                        .then_inc(S["a_vd"], 1)

            def a_exp(f):
                act.wait_ge(S["a_rt"], 2 * f + 2)
                act.activation(qk[:, :], rot[:, :], ACT.Relu, scale=-1.0).then_inc(S["a_mn"], 1)
                act.wait_ge(S["a_mn"], f + 1)
                act.activation(qk[:, :], qk[:, :], ACT.Exp, scale=-1.0).then_inc(S["a_ex"], 1)

            def a_q_T_evac(f, par):
                act.wait_ge(S["a_qT_ps"], f + 1)
                if since(f, 2):
                    act.wait_ge(S["a_qb"], GS * (f - 1))
                act.copy(qT[:, par, :], banks[FRONT1][:, :]).then_inc(S["a_qTd"], 1)

            def a_k_T_evac(f, par):
                act.wait_ge(S["a_kT_ps"], f + 1)
                if since(f, 2):
                    act.wait_ge(S["a_s"], GS * (f - 1))
                else:
                    act.wait_ge(S["set_d"], SET_DVE + 1)
                for c in range(C):
                    act.copy(Kc[c * T:(c + 1) * T, par, :, c, :], halves_of(FRONT0, c)).then_inc(S["a_kcd"], 1)

            def a_out_evac(h):
                act.wait_ge(S["a_yT_ps"], h + 1)
                act.copy(a_yT[:, :], banks[FRONT0][:, :]).then_inc(S["a_yTd"], 1)

            def b_context(h, par, c):
                act.wait_ge(S["b_in"], B_LOADS * 16 * (h + 1))
                if since(h, 2):
                    act.wait_ge(S["b_av"], GS * (h - 1))
                src = ctxD[:, :, :].rearrange("p b (c r q e) -> p c q b r e", c=C, q=2, e=DH)
                for q in range(2):
                    act.activation(Cblk[:, par, :, :, c, q, 0:DH], src[:, c, q], ACT.Copy, scale=halves[:, q:q + 1])\
                        .then_inc(S["b_cb"], 1)

            def b_norm_evac(h, par):
                act.wait_ge(S["b_qT_ps"], h + 1)
                if since(h, 2):
                    act.wait_ge(S["b_s"], GS * (h - 1))
                for c in range(C):
                    act.copy(Qc[c * T:(c + 1) * T, par, :, c, :], halves_of(FRONT1, c)).then_inc(S["b_qcd"], 1)

            def b_exp(b, k, alone):
                act.wait_ge(S["b_mh"], GS * b + k + 1)
                for r in range(R):
                    cols = slice(r * T, (r + 1) * T)
                    ins = act.activation(Ex[:, k % 2, cols], b_bank(alone, k)[:, cols], ACT.Exp,
                                         bias=shift[:, k, r:r + 1], scale=SCALE)
                ins.then_inc(S["b_e"], 1)

            def b_probs_evac(b, k):
                act.wait_ge(S["b_eT_ps"], GS * b + k + 1)
                act.copy(ExT[:, k % 2].rearrange("p r c q -> p (r c q)"), banks[B_T][:, :]).then_inc(S["b_eTd"], 1)

            def c_norm(c, par):
                if since(c, 2):
                    act.wait_ge(c_sc[par], 16 * TOP * GT // 2 * (c - par))
                normalise(c, x_tile(c), c_rs, c_nm, lambda t: c_row[:, par, t, 0, 0:D], S["c_rsd"], S["c_xf"])

            def c_norm_evac(c, par):
                act.wait_ge(S["c_xfT_ps"], c + 1)
                if since(c, 1):
                    act.wait_ge(S["c_lg_ps"], c)
                act.copy(c_xfT[:, :], banks[FRONT1][:, :]).then_inc(S["c_xfTd"], 1)
                act.copy(xfT[:, bass.ds(c * GN, GN)], banks[FRONT1][:, :]).then_inc(S["c_xfTd"], 1)

            def c_second_row(c, par):
                act.wait_ge(S["c_xf"], GT * c + GT)
                act.copy(c_row[:, par, :, 1, 0:D], c_row[:, par, :, 0, 0:D]).then_inc(S["c_cp"], 1)

            def c_exp(c):
                act.wait_ge(S["c_lg"], c + 1)
                act.activation(c_p[:, :, :], c_p[:, :, :], ACT.Exp).then_inc(S["c_ex"], 1)

            def s_high(i):
                if i >= 2:
                    act.wait_ge(S["s_up"], CH * (i - 1))
                else:
                    act.wait_ge(S["a_ph"], GROUPS)
                act.wait_ge(S["c_xfTd"], 2 * i + 2)
                act.copy(s_x_hi[:, i % 2, :], xfT[:, i * GN:(i + 1) * GN]).then_inc(S["s_xh"], 1)

            def s_silu(i):
                for c in range(CH):
                    act.wait_ge(S["s_up"], i * CH + c + 1)
                    if i:
                        act.wait_ge(S["s_hd"], (i - 1) * CH + c + 1)
                    act.activation(s_sg[:, c, :], banks[S_UP[c][0]][:, :], ACT.Silu).then_inc(S["s_si"], 1)

            def step(s, par):
                e, f, a, h, b, c, d = s + 2, s + 1, s, s - 1, s - 2, s - 3, s - BEHIND
                odd = 1 - par
                for k in range(GS):
                    if k == 0 and on(f):
                        a_norm_evac(f)
                    if k == 1 and on(f):
                        a_qk_evac(f)
                    if k == 2 and on(f):
                        a_v_evac(f, odd)
                    if k == 2 and on(h):
                        a_out_evac(h)
                    if k == 3 and on(c) and not b_alone(s):
                        c_norm(c, odd)
                    if k == 4 and on(f):
                        a_exp(f)
                    if k == 5 and on(f):
                        a_q_T_evac(f, odd)
                    if k == 7 and on(h):
                        b_norm_evac(h, odd)
                    for back, n, own in b_ends_of(s, k):
                        if on(s + back):
                            b_probs_evac(s + back, n)
                    if k == 3 and on(c) and b_alone(s):
                        c_norm(c, odd)
                    if k == 6 and on(f):
                        a_k_T_evac(f, odd)
                    if k == 4 and on(c):
                        c_norm_evac(c, odd)
                    if on(b):
                        b_exp(b, k, b_alone(s))
                    if k == 6 and on(c):
                        c_second_row(c, odd)
                    if shared_of(s, k) + 1 in range(GROUPS):
                        s_high(shared_of(s, k) + 1)
                    if shared_of(s, k) in range(GROUPS):
                        s_silu(shared_of(s, k))
                    if k in (1, 3) and on(h):
                        b_context(h, odd, k // 3)
                    if k == (6 if s_before(s, 0) else 5) and on(e):
                        a_norm(e)
                    if k == 7 and on(c):
                        c_exp(c)

            steps(act, step)

            act.wait_ge(S["s_ac"], GROUPS)

            def tile_T_evac(t, u):
                n = t * UNROLL + u
                act.wait_ge(S["f_xT_ps"], n + 1)
                if since(t, 1) or u >= 3:
                    act.wait_ge(S["f_up"], n - 2)
                act.copy(f_xT_hi[:, u % 3, :], banks[F_X][:, 0:P]).then_inc(S["f_xTd"], 1)

            def tile_silu(t, u):
                act.wait_ge(S["f_up"], t * UNROLL + u + 1)
                act.activation(f_sg[:, u % 3, :], banks[F_UP[u % 3]][:, 0:INTER], ACT.Silu).then_inc(S["f_si"], 1)

            def tile_end(t, u):
                act.wait_ge(S["f_dn"], t * UNROLL + u + 1)
                act.activation(f_y[:, u, :], banks[F_O][:, 0:D], ACT.Copy, scale=f_x[:, u, D:D + 1]).then_inc(S["f_yd"], 1)

            def slot(t, u):
                for stage, back in ((tile_T_evac, 0), (tile_silu, 1), (tile_end, 3)):
                    tile = tile_of(t, u, back)
                    if tile:
                        stage(*tile)

            routed_slots(act, slot)

            for i in range(GROUPS):
                act.wait_ge(S["y_sum"], i + 1)
                act.dma_start(tok_out[:, group(i), :], X[:, group(i), :]).then_inc(S["y_st"], 16)

        @block.gpsimd
        def _(pool):
            pool.memset(rot[:, 0:P], 1.0).then_inc(S["set_z"], 1)
            pool.memset(pad[:, :], 0.0).then_inc(S["set_z"], 1)
            pool.memset(ones_row[:, :], 1.0).then_inc(S["set_z"], 1)
            pool.memset(ones[:, :], 1.0).then_inc(S["set_z"], 1)
            pool.memset(minus_half[:, :], -0.5).then_inc(S["set_z"], 1)
            pool.memset(epsilon[:, :], LN_EPS).then_inc(S["set_z"], 1)
            pool.memset(Vblk[:, :, :, :, :, :], 0.0).then_inc(S["set_z"], 1)
            pool.memset(Cblk[:, :, :, :, :, :, :], 0.0).then_inc(S["set_z"], 1)
            def carry_wait(u):
                return pool.tensor_tensor(tick[:, u:u + 1], minus_half[:, 0:1], minus_half[:, 0:1], ALU.add)

            rows = row.rearrange("p (r o) -> p r o", o=1).to_broadcast([P, R, T])

            def rsqrt(i, rs, nm, s_ve, s_pw, s_rs):
                pool.wait_ge(s_ve, 2 * i + 2)
                pool.tensor_tensor(rs[:, :], rs[:, :], minus_half[:, :], ALU.pow).then_inc(s_pw, 1)
                pool.wait_ge(s_pw, i + 1)
                pool.tensor_tensor(nm[:, :], nm[:, :], rs[:, :], ALU.mult).then_inc(s_rs, 1)

            def c_variance(c):
                pool.wait_ge(S["c_rsd"], c + 1)
                pool.tensor_tensor(c_rs2[:, :], c_mv[:, :, 1], c_rs[:, :], ALU.mult).then_inc(S["c_v1"], 1)
                pool.wait_ge(S["c_v1"], c + 1)
                pool.tensor_tensor(c_rs2[:, :], c_rs2[:, :], c_rs[:, :], ALU.mult).then_inc(S["c_v2"], 1)
                pool.wait_ge(S["c_v2"], c + 1)
                pool.tensor_tensor(c_rs2[:, :], c_rs2[:, :], epsilon[:, :], ALU.add).then_inc(S["c_ve2"], 1)
                pool.wait_ge(S["c_ve2"], c + 1)
                pool.tensor_tensor(c_rs2[:, :], c_rs2[:, :], minus_half[:, :], ALU.pow).then_inc(S["c_rsd2"], 1)

            def build(dst, src, k):
                return pool.tensor_tensor(dst[:, k % RING, :, :], src[:, k * T:(k + 1) * T].rearrange("p (o n) -> p o n", o=1)
                                          .to_broadcast([P, R, T]), rows, ALU.mult)

            def a_block(g, k, par):
                if k == 0:
                    pool.wait_ge(S["a_qTd"], g + 1)
                if since(g, 1) or k >= RING:
                    pool.wait_ge(S["a_s"], GS * g + k - RING + 1)
                build(Qblk, qT[:, par, :], k).then_inc(S["a_qb"], 1)

            def b_block(g, k, par):
                if k == 0:
                    pool.wait_ge(S["b_cTd"], g + 1)
                if since(g, 1) or k >= RING:
                    pool.wait_ge(S["b_s"], GS * g + k - RING + 1)
                build(Kblk, ctxT[:, par, :], k).then_inc(S["b_kb"], 1)

            def a_rope(f):
                pool.wait_ge(S["a_qkd"], 2 * f + 2)
                if since(f, 1):
                    pool.wait_ge(S["a_kT_ps"], f)
                src = qk[:, :].rearrange("p (n s f) -> p n s f", s=2, f=HALF)
                dst = phi[:, :].rearrange("p (n s f) -> p n s f", s=2, f=HALF)
                for half in range(2):
                    pool.tensor_tensor(dst[:, :, half, :], src[:, :, 1 - half, :],
                                       sin.rearrange("p (o f) -> p o f", o=1).to_broadcast([P, GT * 2 * H, HALF]),
                                       ALU.mult).then_inc(S["a_r2"], 1)

            def c_scatter(d, par, t):
                if t == 0:
                    pool.wait_ge(S["c_idxd"], d + 1)
                    pool.wait_ge(S["c_cp"], d + 1)
                    pool.wait_ge(S["c_ch"], C_STEPS * d + C_STEPS)
                    if since(d, 1):
                        pool.wait_ge(S["c_tick"], d)
                    carry_wait(1).then_inc(S["c_tick"], 1)
                for n in range(TOP):
                    pool.indirect_dma_start(routed[:, :], bass.IndirectOffsetOnAxis(ap=c_idx[:, par, t, n:n + 1], axis=0),
                                            c_row[:, par, t, n, :], None, bounds_check=E * REGION - 1, oob_is_err=False)\
                        .then_inc(c_sc[par], 16)

            def split_shared_weights():
                pool.wait_ge(S["s_in"], 3 * 16)
                pool.wait_ge(S["a_xnT_ps"], GROUPS)
                pool.wait_ge(S["a_vd"], C * GROUPS)
                pool.tensor_copy(shared_up_hi[:, :, :], shared_up_w[:, :, :]).then_inc(S["w_hi"], 1)
                pool.wait_ge(S["w_hi"], 1)
                pool.tensor_tensor(shared_up_lo[:, :, :], shared_up_w[:, :, :], shared_up_hi[:, :, :], ALU.subtract)\
                    .then_inc(S["w_lo"], 1)

            def split_weights(e):
                pool.wait_ge(S["ffw_in"], (2 + CH) * 16)
                pool.wait_ge(S["s_up"], CH * (WUP_N // GN))
                pool.tensor_copy(wup_hi[:, e, :, :], wup[:, e]).then_inc(S["w_hi"], 1)
                pool.wait_ge(S["w_hi"], e + 2)
                pool.tensor_tensor(wup_lo[:, e, :, :], wup[:, e], wup_hi[:, e, :, :], ALU.subtract).then_inc(S["w_lo"], 1)

            def step(s, par):
                e, f, a, h, b, c, d = s + 2, s + 1, s, s - 1, s - 2, s - 3, s - BEHIND
                odd = 1 - par
                for k in range(GS):
                    if k < 5 and on(a):
                        a_block(a, k + 3, par)
                    if k == 6 and on(f):
                        a_block(f, 0, odd)
                    if k == (4 if b_alone(s) else 6) and on(h):
                        rsqrt(h, b_rs, b_nm, S["b_ve"], S["b_pw"], S["b_rsd"])
                    for n in {6: (1,), 7: (2,)}.get(k, ()):
                        if on(f):
                            a_block(f, n, odd)
                    g, n = slot_of(b, k + 3)
                    if on(g):
                        b_block(g, n, odd if n < 3 else par)
                    if k == 2 and on(f):
                        a_rope(f)
                    if k == 2 and on(c):
                        rsqrt(c, c_rs, c_nm, S["c_ve"], S["c_pw"], S["c_rsd"])
                    if k == 4 and on(c):
                        c_variance(c)
                    if k == 3 and on(e) and not s_before(s, -1):
                        rsqrt(e, a_rs, a_nm, S["a_ve"], S["a_pw"], S["a_rsd"])
                    if k < 2 and on(d - 1) and not s_is_last(s - 1):
                        c_scatter(d - 1, odd, k + 2)
                    if s_is_last(s):
                        for t in range(GT if k == routing(s)[4] else 0):
                            c_scatter(d, par, t)
                    elif k >= 6 and on(d):
                        c_scatter(d, par, k - 6)
                    if isinstance(s, int) and s == GROUPS and k == GS - 1:
                        split_shared_weights()
                    if s_is_last(s):
                        for n in range(3 * k, min(3 * k + 3, E)):
                            split_weights(n)

            pool.wait_ge(S["set_z"], SET_ZERO - 1)
            rsqrt(0, a_rs, a_nm, S["a_ve"], S["a_pw"], S["a_rsd"])
            pool.wait_ge(S["con_in"], 16)
            for m in range(2):
                for c in range(C):
                    mark = halves[:, c:c + 1].rearrange("p (a o) -> p a o", o=1)
                    pool.tensor_copy(Vblk[:, m, :, :, c, DH], mark.to_broadcast([P, GS, R]))
                    for q in range(2):
                        mark = halves[:, q:q + 1].rearrange("p (a o) -> p a o", o=1)
                        ins = pool.tensor_copy(Cblk[:, m, :, :, c, q, DH], mark.to_broadcast([P, GS, R // 2]))
            ins.then_inc(S["set_z"], 1)
            steps(pool, step)

            def tile_scatter(t, u):
                pool.wait_ge(S["f_yd"], t * UNROLL + u + 1)
                if not is_first(t, u):
                    pool.wait_ge(S["f_tick"], t * UNROLL + u)
                carry_wait(0).then_inc(S["f_tick"], 1)
                pool.indirect_dma_start(mixed[:, :],
                                        bass.IndirectOffsetOnAxis(ap=f_x[:, u, D + 1:D + 2].bitcast(I32), axis=0),
                                        f_y[:, u, :], None, bounds_check=TOP * TOKENS - 1, oob_is_err=False)\
                    .then_inc(f_out[u], 16)

            def slot(t, u):
                tile = tile_of(t, u, LAG)
                if tile:
                    tile_scatter(*tile)

            routed_slots(pool, slot)

        @block.vector
        def _(dve):
            def statistics(i, src, stat, mv, rs, nm, s_st, s_ag, s_ve, s_xn):
                for t in range(GT):
                    dve.bn_stats(stat[:, t, :], src(t)).then_inc(s_st, 1)
                dve.wait_ge(s_st, GT * i + GT)
                if since(i, 1):
                    dve.wait_ge(s_xn, GT * i)
                dve.memset(rs[:, :], LN_EPS)
                for t in range(GT):
                    dve.bn_aggr(mv[:, t, :], stat[:, t, :]).then_inc(s_ag, 1)
                dve.wait_ge(s_ag, GT * i + GT)
                dve.tensor_tensor(rs[:, :], rs[:, :], mv[:, :, 1], ALU.add).then_inc(s_ve, 1)
                dve.tensor_scalar(nm[:, :], mv[:, :, 0], -1.0, None, ALU.mult).then_inc(s_ve, 1)

            def x_tile(i):
                return lambda t: X[:, bass.ds(i * GT + t, 1), :].rearrange("p o d -> p (o d)")

            def a_statistics(f):
                dve.wait_ge(S["x_in2" if since(f, X_FIRST // GT) else "x_in1" if f else "x_in0"], 16)
                statistics(f, x_tile(f), a_stat, a_mv, a_rs, a_nm, S["a_st"], S["a_ag"], S["a_ve"], S["a_xnd"])

            def a_rotate(f):
                dve.wait_ge(S["a_qkd"], 2 * f + 2)
                n = GT * 2 * H * 2
                dve.tensor_tensor(rot[:, :].rearrange("p (n f) -> p n f", f=HALF),
                                  qk[:, :].rearrange("p (n f) -> p n f", f=HALF),
                                  cos.rearrange("p (o f) -> p o f", o=1).to_broadcast([P, n, HALF]), ALU.mult)\
                    .then_inc(S["a_r1"], 1)

            def a_rotate2(f):
                dve.wait_ge(S["a_r1"], f + 1)
                dve.wait_ge(S["a_r2"], 2 * f + 2)
                for half, op in ((0, ALU.subtract), (1, ALU.add)):
                    v = rot[:, :].rearrange("p (n s f) -> p n s f", s=2, f=HALF)[:, :, half, :]
                    w = phi[:, :].rearrange("p (n s f) -> p n s f", s=2, f=HALF)[:, :, half, :]
                    dve.tensor_tensor(v, v, w, op).then_inc(S["a_rt"], 1)

            def a_feature(f):
                dve.wait_ge(S["a_ex"], f + 1)
                dve.scalar_tensor_tensor(phi[:, :], rot[:, :], 0.0, qk[:, :], ALU.max, ALU.add).then_inc(S["a_ph"], 1)

            def a_mask(a, k):
                dve.wait_ge(S["a_s"], GS * a + k + 1)
                dve.tensor_tensor(Am[:, k % 2, :].rearrange("p (r n) -> p r n", n=T),
                                  banks[A_S][:, :].rearrange("p (r n) -> p r n", n=T),
                                  causal.rearrange("p (o n) -> p o n", o=1).to_broadcast([P, R, T]), ALU.mult)\
                    .then_inc(S["a_am"], 1)

            def a_divide(g, m):
                dve.wait_ge(S["a_av"], GS * g + (m + 1) * (GS // 2))
                num = banks[A_O][:, 0:2 * H * E9].rearrange("p (t n e) -> p t n e", t=2, e=E9)
                dve.tensor_scalar(a_den[:, :, :], num[:, :, :, DH], DEN_EPS, None, ALU.max).then_inc(S["a_dn"], 1)
                dve.wait_ge(S["a_dn"], 2 * g + m + 1)
                dve.reciprocal(a_rec[:, :, :], a_den[:, :, :]).then_inc(S["a_rc"], 1)
                dve.wait_ge(S["a_rc"], 2 * g + m + 1)
                if m == 0 and since(g, 1):
                    dve.wait_ge(S["a_yT_ps"], g)
                for t in range(2):
                    dst = a_y[:, 2 * m + t, :].rearrange("p (c r e) -> p r c e", c=C, e=DH)
                    src = num[:, t, :, 0:DH].rearrange("p (r c) e -> p r c e", c=C)
                    rec = a_rec[:, t, :].rearrange("p (r c o) -> p r c o", c=C, o=1).to_broadcast([P, R, C, DH])
                    dve.tensor_tensor(dst, src, rec, ALU.mult).then_inc(S["a_yd"], 1)

            def a_residual(h):
                dve.wait_ge(S["a_o"], h + 1)
                xs = X[:, group(h), :]
                dve.tensor_tensor(xs, xs, banks[FRONT1][:, :].rearrange("p (t d) -> p t d", t=GT), ALU.add)\
                    .then_inc(S["a_x1"], 1)
                dve.wait_ge(S["a_x1"], h + 1)

            def b_statistics(h):
                statistics(h, x_tile(h), b_stat, b_mv, b_rs, b_nm, S["b_st"], S["b_ag"], S["b_ve"], S["b_xnd"])

            def b_norm(h):
                if since(h, 1):
                    dve.wait_ge(S["b_qT_ps"], h)
                dve.wait_ge(S["b_rsd"], h + 1)
                for t in range(GT):
                    dve.tensor_scalar(b_xn[:, t, :], x_tile(h)(t), b_mv[:, t, 0:1], b_rs[:, t:t + 1], ALU.subtract, ALU.mult)\
                        .then_inc(S["b_xnd"], 1)

            def b_context(h, par):
                dve.wait_ge(S["b_cT_ps"], h + 1)
                dve.wait_ge(S["b_in"], B_LOADS * 16 * (h + 1))
                if since(h, 2):
                    dve.wait_ge(S["b_s"], GS * (h - 1))
                dve.scalar_tensor_tensor(ctxT[:, par, :], maskB[:, :], 0.0, banks[FRONT1][:, :], ALU.not_equal, ALU.mult)\
                    .then_inc(S["b_cTd"], 1)
                dve.tensor_scalar(bias_row[:, par, :], maskB[0:1, :], 0.0, MASKED, ALU.is_equal, ALU.mult)\
                    .then_inc(S["b_bi"], 1)

            def b_max(b, k, alone):
                dve.wait_ge(S["b_s"], GS * b + k + 1)
                dve.tensor_reduce(mx[:, k, :], b_bank(alone, k)[:, :].rearrange("p (r n) -> p r n", n=T), AX, ALU.max)\
                    .then_inc(S["b_mx"], 1)
                dve.wait_ge(S["b_mx"], GS * b + k + 1)
                dve.tensor_scalar(shift[:, k, :], mx[:, k, :], -SCALE, None, ALU.mult).then_inc(S["b_mh"], 1)

            def b_divide(g, m):
                dve.wait_ge(S["b_av"], GS * g + (m + 1) * (GS // 2))
                num = banks[B_O][:, 0:2 * H * E9].rearrange("p (t n e) -> p t n e", t=2, e=E9)
                dve.reciprocal(b_rec[:, :, :], num[:, :, :, DH]).then_inc(S["b_rc"], 1)
                dve.wait_ge(S["b_rc"], 2 * g + m + 1)
                for t in range(2):
                    for c in range(C):
                        dst = b_y[:, t, :].rearrange("p (c r q e) -> p c r q e", c=C, q=2, e=DH)[:, c]
                        src = num[:, t, :, 0:DH].rearrange("p (r c q) e -> p c r q e", c=C, q=2)[:, c]
                        rec = b_rec[:, t, :].rearrange("p (r c q o) -> p c r q o", c=C, q=2, o=1)[:, c]\
                            .to_broadcast([P, R // 2, 2, DH])
                        ins = dve.tensor_tensor(dst, src, rec, ALU.mult)
                        ins.then_inc(S["b_yd"], 1)
                dve.wait_ge(S["b_yd"], 8 * g + 4 * m + 4)
                xs = X[:, bass.ds(g * GT + 2 * m, 2), :]
                dve.tensor_tensor(xs, xs, b_y[:, :, :], ALU.add).then_inc(S["b_x2"], 1)
                if m == 1:
                    dve.wait_ge(S["b_x2"], 2 * g + 2)

            def c_statistics(c):
                statistics(c, x_tile(c), c_stat, c_mv, c_rs, c_nm, S["c_st"], S["c_ag"], S["c_ve"], S["c_xf"])

            def per_token(v):
                return v.rearrange("p (t o) -> p t o", o=1).to_broadcast([P, GT, E])

            def per_expert(v):
                return v.rearrange("p (o e) -> p o e", o=1).to_broadcast([P, GT, E])

            def c_chain(c):
                def chain(ins, n):
                    ins.then_inc(S["c_ch"], 1)
                    dve.wait_ge(S["c_ch"], C_STEPS * c + n)
                return chain

            hit = c_hit[:, 0, :, :]

            def c_softmax(c):
                chain = c_chain(c)
                dve.wait_ge(S["c_rsd2"], c + 1)
                dve.wait_ge(S["c_lg_ps"], c + 1)
                logits = banks[FRONT0][:, 0:GT * E].rearrange("p (t e) -> p t e", e=E)
                chain(dve.tensor_tensor(c_p[:, :, :], logits, per_token(c_rs2[:, :]), ALU.mult), 1)
                chain(dve.tensor_tensor(c_p[:, :, :], c_p[:, :, :], per_expert(gate_sum[:, :]), ALU.add), 2)
                chain(dve.tensor_reduce(c_m[:, :], c_p[:, :, :], AX, ALU.max), 3)
                dve.tensor_tensor(c_p[:, :, :], c_p[:, :, :], per_token(c_m[:, :]), ALU.subtract).then_inc(S["c_lg"], 1)

            def c_best_of(c, n, chain, at):
                chain(dve.tensor_reduce(c_best[:, n, :], c_t[:, :, :], AX, ALU.max), at)
                chain(dve.tensor_tensor(hit, c_t[:, :, :], per_token(c_best[:, n, :]), ALU.is_equal), at + 1)
                chain(dve.tensor_tensor(hit, hit, per_expert(order), ALU.mult), at + 2)
                chain(dve.tensor_reduce(c_m[:, :], hit, AX, ALU.max), at + 3)
                chain(dve.tensor_tensor(c_pick[:, n, :, :], per_expert(order), per_token(c_m[:, :]), ALU.is_equal), at + 4)

            def c_probabilities(d):
                chain = c_chain(d)
                dve.wait_ge(S["c_ex"], d + 1)
                chain(dve.tensor_reduce(c_m[:, :], c_p[:, :, :], AX, ALU.add), 4)
                chain(dve.reciprocal(c_m[:, :], c_m[:, :]), 5)
                chain(dve.tensor_tensor(c_t[:, :, :], c_p[:, :, :], per_token(c_m[:, :]), ALU.mult), 6)

            def c_first(d):
                chain = c_chain(d)
                c_best_of(d, 0, chain, 7)
                chain(dve.scalar_tensor_tensor(c_t[:, :, :], c_pick[:, 0, :, :], -2.0, c_t[:, :, :], ALU.mult, ALU.add), 12)

            def c_second(d):
                c_best_of(d, 1, c_chain(d), 13)
                dve.tensor_tensor(c_sel[:, :, :], c_pick[:, 0, :, :], c_pick[:, 1, :, :], ALU.add).then_inc(S["c_seld"], 1)

            def c_weights(d, par):
                chain = c_chain(d)
                chain(dve.scalar_tensor_tensor(c_m[:, :], c_best[:, 0, :], TOP_EPS, c_best[:, 1, :], ALU.add, ALU.add), 18)
                chain(dve.reciprocal(c_m[:, :], c_m[:, :]), 19)
                dve.tensor_tensor(c_row[:, par, :, :, D].rearrange("p t n -> p n t"), c_best[:, :, :],
                                  c_m[:, :].rearrange("p (o t) -> p o t", o=1).to_broadcast([P, TOP, GT]), ALU.mult)
                chain(dve.tensor_copy(c_row[:, par, :, :, D + 1:ROW].bitcast(I32).rearrange("p t n o -> p t (n o)"),
                                      c_place[:, :, :]), 20)
                chain(dve.tensor_scalar(c_place[:, :, :], c_place[:, :, :], float(GN), None, ALU.add), C_STEPS)

            def c_index(d, par):
                dve.wait_ge(S["c_ps"], d + 1)
                bank = banks[FRONT0]
                dve.tensor_tensor(c_pos[:, :, :], bank[:, 0:GT * E].rearrange("p (t e) -> p t e", e=E),
                                  per_expert(c_base[:, :]), ALU.add).then_inc(S["c_posd"], 1)
                dve.wait_ge(S["c_posd"], d + 1)
                dve.tensor_tensor(c_base[:, :], c_base[:, :], bank[:, GT * E:(GT + 1) * E], ALU.add).then_inc(S["c_read"], 1)
                dve.tensor_tensor(c_hit[:, :, :, :], c_pick[:, :, :, :],
                                  c_pos[:, :, :].rearrange("p (o t) e -> p o t e", o=1).to_broadcast([P, TOP, GT, E]),
                                  ALU.mult).then_inc(S["c_hitd"], 1)
                dve.wait_ge(S["c_hitd"], d + 1)
                dve.tensor_reduce(c_at[:, :, :].rearrange("p t n -> p n t"), c_hit[:, :, :, :], AX, ALU.add)\
                    .then_inc(S["c_atd"], 1)
                dve.wait_ge(S["c_atd"], d + 1)
                dve.tensor_copy(c_idx[:, par, :, :], c_at[:, :, :]).then_inc(S["c_idxd"], 1)

            links = [0]

            def link(ins):
                links[0] += 1
                ins.then_inc(S["t_ch"], 1)
                dve.wait_ge(S["t_ch"], links[0])

            nt = t_nt[:, :].rearrange("p (o e) -> p o e", o=1)

            def tiles_per_expert():
                dve.wait_ge(S["c_read"], GROUPS)
                link(dve.tensor_copy(t_pad[:, :], c_base[0:1, :]))
                link(dve.tensor_tensor(t_cnt[:, :], c_base[0:1, :], const("region")[0:1, :], ALU.subtract))
                link(dve.tensor_scalar(t_int[:, :], t_cnt[:, :], float(P - 1), None, ALU.add))
                link(dve.tensor_scalar(t_int[:, :], t_int[:, :], TILE_BITS, None, ALU.arith_shift_right))
                link(dve.tensor_copy(t_nt[:, :], t_int[:, :]))
                link(dve.tensor_tensor(t_sq[:, :, :], const("upto")[0:1, :].rearrange("p (a b) -> p a b", b=E),
                                       nt.to_broadcast([1, E, E]), ALU.mult))
                link(dve.tensor_reduce(t_end[:, :], t_sq[:, :, :], AX, ALU.add))

            def tiles(part):
                tile_n = const("tile")[0:1, :]
                by_tile = [1, TILE_MAX, E]
                if part == 0:
                    link(dve.tensor_tensor(t_ge[:, :, :], tile_n.rearrange("p (n o) -> p n o", o=1).to_broadcast(by_tile),
                                           t_end[:, :].rearrange("p (o e) -> p o e", o=1).to_broadcast(by_tile), ALU.is_ge))
                    link(dve.tensor_reduce(t_e[:, :], t_ge[:, :, :], AX, ALU.add))
                elif part == 1:
                    link(dve.tensor_tensor(t_ge[:, :, :], t_ge[:, :, :], nt.to_broadcast(by_tile), ALU.mult))
                    link(dve.tensor_reduce(t_st[:, :], t_ge[:, :, :], AX, ALU.add))
                else:
                    link(dve.tensor_tensor(t_st[:, :], tile_n, t_st[:, :], ALU.subtract))
                    link(dve.tensor_scalar(t_st[:, :], t_st[:, :], float(P), None, ALU.mult))
                    link(dve.scalar_tensor_tensor(t_row[:, :], t_e[:, :], float(REGION), t_st[:, :], ALU.mult, ALU.add))
                    dve.tensor_scalar(t_expert[:, :], t_e[:, :], float(E - 1), None, ALU.min).then_inc(S["t_done"], 1)

            def s_low(i):
                if i >= 2:
                    dve.wait_ge(S["s_up"], CH * (i - 1))
                dve.wait_ge(S["s_xh"], i + 1)
                dve.tensor_tensor(s_x_lo[:, i % 2, :], xfT[:, i * GN:(i + 1) * GN], s_x_hi[:, i % 2, :], ALU.subtract)\
                    .then_inc(S["s_xl"], 1)

            def s_hidden(i):
                for c in range(CH):
                    dve.wait_ge(S["s_si"], i * CH + c + 1)
                    dve.tensor_tensor(s_h[:, i % 2, c, :], s_sg[:, c, :], banks[S_UP[c][1]][:, :], ALU.mult)\
                        .then_inc(S["s_hd"], 1)

            def s_add(i):
                dve.wait_ge(S["s_dn"], i + 1)
                xs = X[:, group(i), :]
                dve.tensor_tensor(xs, xs, banks[S_O[i % 2]][:, :].rearrange("p (t d) -> p t d", t=GT), ALU.add)\
                    .then_inc(S["s_ac"], 1)

            def step(s, par):
                e, f, a, h, b, c, d = s + 2, s + 1, s, s - 1, s - 2, s - 3, s - BEHIND
                odd = 1 - par
                for k in range(GS):
                    if on(b) and b_alone(s):
                        b_max(b, k, True)
                    if k % 4 == 0:
                        g, m = (a, 0) if k else (a - 1, 1)
                        if on(g):
                            a_divide(g, m)
                    half = b_half(s, k)
                    if half and on(s + half[0]):
                        b_divide(s + half[0], half[1])
                    if on(a):
                        a_mask(a, k)
                    if k == 2 and on(f):
                        a_rotate(f)
                    if k == 2 and on(d) and not b_alone(s) and not s_is_last(s):
                        c_first(d)
                    if k == 3 and on(d) and not b_alone(s) and not s_is_last(s):
                        c_second(d)
                    if k == 3 and on(f):
                        a_rotate2(f)
                    if k == 7 and on(s + 3) and not s_before(s, -2):
                        a_statistics(s + 3)
                    if on(b) and not b_alone(s):
                        b_max(b, k, False)
                    if k == 4 and on(f):
                        a_feature(f)
                    if k == 0 and on(h):
                        b_context(h, odd)
                    if k == 0 and on(d):
                        c_probabilities(d)
                    if k == b_last_half(s) and on(c):
                        c_statistics(c)
                    if k == routing(s)[0] and (b_alone(s) or s_is_last(s)):
                        c_first(d)
                    if k == 3 and on(h):
                        a_residual(h)
                    if k == routing(s)[1] and (b_alone(s) or s_is_last(s)):
                        c_second(d)
                    if k == routing(s)[3] and on(d):
                        c_weights(d, par)
                    if k == routing(s)[4] and on(d):
                        c_index(d, par)
                    if k == 3 and s_is_last(s):
                        tiles_per_expert()
                    if k in (4, 5, 6) and s_is_last(s):
                        tiles(k - 4)
                    if k == (3 if b_alone(s) else 5) and on(h):
                        b_statistics(h)
                    if k == (5 if b_alone(s) else 6) and on(h):
                        b_norm(h)
                    if k == 7 and on(c):
                        c_softmax(c)
                    i = shared_of(s, k)
                    if i + 1 in range(GROUPS):
                        s_low(i + 1)
                    if i in range(GROUPS):
                        s_hidden(i)
                    if i in range(1, GROUPS + 1):
                        s_add(i - 1)

            a_statistics(0)
            dve.wait_ge(S["set_z"], 2)
            dve.memset(pad[:, D + 1:D + 2].bitcast(I32), NOWHERE).then_inc(S["set_d"], 1)
            dve.wait_ge(S["con_in"], 16)
            dve.tensor_copy(before[:, :], const("before")).then_inc(S["set_d"], 1)
            dve.tensor_copy(c_base[:, :], const("region")).then_inc(S["set_d"], 1)
            dve.tensor_copy(c_place[:, :, :].rearrange("p t n -> p (t n)"), const("place")).then_inc(S["set_d"], 1)
            dve.wait_ge(S["w_in"], 7 * 16)
            dve.wait_ge(S["set_ps"], 1)
            dve.tensor_scalar(gateT[:, :], banks[1][:, 0:E], lnp[:, 0:1], None, ALU.mult).then_inc(S["set_d"], 1)
            dve.tensor_scalar(rot[:, P:P + E], banks[1][:, 0:E], lnp[:, 1:2], None, ALU.mult).then_inc(S["set_d"], 1)
            dve.memset(KQ[:, :, :, :, :, :], 0.0).then_inc(S["set_d"], 1)
            dve.wait_ge(S["set_cp"], 3)
            steps(dve, step)

            def tile_low(t, u):
                n = t * UNROLL + u
                dve.wait_ge(S["f_xTd"], n + 1)
                if since(t, 1) or u >= 3:
                    dve.wait_ge(S["f_up"], n - 2)
                dve.tensor_tensor(f_xT_lo[:, u % 3, :], banks[F_X][:, 0:P], f_xT_hi[:, u % 3, :], ALU.subtract)\
                    .then_inc(S["f_xTl"], 1)

            def hidden(t, u):
                dve.wait_ge(S["f_si"], t * UNROLL + u + 1)
                dve.tensor_tensor(f_h[:, u % 3, :], f_sg[:, u % 3, :], banks[F_UP[u % 3]][:, INTER:2 * INTER],
                                  ALU.mult).then_inc(S["f_hd"], 1)

            def hidden_evac(t, u):
                dve.wait_ge(S["f_hT_ps"], t * UNROLL + u + 1)
                dve.tensor_copy(f_hT[:, u % 3, :], banks[F_HT[u % 3]][:, 0:INTER]).then_inc(S["f_hTd"], 1)

            def slot(t, u):
                for stage, back in ((tile_low, 0), (hidden, 1), (hidden_evac, 2)):
                    tile = tile_of(t, u, back)
                    if tile:
                        stage(*tile)

            routed_slots(dve, slot)

            for i in range(GROUPS):
                u = i % Y_RING
                dve.wait_ge(y_ld[u], 32 * (i // Y_RING + 1))
                xs = X[:, group(i), :].rearrange("p t d -> p (t d)")
                dve.tensor_tensor(xs, xs, y_in[:, u * GN:(u + 1) * GN], ALU.add).then_inc(S["y_ad"], 1)
                dve.wait_ge(S["y_ad"], i + 1)
                dve.tensor_tensor(xs, xs, y_in2[:, u * GN:(u + 1) * GN], ALU.add).then_inc(S["y_sum"], 1)


_INS = ["x", "ctx_1024", "mask_BxS2_if1", "L0_attn_Wq", "L0_attn_Wk", "L0_attn_Wv", "L0_attn_Wo", "L0_ffn_ln_scale",
        "L0_ffn_ln_bias", "L0_ffn_gate_w", "L0_ffn_Wg", "L0_ffn_Wu", "L0_ffn_Wd", "L0_ffn_sWg", "L0_ffn_sWu",
        "L0_ffn_sWd"]


def kernel(**inputs):
    import numpy as _np
    import concourse.bacc as _bacc
    from concourse import mybir as _mybir
    from concourse.bass_utils import run_bass_kernel_spmd as _run

    nc = _bacc.Bacc("TRN2", target_bir_lowering=False, num_devices=1)
    arrays, args = {}, []
    for name in _INS:
        a = _np.ascontiguousarray(inputs[name])
        arrays[f"in_{name}"] = a
        args.append(nc.dram_tensor(f"in_{name}", a.shape, _mybir.dt.from_np(a.dtype), kind="ExternalInput").ap())
    a = shape_constants()
    arrays["shape_constants"] = a
    args.append(nc.dram_tensor("shape_constants", a.shape, _mybir.dt.from_np(a.dtype), kind="ExternalInput").ap())
    args.append(nc.dram_tensor("block_out", (SEQS, T, D), _mybir.dt.float32, kind="ExternalOutput").ap())
    decoder_block(nc, *args)
    r = _run(nc, [arrays], core_ids=[0])
    return r.results[0]["block_out"]
```
